# Optimizing a Trainium2 kernel written in Bass

```python
import numpy as np
import jax
import jax.numpy as jnp

def _softmax(x, axis=-1):
    return jax.nn.softmax(x, axis=axis)

def _gelu(x):
    return jax.nn.gelu(x, approximate=True)

def _silu(x):
    return jax.nn.silu(x)

def _sigmoid(x):
    return jax.nn.sigmoid(x)

def _layernorm(x, axis=-1, eps=1e-05):
    m = jnp.mean(x, axis=axis, keepdims=True)
    v = jnp.var(x, axis=axis, keepdims=True)
    return (x - m) / jnp.sqrt(v + eps)

def _scatter_add(tgt, idx, src, axis=0):
    return tgt.at[idx].add(src)

def _segment_sum(src, seg, n):
    return jax.ops.segment_sum(src, seg, n)
kernel_name = 'mk_gnn_preln_d2_gnn_r64_336cae'

def setup_inputs(seed: int=0):
    np.random.seed(seed)
    _w = jnp.asarray

    def _rec_inputs():
        import jax
        import jax.numpy as jnp
        _gk = jax.random.key(seed)
        x = -0.000202 + 1 * jax.random.normal(jax.random.fold_in(_gk, 1), (100000, 64), jnp.float32)
        src = jax.random.randint(jax.random.fold_in(_gk, 2), (25000,), 0, 100000, jnp.int32)
        dst = jax.random.randint(jax.random.fold_in(_gk, 3), (25000,), 0, 100000, jnp.int32)
        _o = jnp.argsort(dst, stable=True)
        src = src[_o]
        dst = dst[_o]
        edge_attr_64 = -5.16925e-05 + 1.00005 * jax.random.normal(jax.random.fold_in(_gk, 11), (25000, 64), jnp.float32)
        return (x, src, dst, edge_attr_64)
    x, src, dst, edge_attr_64 = _rec_inputs()

    def _L0_gnn_setup():
        import jax, jax.numpy as jnp
        import numpy as np
        NUM_NODES = 100000
        NUM_HYPEREDGES = 3125
        NNZ = 18750
        IN_DIM = 64
        HID_DIM = 64
        OUT_DIM = 64

        def _hypergraph_conv(x, node_idx, edge_idx, D_inv, B_inv, W, b):
            xt = x @ W
            e = B_inv[:, None] * jax.ops.segment_sum(xt[node_idx], edge_idx, num_segments=NUM_HYPEREDGES)
            out = D_inv[:, None] * jax.ops.segment_sum(e[edge_idx], node_idx, num_segments=NUM_NODES)
            return out + b
        key = jax.random.key(seed)
        k1, k2, k3, k4, k5, k6, k7, k8 = jax.random.split(key, 8)
        x = jax.random.normal(k1, (NUM_NODES, IN_DIM), dtype=jnp.float32)
        node_idx = jax.random.randint(k2, (NNZ,), 0, NUM_NODES, dtype=jnp.int64)
        edge_idx = jax.random.randint(k3, (NNZ,), 0, NUM_HYPEREDGES, dtype=jnp.int64)
        hyperedge_index = jnp.stack([node_idx, edge_idx], axis=0)
        s1 = 1.0 / np.sqrt(IN_DIM)
        s2 = 1.0 / np.sqrt(HID_DIM)
        W1 = jax.random.uniform(k4, (IN_DIM, HID_DIM), jnp.float32, -s1, s1)
        b1 = jax.random.uniform(k5, (HID_DIM,), jnp.float32, -s1, s1)
        W2 = jax.random.uniform(k6, (HID_DIM, OUT_DIM), jnp.float32, -s2, s2)
        b2 = jax.random.uniform(k7, (OUT_DIM,), jnp.float32, -s2, s2)
        return {'x': x, 'hyperedge_index': hyperedge_index, 'W1': W1, 'b1': b1, 'W2': W2, 'b2': b2}
    _L0_gnn_all = _L0_gnn_setup()
    _L0_gnn_in = {k: v for k, v in _L0_gnn_all.items() if k in ('W1', 'b1', 'W2', 'b2')}
    del _L0_gnn_all

    def _L1_gnn_setup():
        import jax, jax.numpy as jnp
        import numpy as np
        N = 100000
        E = 25000
        D = 64
        EPS = 1e-05

        def _gcn_conv(x, src, dst, dinv, W, b):
            h = x @ W
            norm = (dinv[src] * dinv[dst])[:, None]
            agg = jax.ops.segment_sum(h[src] * norm, dst, num_segments=N)
            agg = agg + (dinv * dinv)[:, None] * h
            return agg + b

        def _bn(x, gamma, beta):
            mean = jnp.mean(x, axis=0)
            var = jnp.var(x, axis=0)
            return gamma * (x - mean) * jax.lax.rsqrt(var + EPS) + beta
        key = jax.random.key(seed)
        ks = jax.random.split(key, 16)
        edge_index = jax.random.randint(ks[0], (2, E), 0, N, dtype=jnp.int64)
        node_attr = jax.random.normal(ks[1], (N, D), dtype=jnp.float32)
        edge_attr = jax.random.normal(ks[2], (E, D), dtype=jnp.float32)
        scale = 1.0 / np.sqrt(D)
        params = {}
        for i, k in enumerate(range(3, 3 + 3)):
            li = i + 1
            kw, kb = jax.random.split(ks[k])
            params[f'W{li}'] = jax.random.uniform(kw, (D, D), jnp.float32, -scale, scale)
            params[f'b{li}'] = jax.random.uniform(kb, (D,), jnp.float32, -scale, scale)
            params[f'gamma{li}'] = jnp.ones((D,), jnp.float32)
            params[f'beta{li}'] = jnp.zeros((D,), jnp.float32)
        return {'edge_index': edge_index, 'node_attr': node_attr, 'edge_attr': edge_attr, **params}
    _L1_gnn_all = _L1_gnn_setup()
    _L1_gnn_in = {k: v for k, v in _L1_gnn_all.items() if k in ('W1', 'b1', 'gamma1', 'beta1', 'W2', 'b2', 'gamma2', 'beta2', 'W3', 'b3', 'gamma3', 'beta3')}
    del _L1_gnn_all
    return {'x': x, 'src': src, 'dst': dst, 'edge_attr_64': edge_attr_64, 'L0_gnn_W1': _L0_gnn_in['W1'], 'L0_gnn_b1': _L0_gnn_in['b1'], 'L0_gnn_W2': _L0_gnn_in['W2'], 'L0_gnn_b2': _L0_gnn_in['b2'], 'L1_gnn_W1': _L1_gnn_in['W1'], 'L1_gnn_b1': _L1_gnn_in['b1'], 'L1_gnn_gamma1': _L1_gnn_in['gamma1'], 'L1_gnn_beta1': _L1_gnn_in['beta1'], 'L1_gnn_W2': _L1_gnn_in['W2'], 'L1_gnn_b2': _L1_gnn_in['b2'], 'L1_gnn_gamma2': _L1_gnn_in['gamma2'], 'L1_gnn_beta2': _L1_gnn_in['beta2'], 'L1_gnn_W3': _L1_gnn_in['W3'], 'L1_gnn_b3': _L1_gnn_in['b3'], 'L1_gnn_gamma3': _L1_gnn_in['gamma3'], 'L1_gnn_beta3': _L1_gnn_in['beta3']}

def reference(x, src, dst, edge_attr_64, L0_gnn_W1, L0_gnn_b1, L0_gnn_W2, L0_gnn_b2, L1_gnn_W1, L1_gnn_b1, L1_gnn_gamma1, L1_gnn_beta1, L1_gnn_W2, L1_gnn_b2, L1_gnn_gamma2, L1_gnn_beta2, L1_gnn_W3, L1_gnn_b3, L1_gnn_gamma3, L1_gnn_beta3):
    import jax
    import jax.numpy as jnp

    def _L0_gnn_ref(x, hyperedge_index, W1, b1, W2, b2):
        import jax, jax.numpy as jnp
        import numpy as np
        NUM_NODES = 100000
        NUM_HYPEREDGES = 3125
        NNZ = 18750
        IN_DIM = 64
        HID_DIM = 64
        OUT_DIM = 64

        def _hypergraph_conv(x, node_idx, edge_idx, D_inv, B_inv, W, b):
            xt = x @ W
            e = B_inv[:, None] * jax.ops.segment_sum(xt[node_idx], edge_idx, num_segments=NUM_HYPEREDGES)
            out = D_inv[:, None] * jax.ops.segment_sum(e[edge_idx], node_idx, num_segments=NUM_NODES)
            return out + b
        node_idx = hyperedge_index[0]
        edge_idx = hyperedge_index[1]
        ones = jnp.ones((node_idx.shape[0],), dtype=x.dtype)
        D = jax.ops.segment_sum(ones, node_idx, num_segments=NUM_NODES)
        B = jax.ops.segment_sum(ones, edge_idx, num_segments=NUM_HYPEREDGES)
        D_inv = jnp.where(D > 0, 1.0 / D, 0.0)
        B_inv = jnp.where(B > 0, 1.0 / B, 0.0)
        h = jax.nn.relu(_hypergraph_conv(x, node_idx, edge_idx, D_inv, B_inv, W1, b1))
        y = _hypergraph_conv(h, node_idx, edge_idx, D_inv, B_inv, W2, b2)
        return y

    def _L1_gnn_ref(edge_index, node_attr, edge_attr, W1, b1, gamma1, beta1, W2, b2, gamma2, beta2, W3, b3, gamma3, beta3):
        import jax, jax.numpy as jnp
        import numpy as np
        N = 100000
        E = 25000
        D = 64
        EPS = 1e-05

        def _gcn_conv(x, src, dst, dinv, W, b):
            h = x @ W
            norm = (dinv[src] * dinv[dst])[:, None]
            agg = jax.ops.segment_sum(h[src] * norm, dst, num_segments=N)
            agg = agg + (dinv * dinv)[:, None] * h
            return agg + b

        def _bn(x, gamma, beta):
            mean = jnp.mean(x, axis=0)
            var = jnp.var(x, axis=0)
            return gamma * (x - mean) * jax.lax.rsqrt(var + EPS) + beta
        src, dst = (edge_index[0], edge_index[1])
        deg = jnp.zeros((N,), jnp.float32).at[dst].add(1.0) + 1.0
        dinv = jax.lax.rsqrt(deg)
        x = _bn(jax.nn.relu(_gcn_conv(node_attr, src, dst, dinv, W1, b1)), gamma1, beta1)
        x = _bn(jax.nn.relu(_gcn_conv(x, src, dst, dinv, W2, b2)), gamma2, beta2)
        x = _bn(jax.nn.relu(_gcn_conv(x, src, dst, dinv, W3, b3)), gamma3, beta3)
        return x
    edge_index = jnp.stack([src, dst])
    h = jnp.maximum(_layernorm(x, axis=-1), 0.0)
    x = x + _L0_gnn_ref(h, edge_index, L0_gnn_W1, L0_gnn_b1, L0_gnn_W2, L0_gnn_b2)
    h = jnp.maximum(_layernorm(x, axis=-1), 0.0)
    x = x + _L1_gnn_ref(edge_index, h, edge_attr_64, L1_gnn_W1, L1_gnn_b1, L1_gnn_gamma1, L1_gnn_beta1, L1_gnn_W2, L1_gnn_b2, L1_gnn_gamma2, L1_gnn_beta2, L1_gnn_W3, L1_gnn_b3, L1_gnn_gamma3, L1_gnn_beta3)
    return x

_drawn_inputs = setup_inputs


def setup_inputs(seed=0):
    import zlib

    import numpy as np

    out = dict(_drawn_inputs(seed))
    spreads = {'L1_gnn_gamma1': (1.0, 0.2),
     'L1_gnn_beta1': (0.0, 0.1),
     'L1_gnn_gamma2': (1.0, 0.2),
     'L1_gnn_beta2': (0.0, 0.1),
     'L1_gnn_gamma3': (1.0, 0.2),
     'L1_gnn_beta3': (0.0, 0.1)}
    factors = {}
    for name, (base, spread) in spreads.items():
        noise = np.random.default_rng([zlib.crc32(name.encode()), seed]).standard_normal(out[name].shape)
        drawn = base * np.exp(spread * noise) if base else spread * noise
        out[name] = jnp.asarray(drawn.astype(out[name].dtype))
    for name, factor in factors.items():
        out[name] = (out[name] * factor).astype(out[name].dtype)
    return out
```

```python
import concourse.bass as bass
from concourse import mybir
from contextlib import ExitStack

F32 = mybir.dt.float32
F16 = mybir.dt.float16
I32 = mybir.dt.int32
ACT = mybir.ActivationFunctionType
ALU = mybir.AluOpType
AX = mybir.AxisListType

P = 128
N, E, F = 100000, 25000, 64
HYPER = 3125
EPS = 1e-5

G = 16
CHUNK = P * G
NC = -(-N // CHUNK)
NP = NC * CHUNK
TAIL_P = (N - (NC - 1) * CHUNK) // G
COLS = NC * G
DUMMY = NP

TILES = -(-E // P)
LANES = 7
STEPS = TILES // LANES
EP = TILES * P
PAD_NODE = NP - 1
ROWS2 = TILES - P
HDUMMY = HYPER
HROWS = 26 * P
HW = F + 1


def node_chunks(table, rows=NP):
    return table[0:rows, :].rearrange("(c p g) f -> c p (g f)", p=P, g=G)


def chunk_of(view, c):
    return view[bass.ds(c, 1), :, :].rearrange("a p n -> (a p) n")


class Net:

    def __init__(self, nc, ctx, args):
        self.nc, self.args = nc, args

        def sb(name, shape, dt=F32):
            return ctx.enter_context(nc.sbuf_tensor(name, shape, dt))

        def dram(name, shape, dt=F32):
            return nc.dram_tensor(name, shape, dt, kind="Internal").ap()

        self.passed = ctx.enter_context(nc.semaphore("passed"))
        self.x1 = dram("x1_rows", (NP + P, F))
        self.conv = dram("conv_rows", (NP + P, F))
        self.y = dram("y_rows", (NP, F))
        self.v = dram("v_rows", (NP + P, F))
        self.z = dram("z_units", (NC, P, G // 2 * P))
        self.node_scalars = dram("node_scalars", (NP, 2))
        self.hyper1 = dram("hyper1_rows", (HROWS, HW))
        self.hyper2 = dram("hyper2_rows", (HROWS, HW))
        self.src_padded = dram("src_padded", (TILES, P), I32)
        self.dst_padded = dram("dst_padded", (TILES, P), I32)
        self.same_dst = dram("same_dst", (STEPS, P, LANES * P))
        self.src_f = sb("src_f", [P, TILES])
        self.dst_f = sb("dst_f", [P, TILES])
        self.light = sb("light", [P, TILES])
        self.src_idx = sb("src_idx", [P, TILES], I32)
        self.clip_idx = sb("clip_idx", [P, TILES], I32)
        self.light_idx = sb("light_idx", [P, TILES], I32)
        self.dst_idx = sb("dst_idx", [P, TILES], I32)
        self.bounds = sb("bounds", [1, 2], I32)
        self.dinv = sb("dinv", [P, COLS])
        self.far_share = sb("far_share", [P, COLS])
        self.ident = sb("ident", [P, P])
        self.before = sb("before", [P, P])
        self.pair_mean = sb("pair_mean", [P, P])
        self.part = sb("part", [P, 1])
        self.eps = sb("eps", [P, 1])
        self.conv_w = [sb(f"conv_w{i}", [F, F]) for i in range(2)]
        self.conv_b = [sb(f"conv_b{i}", [P, F]) for i in range(2)]
        self.gcn_w = [sb(f"gcn_w{i}", [P, P]) for i in range(3)]
        self.gcn_b = sb("gcn_b", [P, 3])
        self.gamma = sb("gamma", [P, 3])
        self.beta = sb("beta", [P, 3])
        self.e1_last = sb("e1_last", [P, F])
        self.e2_last = sb("e2_last", [P, F])


def wait_alone(engine, sem, value, net):
    engine.wait_ge(sem, value)
    engine.sem_inc(net.passed, 1)


class Chain:

    def __init__(self, engine, sem, base=0, net=None):
        self.engine, self.sem, self.base, self.n, self.net = engine, sem, base, 0, net

    def __call__(self, instruction):
        self.n += 1
        instruction.then_inc(self.sem, 1)
        if self.net is None:
            self.engine.wait_ge(self.sem, self.base + self.n)
        else:
            wait_alone(self.engine, self.sem, self.base + self.n, self.net)


def load_tables(net):
    nc, a = net.nc, net.args
    with ExitStack() as ctx:
        def sb(name, shape, dt=F32):
            return ctx.enter_context(nc.sbuf_tensor(f"load_{name}", shape, dt))

        def sem(name):
            return ctx.enter_context(nc.semaphore(f"load_{name}"))

        names = ["src", "dst", "next"]
        rows = {n: sb(f"{n}_rows", [P, 2, P], I32) for n in names}
        rows_f = {n: sb(f"{n}_rows_f", [P, 2, P]) for n in names}
        zero = sb("zero", [P, 2512])
        worse = sb("worse", [P, 2])
        last_tile = sb("last_tile", [P, 2])
        tile_no = sb("tile_no", [P, TILES])
        light_no = sb("light_no", [P, TILES])
        flags = sb("flags", [1, 2])
        cols = {n: ctx.enter_context(nc.psum_tensor(f"{n}_cols", [P, 512], F32)) for n in ("src", "dst")}
        flag_rows = ctx.enter_context(nc.psum_tensor("flag_rows", [P, 512], F32))
        padded, edges_in, rows_ready, cols_ready = sem("padded"), sem("edges_in"), sem("rows_ready"), sem("cols_ready")
        consts_ready, zero_ready = sem("consts_ready"), sem("zero_ready")
        weights_in, copied, zeroed, padded_out = sem("weights_in"), sem("copied"), sem("zeroed"), sem("padded_out")
        flags_ready, flags_out, dve_step, pool_step = sem("flags_ready"), sem("flags_out"), sem("dve_step"), sem("pool_step")
        with nc.Block() as block:
            @block.sync
            def _(sp):
                sp.wait_ge(padded, 3)
                full = E // P - P
                rest = E - (P + full) * P
                count = 0
                for name, flat, off in (("src", a["src"], 0), ("dst", a["dst"], 0), ("next", a["dst"], 1)):
                    left = rest - off
                    sp.dma_start(rows[name][:, 0, :], flat[off:off + P * P].rearrange("(t p) -> t p", p=P)).then_inc(edges_in, 16)
                    sp.dma_start(rows[name][0:full, 1, :],
                                 flat[off + P * P:off + (P + full) * P].rearrange("(t p) -> t p", p=P)).then_inc(edges_in, 16)
                    sp.dma_start(rows[name][full:full + 1, 1, 0:left],
                                 flat[off + (P + full) * P:E].rearrange("(a p) -> a p", a=1)).then_inc(edges_in, 16)
                    count += 48
                sp.wait_ge(edges_in, count)
                for name, table in (("src", net.src_padded), ("dst", net.dst_padded)):
                    sp.dma_start(table[0:P, :], rows[name][:, 0, :]).then_inc(padded_out, 16)
                    sp.dma_start(table[P:TILES, :], rows[name][0:ROWS2, 1, :]).then_inc(padded_out, 16)
                sp.dma_start(net.x1[0:N, :].rearrange("(a b) f -> a (b f)", b=50),
                             a["x"].rearrange("(a b) f -> a (b f)", b=50)).then_inc(copied, 16)
                sp.wait_ge(padded_out, 64)
                sp.wait_ge(copied, 16)

            @block.scalar
            def _(act):
                act.wait_ge(zero_ready, 4)
                small = [(net.conv_w[0][:, :], a["L0_gnn_W1"]), (net.conv_w[1][:, :], a["L0_gnn_W2"])]
                for i, name in enumerate(("L0_gnn_b1", "L0_gnn_b2")):
                    small.append((net.conv_b[i][:, :], a[name].rearrange("(o f) -> o f", o=1).broadcast_to([P, F])))
                for i in range(3):
                    for h in range(2):
                        part = slice(h * F, (h + 1) * F)
                        small.append((net.gcn_w[i][part, part], a[f"L1_gnn_W{i + 1}"]))
                        for table, name in ((net.gcn_b, "b"), (net.gamma, "gamma"), (net.beta, "beta")):
                            small.append((table[part, i:i + 1], a[f"L1_gnn_{name}{i + 1}"].rearrange("(f o) -> f o", o=1)))
                for dst, src in small:
                    act.dma_start(dst, src).then_inc(weights_in, 16)
                act.dma_start(net.hyper1.rearrange("(p r) f -> p (r f)", p=P), zero[:, 0:HROWS // P * HW]).then_inc(zeroed, 16)
                act.dma_start(net.hyper2.rearrange("(p r) f -> p (r f)", p=P), zero[:, 0:HROWS // P * HW]).then_inc(zeroed, 16)
                act.dma_start(net.v[NP:NP + P, :], zero[:, 0:F]).then_inc(zeroed, 16)
                pads = (NP + P - N) * F // P
                act.dma_start(net.x1[N:NP + P, :].rearrange("(p r) f -> p (r f)", p=30),
                              zero[0:30, 0:(NP + P - N) * F // 30]).then_inc(zeroed, 16)
                width = (NP + P) * F // P
                conv = net.conv.rearrange("(p r) f -> p (r f)", p=P)
                for q in range(width // 2512):
                    act.dma_start(conv[:, q * 2512:(q + 1) * 2512], zero[:, :]).then_inc(zeroed, 16)
                act.wait_ge(weights_in, 16 * len(small))
                act.wait_ge(zeroed, 16 * (4 + width // 2512))

            @block.gpsimd
            def _(pool):
                for name in names:
                    nc.gpsimd.memset(rows[name][:, :, :], PAD_NODE).then_inc(padded, 1)
                for w in net.gcn_w:
                    nc.gpsimd.memset(w[:, :], 0.0).then_inc(zero_ready, 1)
                nc.gpsimd.memset(zero[:, :], 0.0).then_inc(zero_ready, 1)
                nc.gpsimd.memset(net.eps[:, :], EPS).then_inc(consts_ready, 1)
                step = Chain(pool, pool_step)
                step(nc.gpsimd.memset(net.ident[:, :], 0.0))
                nc.gpsimd.affine_select(out=net.ident[:, :], in_=net.ident[:, :], compare_op=ALU.not_equal, fill=1.0,
                                        base=0, pattern=[[-1, P]], channel_multiplier=1).then_inc(consts_ready, 1)
                step(nc.gpsimd.memset(net.before[:, :], 1.0))
                nc.gpsimd.affine_select(out=net.before[:, :], in_=net.before[:, :], compare_op=ALU.is_gt, fill=0.0,
                                        base=0, pattern=[[-1, P]], channel_multiplier=1).then_inc(consts_ready, 1)
                step(nc.gpsimd.memset(net.pair_mean[:, :], 0.0))
                for off in (-F, 0, F):
                    step(nc.gpsimd.affine_select(out=net.pair_mean[:, :], in_=net.pair_mean[:, :],
                                                 compare_op=ALU.not_equal, fill=0.5, base=off,
                                                 pattern=[[-1, P]], channel_multiplier=1))
                nc.gpsimd.iota(net.part[:, :], pattern=[[0, 1]], base=0, channel_multiplier=1,
                               allow_small_or_imprecise_dtypes=True).then_inc(consts_ready, 1)
                nc.gpsimd.iota(tile_no[:, :], pattern=[[1, TILES]], base=1, channel_multiplier=0,
                               allow_small_or_imprecise_dtypes=True).then_inc(consts_ready, 1)

            @block.vector
            def _(dve):
                step = Chain(dve, dve_step)
                dve.wait_ge(edges_in, 144)
                for name in names:
                    nc.vector.tensor_copy(rows_f[name][:, :, :], rows[name][:, :, :]).then_inc(rows_ready, 1)
                dve.wait_ge(consts_ready, 5)
                dve.wait_ge(rows_ready, 3)
                step(nc.vector.tensor_tensor(rows_f["next"][:, :, :], rows_f["dst"][:, :, :], rows_f["next"][:, :, :], ALU.is_gt))
                step(nc.vector.tensor_reduce(worse[:, :], rows_f["next"][:, :, :], AX.X, ALU.max))
                step(nc.vector.tensor_reduce(last_tile[:, 1:2], worse[:, :], AX.X, ALU.max))
                dve.wait_ge(cols_ready, 4)
                for name, table in (("src", net.src_f), ("dst", net.dst_f)):
                    step(nc.vector.tensor_copy(table[:, :], cols[name][:, 0:TILES]))
                step(nc.vector.tensor_copy(net.src_idx[:, :], net.src_f[:, :]))
                step(nc.vector.tensor_scalar(net.light[:, :], net.dst_f[:, :], float(HYPER), None, ALU.is_lt))
                step(nc.vector.tensor_scalar(net.clip_idx[:, :], net.dst_f[:, :], float(HYPER - 1), None, ALU.min))
                step(nc.vector.tensor_tensor(light_no[:, :], net.light[:, :], tile_no[:, :], ALU.mult))
                step(nc.vector.tensor_reduce(last_tile[:, 0:1], light_no[:, :], AX.X, ALU.max))
                nc.vector.tensor_scalar(last_tile[:, 0:1], last_tile[:, 0:1], 1.0, None, ALU.max).then_inc(flags_ready, 1)
                dve.wait_ge(flags_out, 2)
                for k in range(2):
                    step(nc.vector.tensor_reduce(flags[:, k:k + 1], flag_rows[0:1, k * P:(k + 1) * P], AX.X, ALU.max))
                step(nc.vector.tensor_copy(net.bounds[:, :], flags[:, :]))

            @block.tensor
            def _(pe):
                pe.wait_ge(consts_ready, 5)
                pe.wait_ge(rows_ready, 3)
                for name in ("src", "dst"):
                    nc.tensor.transpose(cols[name][:, 0:P], rows_f[name][:, 0, :], net.ident[:, :]).then_inc(cols_ready, 1)
                    nc.tensor.transpose(cols[name][:, P:TILES], rows_f[name][0:ROWS2, 1, :],
                                        net.ident[0:ROWS2, 0:ROWS2]).then_inc(cols_ready, 1)
                pe.wait_ge(flags_ready, 1)
                for k in range(2):
                    nc.tensor.transpose(flag_rows[0:1, k * P:(k + 1) * P], last_tile[:, k:k + 1], net.ident[:, :]).then_inc(flags_out, 1)


def count_nodes(net):
    nc = net.nc
    half = COLS // 2
    with ExitStack() as ctx:
        def sb(name, shape, dt=F32):
            return ctx.enter_context(nc.sbuf_tensor(f"count_{name}", shape, dt))

        def sem(name):
            return ctx.enter_context(nc.semaphore(f"count_{name}"))

        iota_col = sb("iota_col", [P, COLS], F16)
        iota_part = sb("iota_part", [P, P], F16)
        ints = [sb(f"ints{i}", [P, TILES], I32) for i in range(3)]
        col_f = {n: sb(f"{n}_col", [P, TILES]) for n in ("src", "dst")}
        part_f = {n: sb(f"{n}_part", [P, TILES]) for n in ("src", "dst")}
        hot_col = {n: [sb(f"{n}_hot_col{i}", [P, COLS], F16) for i in range(2)] for n in ("src", "dst")}
        hot_part = {n: [sb(f"{n}_hot_part{i}", [P, P], F16) for i in range(2)] for n in ("src", "dst")}
        nothing = sb("nothing", [P, 512], F16)
        dst_row = [sb(f"dst_row{i}", [P, LANES, P], I32) for i in range(2)]
        same = [sb(f"same{i}", [P, LANES, P]) for i in range(2)]
        earlier = sb("earlier", [P, LANES, P])
        n_earlier = sb("n_earlier", [P, TILES])
        first = sb("first", [P, TILES])
        row = sb("row", [P, TILES])
        dummy = sb("dummy", [P, 1])
        members = sb("members", [P, COLS])
        pairs = sb("pairs", [P, COLS, 2])
        names = ("dst", "src", "light")
        counts = {n: [ctx.enter_context(nc.psum_tensor(f"{n}_count{h}", [P, 512], F32)) for h in range(2)] for n in names}
        iotas_ready, hots_ready, hots_used = sem("iotas_ready"), [sem("hots_ready0"), sem("hots_ready1")], [sem("hots_used0"), sem("hots_used1")]
        light_hot, light_used, counted = sem("light_hot"), sem("light_used"), sem("counted")
        rows_in = [sem("rows_in0"), sem("rows_in1")]
        rows_used = [sem("rows_used0"), sem("rows_used1")]
        same_out = [sem("same_out0"), sem("same_out1")]
        dve_step, earlier_step, degree_ready, root_ready = sem("dve_step"), sem("earlier_step"), sem("degree_ready"), sem("root_ready")
        scalars_ready, scalars_out = sem("scalars_ready"), sem("scalars_out")
        dst_rows = net.dst_padded.rearrange("(u i) k -> i u k", u=LANES)

        with nc.Block() as block:
            @block.gpsimd
            def _(pool):
                nc.gpsimd.iota(iota_col[:, :], pattern=[[1, COLS]], base=0, channel_multiplier=0,
                               allow_small_or_imprecise_dtypes=True).then_inc(iotas_ready, 1)
                nc.gpsimd.iota(iota_part[:, :], pattern=[[1, P]], base=0, channel_multiplier=0,
                               allow_small_or_imprecise_dtypes=True).then_inc(iotas_ready, 1)
                nc.gpsimd.memset(nothing[:, :], 0.0).then_inc(iotas_ready, 1)

            @block.sync
            def _(sp):
                with sp.Fori(0, STEPS // 2) as i:
                    for k in range(2):
                        sp.wait_ge(rows_used[k], i)
                        sp.dma_start(dst_row[k][:, :, :],
                                     dst_rows[bass.ds(2 * i + k, 1), :, :].broadcast_to([P, LANES, P])).then_inc(rows_in[k], 16)

            @block.scalar
            def _(act):
                with act.Fori(0, STEPS // 2) as i:
                    for k in range(2):
                        act.wait_ge(rows_used[k], i + 1)
                        act.dma_start(chunk_of(net.same_dst, 2 * i + k),
                                      same[k][:, :, :].rearrange("p u k -> p (u k)")).then_inc(same_out[k], 16)
                for k in range(2):
                    act.wait_ge(same_out[k], 16 * (STEPS // 2))
                act.wait_ge(degree_ready, 1)
                nc.scalar.activation(net.dinv[:, :], net.dinv[:, :], ACT.Sqrt).then_inc(root_ready, 1)
                act.wait_ge(scalars_ready, 1)
                act.dma_start(net.node_scalars.rearrange("(c p g) w -> p c (g w)", p=P, g=G),
                              pairs[:, :, :].rearrange("p (c g) w -> p c (g w)", g=G)).then_inc(scalars_out, 16)
                act.wait_ge(scalars_out, 16)

            @block.vector
            def _(dve):
                step = Chain(dve, dve_step)
                for name, table in (("src", net.src_f), ("dst", net.dst_f)):
                    step(nc.vector.tensor_copy(ints[0][:, :], table[:, :]))
                    step(nc.vector.tensor_scalar(ints[1][:, :], ints[0][:, :], 11, 4, ALU.logical_shift_right, ALU.logical_shift_left))
                    step(nc.vector.tensor_scalar(ints[2][:, :], ints[0][:, :], G - 1, None, ALU.bitwise_and))
                    step(nc.vector.tensor_tensor(col_f[name][:, :], ints[1][:, :], ints[2][:, :], ALU.add))
                    step(nc.vector.tensor_scalar(ints[1][:, :], ints[0][:, :], 4, P - 1, ALU.logical_shift_right, ALU.bitwise_and))
                    step(nc.vector.tensor_copy(part_f[name][:, :], ints[1][:, :]))
                dve.wait_ge(iotas_ready, 3)
                with dve.Fori(0, TILES // 2) as i:
                    for k in range(2):
                        dve.wait_ge(hots_used[k], i)
                        for name in ("dst", "src"):
                            nc.vector.tensor_scalar(hot_col[name][k][:, :], iota_col[:, :],
                                                    col_f[name][:, bass.ds(2 * i + k, 1)], None, ALU.is_equal).then_inc(hots_ready[k], 1)
                            nc.vector.tensor_scalar(hot_part[name][k][:, :], iota_part[:, :],
                                                    part_f[name][:, bass.ds(2 * i + k, 1)], None, ALU.is_equal).then_inc(hots_ready[k], 1)
                for k in range(2):
                    dve.wait_ge(hots_used[k], TILES // 2)
                n_light = dve.value_load(net.bounds[0:1, 0:1], min_val=1, max_val=TILES)
                with dve.Fori(0, n_light) as i:
                    dve.wait_ge(light_used, i)
                    nc.vector.tensor_scalar(hot_col["src"][0][:, :], iota_col[:, :],
                                            col_f["src"][:, bass.ds(i, 1)], None, ALU.is_equal).then_inc(light_hot, 1)
                    nc.vector.tensor_scalar(hot_part["src"][0][:, :], iota_part[:, :],
                                            part_f["src"][:, bass.ds(i, 1)], net.light[:, bass.ds(i, 1)],
                                            ALU.is_equal, ALU.mult).then_inc(light_hot, 1)
                dst_cols = net.dst_f[:, :].rearrange("p (u i) -> p i u", u=LANES)
                earlier_cols = n_earlier[:, :].rearrange("p (u i) -> p i u", u=LANES)
                with dve.Fori(0, STEPS // 2) as i:
                    for k in range(2):
                        dve.wait_ge(rows_in[k], 16 * i + 16)
                        dve.wait_ge(same_out[k], 16 * i)
                        col = dst_cols[:, bass.ds(2 * i + k, 1), :].rearrange("p a u -> p (a u)")
                        nc.vector.tensor_tensor(same[k][:, :, :], dst_row[k][:, :, :],
                                                col.rearrange("p (u o) -> p u o", o=1).broadcast_to([P, LANES, P]),
                                                ALU.is_equal).then_inc(rows_used[k], 1)
                        dve.wait_ge(rows_used[k], i + 1)
                        nc.vector.tensor_tensor(earlier[:, :, :], same[k][:, :, :],
                                                net.before[:, :].rearrange("p (o k) -> p o k", o=1).broadcast_to([P, LANES, P]),
                                                ALU.mult).then_inc(earlier_step, 1)
                        dve.wait_ge(earlier_step, 4 * i + (2 * k + 1))
                        nc.vector.tensor_reduce(earlier_cols[:, bass.ds(2 * i + k, 1), :].rearrange("p a u -> p (a u)"),
                                                earlier[:, :, :], AX.X, ALU.add).then_inc(earlier_step, 1)
                        dve.wait_ge(earlier_step, 4 * i + (2 * k + 2))
                step(nc.vector.tensor_scalar(first[:, :], n_earlier[:, :], 0.0, None, ALU.is_equal))
                step(nc.vector.tensor_scalar(dummy[:, :], net.part[:, :], float(DUMMY), None, ALU.add))
                step(nc.vector.tensor_scalar(row[:, :], net.dst_f[:, :], dummy[:, :], None, ALU.subtract))
                step(nc.vector.tensor_tensor(row[:, :], row[:, :], first[:, :], ALU.mult))
                step(nc.vector.tensor_scalar(net.dst_idx[:, :], row[:, :], dummy[:, :], None, ALU.add))
                step(nc.vector.tensor_scalar(dummy[:, :], net.part[:, :], float(HDUMMY), None, ALU.add))
                step(nc.vector.tensor_scalar(row[:, :], net.dst_f[:, :], dummy[:, :], None, ALU.subtract))
                step(nc.vector.tensor_tensor(row[:, :], row[:, :], first[:, :], ALU.mult))
                step(nc.vector.tensor_tensor(row[:, :], row[:, :], net.light[:, :], ALU.mult))
                step(nc.vector.tensor_scalar(net.light_idx[:, :], row[:, :], dummy[:, :], None, ALU.add))
                dve.wait_ge(counted, 1)
                far, inverse = pairs[:, :, 0], pairs[:, :, 1]
                for h in range(2):
                    part = slice(h * half, (h + 1) * half)
                    step(nc.vector.tensor_scalar(net.dinv[:, part], counts["dst"][h][:, 0:half], 1.0, None, ALU.add))
                    step(nc.vector.tensor_copy(members[:, part], counts["src"][h][:, 0:half]))
                    step(nc.vector.tensor_tensor(far[:, part], members[:, part], counts["light"][h][:, 0:half], ALU.subtract))
                dve.engine_nop().then_inc(degree_ready, 1)
                step(nc.vector.tensor_scalar(members[:, :], members[:, :], 1.0, None, ALU.max))
                step(nc.vector.reciprocal(inverse, members[:, :]))
                nc.vector.tensor_tensor(net.far_share[:, :], far, inverse, ALU.mult).then_inc(scalars_ready, 1)
                dve.wait_ge(root_ready, 1)
                step(nc.vector.reciprocal(net.dinv[:, :], net.dinv[:, :]))

            @block.tensor
            def _(pe):
                pe.wait_ge(iotas_ready, 3)
                for n in names:
                    for h in range(2):
                        last = nc.tensor.matmul(counts[n][h][:, :], nothing[:, 0:P], nothing[:, :], start=True, stop=False)
                with pe.Fori(0, TILES // 2) as i:
                    for k in range(2):
                        pe.wait_ge(hots_ready[k], 4 * i + 4)
                        for name in ("dst", "src"):
                            for h in range(2):
                                last = nc.tensor.matmul(counts[name][h][:, 0:half], hot_part[name][k][:, :],
                                                        hot_col[name][k][:, h * half:(h + 1) * half], start=False, stop=False)
                        last.then_inc(hots_used[k], 1)
                n_light = pe.value_load(net.bounds[0:1, 0:1], min_val=1, max_val=TILES)
                with pe.Fori(0, n_light) as i:
                    pe.wait_ge(light_hot, 2 * i + 2)
                    for h in range(2):
                        last = nc.tensor.matmul(counts["light"][h][:, 0:half], hot_part["src"][0][:, :],
                                                hot_col["src"][0][:, h * half:(h + 1) * half], start=False, stop=False)
                    last.then_inc(light_used, 1)
                for n in names:
                    for h in range(2):
                        last = nc.tensor.matmul(counts[n][h][:, :], nothing[:, 0:P], nothing[:, :], start=False, stop=True)
                last.then_inc(counted, 1)


def nodes_to_hyperedges(net, stage):
    nc = net.nc
    table = (net.hyper1, net.hyper2)[stage]
    source = net.args["x"] if stage == 0 else net.conv
    with ExitStack() as ctx:
        def sb(name, shape, dt=F32):
            return ctx.enter_context(nc.sbuf_tensor(f"h{stage}_{name}", shape, dt))

        def sem(name):
            return ctx.enter_context(nc.semaphore(f"h{stage}_{name}"))

        src_i, to_i = sb("src_i", [P, 1], I32), sb("to_i", [P, 1], I32)
        got, scal, stats, mv = sb("got", [P, F]), sb("scal", [P, 2]), sb("stats", [P, 6]), sb("mv", [P, 2])
        root, shift = sb("root", [P, 1]), sb("shift", [P, 1])
        act_row, msg, summed = sb("act_row", [P, F]), sb("msg", [P, HW]), sb("summed", [P, HW])
        same = sb("same", [P, P])
        sums = ctx.enter_context(nc.psum_tensor(f"h{stage}_sums", [P, 512], F32))
        idx_ready, gathered, same_in = sem("idx_ready"), sem("gathered"), sem("same_in")
        if stage == 0:
            root_in, root_out = sem("root_in"), sem("root_out")
        act_in, act_out, msg_ready, sums_ready, summed_ready, added = sem("act_in"), sem("act_out"), sem("msg_ready"), sem("sums_ready"), sem("summed_ready"), sem("added")
        dve_step = sem("dve_step")
        n_steps = 3 if stage == 0 else 2
        gathers = 16 if stage == 0 else 32

        with nc.Block() as block:
            @block.sync
            def _(sp):
                n_light = sp.value_load(net.bounds[0:1, 0:1], min_val=1, max_val=TILES)
                tiles = net.same_dst.rearrange("i p (u k) -> u i p k", u=LANES)
                with sp.Fori(0, n_light) as i:
                    sp.wait_ge(sums_ready, i)
                    sp.dma_start(same[:, :], tiles[bass.ds(i // STEPS, 1), bass.ds(i % STEPS, 1), :, :]
                                 .rearrange("a b p k -> (a b p) k")).then_inc(same_in, 16)

            @block.gpsimd
            def _(pool):
                n_light = pool.value_load(net.bounds[0:1, 0:1], min_val=1, max_val=TILES)
                with pool.Fori(0, n_light) as i:
                    wait_alone(pool, idx_ready, 2 * i + 2, net)
                    at = bass.IndirectOffsetOnAxis(ap=src_i[:, :], axis=0)
                    pool.indirect_dma_start(out=got[:, :], out_offset=None, in_=source[:, :], in_offset=at).then_inc(gathered, 16)
                    if stage == 1:
                        pool.indirect_dma_start(out=scal[:, :], out_offset=None, in_=net.node_scalars[:, :],
                                                in_offset=at).then_inc(gathered, 16)
                    wait_alone(pool, summed_ready, i + 1, net)
                    pool.indirect_dma_start(out=table[:, :], out_offset=bass.IndirectOffsetOnAxis(ap=to_i[:, :], axis=0),
                                            in_=summed[:, :], in_offset=None, compute_op=ALU.add).then_inc(added, 16)
                    pool.wait_ge(added, 16 * i + 16)

            @block.vector
            def _(dve):
                n_light = dve.value_load(net.bounds[0:1, 0:1], min_val=1, max_val=TILES)
                with dve.Fori(0, n_light) as i:
                    step = Chain(dve, dve_step, i * n_steps, net)
                    wait_alone(dve, added, 16 * i, net)
                    nc.vector.tensor_copy(src_i[:, :], net.src_idx[:, bass.ds(i, 1)]).then_inc(idx_ready, 1)
                    nc.vector.tensor_copy(to_i[:, :], net.light_idx[:, bass.ds(i, 1)]).then_inc(idx_ready, 1)
                    dve.wait_ge(gathered, gathers * i + gathers)
                    if stage == 0:
                        step(nc.vector.bn_stats(stats[:, :], got[:, :]))
                        nc.vector.bn_aggr(mv[:, :], stats[:, :]).then_inc(root_in, 1)
                        dve.wait_ge(root_out, i + 1)
                        step(nc.vector.reciprocal(root[:, :], root[:, :]))
                        nc.vector.tensor_scalar(shift[:, :], mv[:, 0:1], root[:, :], -1.0, ALU.mult, ALU.mult).then_inc(act_in, 1)
                    else:
                        step(nc.vector.scalar_tensor_tensor(out=got[:, :], in0=net.e1_last[:, :], scalar=scal[:, 0:1],
                                                            in1=got[:, :], op0=ALU.mult, op1=ALU.add))
                        nc.vector.scalar_tensor_tensor(out=act_row[:, :], in0=got[:, :], scalar=scal[:, 1:2],
                                                       in1=net.conv_b[0][:, :], op0=ALU.mult, op1=ALU.add).then_inc(act_in, 1)
                    dve.wait_ge(act_out, i + 1)
                    step(nc.vector.tensor_scalar(msg[:, 0:F], act_row[:, :], net.light[:, bass.ds(i, 1)], None, ALU.mult))
                    nc.vector.tensor_copy(msg[:, F:HW], net.light[:, bass.ds(i, 1)]).then_inc(msg_ready, 1)
                    dve.wait_ge(sums_ready, i + 1)
                    nc.vector.tensor_copy(summed[:, :], sums[:, 0:HW]).then_inc(summed_ready, 1)

            @block.scalar
            def _(act):
                n_light = act.value_load(net.bounds[0:1, 0:1], min_val=1, max_val=TILES)
                with act.Fori(0, n_light) as i:
                    if stage == 0:
                        act.wait_ge(root_in, i + 1)
                        nc.scalar.activation(root[:, :], mv[:, 1:2], ACT.Sqrt, bias=net.eps[:, :]).then_inc(root_out, 1)
                        act.wait_ge(act_in, i + 1)
                        nc.scalar.activation(act_row[:, :], got[:, :], ACT.Relu, bias=shift[:, :], scale=root[:, :]).then_inc(act_out, 1)
                    else:
                        act.wait_ge(act_in, i + 1)
                        nc.scalar.activation(act_row[:, :], act_row[:, :], ACT.Relu).then_inc(act_out, 1)

            @block.tensor
            def _(pe):
                n_light = pe.value_load(net.bounds[0:1, 0:1], min_val=1, max_val=TILES)
                with pe.Fori(0, n_light) as i:
                    pe.wait_ge(msg_ready, i + 1)
                    pe.wait_ge(same_in, 16 * i + 16)
                    nc.tensor.matmul(sums[:, 0:HW], same[:, :], msg[:, :], start=True, stop=True).then_inc(sums_ready, 1)


def hyperedges_to_nodes(net, stage):
    nc = net.nc
    table = (net.hyper1, net.hyper2)[stage]
    target = (net.conv, net.x1)[stage]
    last_row = (net.e1_last, net.e2_last)[stage]
    with ExitStack() as ctx:
        def sb(name, shape, dt=F32):
            return ctx.enter_context(nc.sbuf_tensor(f"n{stage}_{name}", shape, dt))

        def sem(name):
            return ctx.enter_context(nc.semaphore(f"n{stage}_{name}"))

        from_i, src_i, to_i, src_row = sb("from_i", [P, 1], I32), sb("src_i", [P, 1], I32), sb("to_i", [P, 1], I32), sb("src_row", [P, P], I32)
        got, last_got, scal, inverse = sb("got", [P, HW]), sb("last_got", [P, HW]), sb("scal", [P, 2]), sb("inverse", [P, 1])
        mean, mean_t, msg, summed = sb("mean", [P, F]), sb("mean_t", [F, P]), sb("msg", [P, F]), sb("summed", [P, F])
        same, earlier, n_earlier, row, dummy = sb("same", [P, P]), sb("earlier", [P, P]), sb("n_earlier", [P, 1]), sb("row", [P, 1]), sb("dummy", [P, 1])
        turned = ctx.enter_context(nc.psum_tensor(f"n{stage}_turned", [P, 512], F32))
        product = ctx.enter_context(nc.psum_tensor(f"n{stage}_product", [P, 512], F32))
        sums = ctx.enter_context(nc.psum_tensor(f"n{stage}_sums", [P, 512], F32))
        last_in, idx_ready, to_ready, gathered, row_in = sem("last_in"), sem("idx_ready"), sem("to_ready"), sem("gathered"), sem("row_in")
        row_used, mean_ready, turned_ready, mean_t_ready, product_ready = sem("row_used"), sem("mean_ready"), sem("turned_ready"), sem("mean_t_ready"), sem("product_ready")
        msg_ready, sums_ready, summed_ready, added, dve_step = sem("msg_ready"), sem("sums_ready"), sem("summed_ready"), sem("added"), sem("dve_step")
        gathers = 16 if stage == 0 else 32
        n_steps = 7 if stage == 0 else 8
        before_loop = 5

        with nc.Block() as block:
            @block.sync
            def _(sp):
                sp.dma_start(last_got[:, :], table[HYPER - 1:HYPER, :].broadcast_to([P, HW])).then_inc(last_in, 16)
                n_light = sp.value_load(net.bounds[0:1, 0:1], min_val=1, max_val=TILES)
                with sp.Fori(0, n_light) as i:
                    sp.wait_ge(row_used, i)
                    sp.dma_start(src_row[:, :], net.src_padded[bass.ds(i, 1), :].broadcast_to([P, P])).then_inc(row_in, 16)

            @block.gpsimd
            def _(pool):
                n_light = pool.value_load(net.bounds[0:1, 0:1], min_val=1, max_val=TILES)
                with pool.Fori(0, n_light) as i:
                    wait_alone(pool, idx_ready, 2 * i + 2, net)
                    pool.indirect_dma_start(out=got[:, :], out_offset=None, in_=table[:, :],
                                            in_offset=bass.IndirectOffsetOnAxis(ap=from_i[:, :], axis=0)).then_inc(gathered, 16)
                    if stage == 1:
                        pool.indirect_dma_start(out=scal[:, :], out_offset=None, in_=net.node_scalars[:, :],
                                                in_offset=bass.IndirectOffsetOnAxis(ap=src_i[:, :], axis=0)).then_inc(gathered, 16)
                    pool.wait_ge(to_ready, i + 1)
                    wait_alone(pool, summed_ready, i + 1, net)
                    pool.indirect_dma_start(out=target[:, :], out_offset=bass.IndirectOffsetOnAxis(ap=to_i[:, :], axis=0),
                                            in_=summed[:, :], in_offset=None, compute_op=ALU.add).then_inc(added, 16)
                    pool.wait_ge(added, 16 * i + 16)

            @block.vector
            def _(dve):
                def to_mean(step, rows):
                    step(nc.vector.tensor_scalar(inverse[:, :], rows[:, F:HW], 1.0, None, ALU.max))
                    step(nc.vector.reciprocal(inverse[:, :], inverse[:, :]))
                    nc.vector.tensor_scalar(mean[:, :], rows[:, 0:F], inverse[:, :], None, ALU.mult).then_inc(mean_ready, 1)

                step = Chain(dve, dve_step)
                step(nc.vector.tensor_scalar(dummy[:, :], net.part[:, :], float(DUMMY), None, ALU.add))
                dve.wait_ge(last_in, 16)
                to_mean(step, last_got)
                dve.wait_ge(turned_ready, 1)
                nc.vector.tensor_copy(mean_t[:, :], turned[0:F, 0:P]).then_inc(mean_t_ready, 1)
                dve.wait_ge(product_ready, 1)
                step(nc.vector.tensor_copy(last_row[:, :], product[:, 0:F]))
                step(nc.vector.tensor_scalar(inverse[:, :], inverse[:, :], 1.0, None, ALU.mult))
                assert step.n == before_loop
                n_light = dve.value_load(net.bounds[0:1, 0:1], min_val=1, max_val=TILES)
                with dve.Fori(0, n_light) as i:
                    step = Chain(dve, dve_step, i * n_steps + before_loop)
                    wait_alone(dve, added, 16 * i, net)
                    nc.vector.tensor_copy(from_i[:, :], net.clip_idx[:, bass.ds(i, 1)]).then_inc(idx_ready, 1)
                    nc.vector.tensor_copy(src_i[:, :], net.src_idx[:, bass.ds(i, 1)]).then_inc(idx_ready, 1)
                    dve.wait_ge(row_in, 16 * i + 16)
                    nc.vector.tensor_scalar(same[:, :], src_row[:, :], net.src_f[:, bass.ds(i, 1)], None, ALU.is_equal).then_inc(row_used, 1)
                    dve.wait_ge(row_used, i + 1)
                    step(nc.vector.tensor_tensor(earlier[:, :], same[:, :], net.before[:, :], ALU.mult))
                    step(nc.vector.tensor_reduce(n_earlier[:, :], earlier[:, :], AX.X, ALU.add))
                    step(nc.vector.tensor_scalar(n_earlier[:, :], n_earlier[:, :], 0.0, None, ALU.is_equal))
                    step(nc.vector.tensor_scalar(row[:, :], net.src_f[:, bass.ds(i, 1)], dummy[:, :], n_earlier[:, :], ALU.subtract, ALU.mult))
                    nc.vector.tensor_scalar(to_i[:, :], row[:, :], dummy[:, :], None, ALU.add).then_inc(to_ready, 1)
                    dve.wait_ge(gathered, gathers * i + gathers)
                    to_mean(step, got)
                    dve.wait_ge(turned_ready, i + 2)
                    nc.vector.tensor_copy(mean_t[:, :], turned[0:F, 0:P]).then_inc(mean_t_ready, 1)
                    dve.wait_ge(product_ready, i + 2)
                    if stage == 0:
                        step(nc.vector.tensor_copy(mean[:, :], product[:, 0:F]))
                        nc.vector.tensor_scalar(msg[:, :], mean[:, :], net.light[:, bass.ds(i, 1)], None, ALU.mult).then_inc(msg_ready, 1)
                    else:
                        step(nc.vector.tensor_copy(mean[:, :], product[:, 0:F]))
                        step(nc.vector.tensor_scalar(mean[:, :], mean[:, :], scal[:, 1:2], None, ALU.mult))
                        nc.vector.tensor_scalar(msg[:, :], mean[:, :], net.light[:, bass.ds(i, 1)], None, ALU.mult).then_inc(msg_ready, 1)
                    dve.wait_ge(sums_ready, i + 1)
                    nc.vector.tensor_copy(summed[:, :], sums[:, 0:F]).then_inc(summed_ready, 1)
                    assert step.n == n_steps

            @block.tensor
            def _(pe):
                def through_w(n):
                    wait_alone(pe, mean_ready, n, net)
                    nc.tensor.transpose(turned[0:F, 0:P], mean[:, :], net.ident[:, :]).then_inc(turned_ready, 1)
                    pe.wait_ge(mean_t_ready, n)
                    nc.tensor.matmul(product[:, 0:F], mean_t[:, :], net.conv_w[stage][:, :], start=True, stop=True).then_inc(product_ready, 1)

                through_w(1)
                n_light = pe.value_load(net.bounds[0:1, 0:1], min_val=1, max_val=TILES)
                with pe.Fori(0, n_light) as i:
                    through_w(i + 2)
                    pe.wait_ge(msg_ready, i + 1)
                    nc.tensor.matmul(sums[:, 0:F], same[:, :], msg[:, :], start=True, stop=True).then_inc(sums_ready, 1)


def norm_nodes(net):
    nc = net.nc
    with ExitStack() as ctx:
        def sb(name, shape, dt=F32):
            return ctx.enter_context(nc.sbuf_tensor(f"ln_{name}", shape, dt))

        def sem(name):
            return ctx.enter_context(nc.semaphore(f"ln_{name}"))

        S = 2
        bias = sb("bias", [P, G, F])
        xt = [sb(f"xt{k}", [P, G, F]) for k in range(S)]
        far = [sb(f"far{k}", [P, G, F]) for k in range(S)]
        dev = [sb(f"dev{k}", [P, G, F]) for k in range(S)]
        sq = [sb(f"sq{k}", [P, G, F]) for k in range(S)]
        h = [sb(f"h{k}", [P, G, F]) for k in range(S)]
        mean = [sb(f"mean{k}", [P, G]) for k in range(S)]
        var = [sb(f"var{k}", [P, G]) for k in range(S)]
        scale = [sb(f"scale{k}", [P, G]) for k in range(S)]
        bias_ready = sem("bias_ready")
        loaded, far_ready, far_step, x_ready, dev_ready, sq_ready = ([sem(f"{n}{k}") for k in range(S)] for n in
            ("loaded", "far_ready", "far_step", "x_ready", "dev_ready", "sq_ready"))
        var_ready, root_ready, scaled, h_ready, stored = ([sem(f"{n}{k}") for k in range(S)] for n in
            ("var_ready", "root_ready", "scaled", "h_ready", "stored"))
        dve_step = [sem(f"dve_step{k}") for k in range(S)]
        x1, y, v = node_chunks(net.x1), node_chunks(net.y), node_chunks(net.v)

        def over_features(t):
            return t.rearrange("p (g o) -> p g o", o=1).broadcast_to([P, G, F])

        def flat(t):
            return t[:, :, :].rearrange("p g f -> p (g f)")

        def rounds(engine, body):
            with engine.Fori(0, NC // S) as i:
                for k in range(S):
                    body(i, k, i * S + k)
            body(NC // S, 0, NC - 1)

        with nc.Block() as block:
            @block.sync
            def _(sp):
                def body(i, k, c):
                    sp.wait_ge(stored[k], 48 * i)
                    sp.dma_start(flat(xt[k]), chunk_of(x1, c)).then_inc(loaded[k], 16)
                rounds(sp, body)

            @block.gpsimd
            def _(pool):
                nc.gpsimd.tensor_copy(bias[:, :, :], net.conv_b[1][:, :].rearrange("p (o f) -> p o f", o=1).broadcast_to([P, G, F])).then_inc(bias_ready, 1)
                pool.wait_ge(bias_ready, 1)

                def body(i, k, c):
                    pool.wait_ge(x_ready[k], i)
                    nc.gpsimd.tensor_tensor(far[k][:, :, :], over_features(net.far_share[:, bass.ds(c * G, G)]),
                                            net.e2_last[:, :].rearrange("p (o f) -> p o f", o=1).broadcast_to([P, G, F]),
                                            ALU.mult).then_inc(far_step[k], 1)
                    pool.wait_ge(far_step[k], i + 1)
                    nc.gpsimd.tensor_tensor(far[k][:, :, :], far[k][:, :, :], bias[:, :, :], ALU.add).then_inc(far_ready[k], 1)
                rounds(pool, body)

            @block.vector
            def _(dve):
                def body(i, k, c):
                    step = Chain(dve, dve_step[k], i * 3)
                    dve.wait_ge(loaded[k], 16 * i + 16)
                    dve.wait_ge(far_ready[k], i + 1)
                    nc.vector.tensor_tensor(xt[k][:, :, :], xt[k][:, :, :], far[k][:, :, :], ALU.add).then_inc(x_ready[k], 1)
                    dve.wait_ge(x_ready[k], i + 1)
                    step(nc.vector.tensor_reduce(mean[k][:, :], xt[k][:, :, :], AX.X, ALU.add))
                    step(nc.vector.tensor_scalar(mean[k][:, :], mean[k][:, :], 1.0 / F, None, ALU.mult))
                    nc.vector.tensor_tensor(dev[k][:, :, :], xt[k][:, :, :], over_features(mean[k][:, :]), ALU.subtract).then_inc(dev_ready[k], 1)
                    dve.wait_ge(sq_ready[k], i + 1)
                    nc.vector.tensor_reduce(var[k][:, :], sq[k][:, :, :], AX.X, ALU.add).then_inc(var_ready[k], 1)
                    dve.wait_ge(root_ready[k], i + 1)
                    step(nc.vector.reciprocal(scale[k][:, :], scale[k][:, :]))
                    nc.vector.tensor_tensor(scale[k][:, :], scale[k][:, :], net.dinv[:, bass.ds(c * G, G)], ALU.mult).then_inc(scaled[k], 1)
                    dve.wait_ge(scaled[k], 2 * i + 1)
                    nc.vector.tensor_tensor(dev[k][:, :, :], dev[k][:, :, :], over_features(scale[k][:, :]), ALU.mult).then_inc(scaled[k], 1)
                rounds(dve, body)

            @block.scalar
            def _(act):
                def body(i, k, c):
                    act.wait_ge(dev_ready[k], i + 1)
                    nc.scalar.activation(sq[k][:, :, :], dev[k][:, :, :], ACT.Square).then_inc(sq_ready[k], 1)
                    act.wait_ge(var_ready[k], i + 1)
                    nc.scalar.activation(scale[k][:, :], var[k][:, :], ACT.Sqrt, bias=net.eps[:, :], scale=1.0 / F).then_inc(root_ready[k], 1)
                    act.wait_ge(scaled[k], 2 * i + 2)
                    act.wait_ge(stored[k], 48 * i)
                    nc.scalar.activation(h[k][:, :, :], dev[k][:, :, :], ACT.Relu).then_inc(h_ready[k], 1)
                    act.dma_start(chunk_of(x1, c), flat(xt[k])).then_inc(stored[k], 16)
                    act.wait_ge(h_ready[k], i + 1)
                    act.dma_start(chunk_of(y, c), flat(h[k])).then_inc(stored[k], 16)
                    act.dma_start(chunk_of(v, c), flat(h[k])).then_inc(stored[k], 16)
                rounds(act, body)
                act.wait_ge(stored[0], 48 * (NC // S + 1))
                act.wait_ge(stored[1], 48 * (NC // S))


def add_edges(net, layer, sems):
    nc = net.nc
    with ExitStack() as ctx:
        def sb(name, shape, dt=F32):
            return ctx.enter_context(nc.sbuf_tensor(f"e{layer}_{name}", shape, dt))

        B = 2
        src_i = [sb(f"src_i{b}", [P, LANES], I32) for b in range(B)]
        dst_i = [sb(f"dst_i{b}", [P, LANES], I32) for b in range(B)]
        same = [sb(f"same{b}", [P, LANES, P]) for b in range(B)]
        got = [sb(f"got{b}", [P, LANES, F]) for b in range(B)]
        summed = [sb(f"summed{b}", [P, LANES, F]) for b in range(B)]
        sums = [ctx.enter_context(nc.psum_tensor(f"e{layer}_sums{b}", [P, 512], F32)) for b in range(B)]
        idx_ready, same_in, gathered, sums_ready, summed_ready, added = (sems[n] for n in
            ("idx_ready", "same_in", "gathered", "sums_ready", "summed_ready", "added"))
        done = layer * (STEPS // B)
        src_cols = net.src_idx[:, :].rearrange("p (u i) -> p i u", u=LANES)
        dst_cols = net.dst_idx[:, :].rearrange("p (u i) -> p i u", u=LANES)

        with nc.Block() as block:
            @block.sync
            def _(sp):
                with sp.Fori(0, STEPS // B) as i:
                    for b in range(B):
                        sp.wait_ge(sums_ready[b], done + i)
                        sp.dma_start(same[b][:, :, :].rearrange("p u k -> p (u k)"),
                                     chunk_of(net.same_dst, i * B + b)).then_inc(same_in[b], 16)

            @block.gpsimd
            def _(pool):
                with pool.Fori(0, STEPS // B) as i:
                    for b in range(B):
                        pool.wait_ge(idx_ready[b], 2 * done + 2 * i + 2)
                        wait_alone(pool, sums_ready[b], done + i, net)
                        for u in range(LANES):
                            pool.indirect_dma_start(out=got[b][:, u, :], out_offset=None, in_=net.y[:, :],
                                                    in_offset=bass.IndirectOffsetOnAxis(ap=src_i[b][:, u:u + 1], axis=0)
                                                    ).then_inc(gathered[b], 16)
                    for b in range(B):
                        wait_alone(pool, summed_ready[b], done + i + 1, net)
                        for u in range(LANES):
                            pool.indirect_dma_start(out=net.v[:, :],
                                                    out_offset=bass.IndirectOffsetOnAxis(ap=dst_i[b][:, u:u + 1], axis=0),
                                                    in_=summed[b][:, u, :], in_offset=None, compute_op=ALU.add
                                                    ).then_inc(added[b], 16)
                            wait_alone(pool, added[b], 16 * LANES * (done + i) + 16 * (u + 1), net)

            @block.vector
            def _(dve):
                with dve.Fori(0, STEPS // B) as i:
                    for b in range(B):
                        wait_alone(dve, added[b], 16 * LANES * (done + i), net)
                        for table, cols in ((src_i, src_cols), (dst_i, dst_cols)):
                            nc.vector.tensor_copy(table[b][:, :], cols[:, bass.ds(i * B + b, 1), :].rearrange("p a u -> p (a u)")
                                                  ).then_inc(idx_ready[b], 1)
                    for b in range(B):
                        dve.wait_ge(sums_ready[b], done + i + 1)
                        nc.vector.tensor_copy(summed[b][:, :, :].rearrange("p u f -> p (u f)"),
                                              sums[b][:, 0:LANES * F]).then_inc(summed_ready[b], 1)

            @block.tensor
            def _(pe):
                with pe.Fori(0, STEPS // B) as i:
                    for b in range(B):
                        pe.wait_ge(same_in[b], 16 * (done + i) + 16)
                        pe.wait_ge(gathered[b], 16 * LANES * (done + i) + 16 * LANES)
                        pe.wait_ge(summed_ready[b], done + i)
                        for u in range(LANES):
                            last = nc.tensor.matmul(sums[b][:, u * F:(u + 1) * F], same[b][:, u, :], got[b][:, u, :],
                                                    start=True, stop=True)
                        last.then_inc(sums_ready[b], 1)


def transform(net, layer, sems, stats):
    nc = net.nc
    S = 2
    with ExitStack() as ctx:
        def sb(name, shape, dt=F32):
            return ctx.enter_context(nc.sbuf_tensor(f"t{layer}_{name}", shape, dt))

        rows = [sb(f"rows{k}", [P, G, F]) for k in range(S)]
        scaled = [sb(f"scaled{k}", [P, G, F]) for k in range(S)]
        turned = [sb(f"turned{k}", [P, G * F]) for k in range(S)]
        zt = [sb(f"zt{k}", [P, G * F]) for k in range(S)]
        t_ps = [ctx.enter_context(nc.psum_tensor(f"t{layer}_t_ps{k}", [P, G * F], F32)) for k in range(S)]
        m_ps = [ctx.enter_context(nc.psum_tensor(f"t{layer}_m_ps{k}", [P, G * F], F32)) for k in range(S)]
        loaded, scaled_ready, t_ready, turned_ready, m_ready, z_ready, counted, z_stored = (sems[n] for n in
            ("loaded", "scaled_ready", "t_ready", "turned_ready", "m_ready", "z_ready", "counted", "z_stored"))
        v = node_chunks(net.v)
        done = [layer * (NC // S + 1), layer * (NC // S)]

        def rounds(engine, body):
            with engine.Fori(0, NC // S) as i:
                for k in range(S):
                    body(i + done[k], k, i * S + k, False)
            body(NC // S + done[0], 0, NC - 1, True)

        with nc.Block() as block:
            @block.sync
            def _(sp):
                def body(r, k, c, last):
                    sp.wait_ge(scaled_ready[k], r)
                    sp.dma_start(rows[k][:, :, :].rearrange("p g f -> p (g f)"), chunk_of(v, c)).then_inc(loaded[k], 16)
                rounds(sp, body)

            @block.gpsimd
            def _(pool):
                def body(r, k, c, last):
                    pool.wait_ge(z_ready[k], 2 * r + 2)
                    pool.dma_start(chunk_of(net.z, c), zt[k][:, :]).then_inc(z_stored[k], 16)
                rounds(pool, body)
                for k in range(S):
                    pool.wait_ge(z_stored[k], 16 * (done[k] + NC // S + (k == 0)))

            @block.vector
            def _(dve):
                def body(r, k, c, last):
                    dve.wait_ge(loaded[k], 16 * r + 16)
                    dve.wait_ge(t_ready[k], 2 * r)
                    nc.vector.tensor_tensor(scaled[k][:, :, :], rows[k][:, :, :],
                                            net.dinv[:, bass.ds(c * G, G)].rearrange("p (g o) -> p g o", o=1).broadcast_to([P, G, F]),
                                            ALU.mult).then_inc(scaled_ready[k], 1)
                    for h in range(2):
                        dve.wait_ge(z_ready[k], 2 * r + (h + 1))
                        unit = zt[k][:, h * 512:(h + 1) * 512]
                        if last:
                            unit = unit.rearrange("q (j p) -> q j p", p=P)[:, :, 0:TAIL_P]
                        nc.vector.bn_stats(stats[:, bass.ds(2 * c + h, 1), :].rearrange("p a s -> p (a s)"), unit).then_inc(counted[k], 1)
                rounds(dve, body)

            @block.tensor
            def _(pe):
                def body(r, k, c, last):
                    pe.wait_ge(scaled_ready[k], r + 1)
                    for h in range(2):
                        pe.wait_ge(turned_ready[k], 2 * r + h if h == 0 else 2 * r)
                        for j in range(4 * h, 4 * h + 4):
                            t = nc.tensor.transpose(t_ps[k][:, j * P:(j + 1) * P],
                                                    scaled[k][:, 2 * j:2 * j + 2, :].rearrange("p g f -> p (g f)"), net.ident[:, :])
                        t.then_inc(t_ready[k], 1)
                    for h in range(2):
                        pe.wait_ge(turned_ready[k], 2 * r + (h + 1))
                        pe.wait_ge(z_ready[k], 2 * r)
                        nc.tensor.matmul(m_ps[k][:, h * 512:(h + 1) * 512], net.gcn_w[layer][:, :],
                                         turned[k][:, h * 512:(h + 1) * 512], start=True, stop=True).then_inc(m_ready[k], 1)
                rounds(pe, body)

            @block.scalar
            def _(act):
                def body(r, k, c, last):
                    for h in range(2):
                        part = slice(h * 512, (h + 1) * 512)
                        act.wait_ge(t_ready[k], 2 * r + (h + 1))
                        act.wait_ge(m_ready[k], 2 * r)
                        nc.scalar.activation(turned[k][:, part], t_ps[k][:, part], ACT.Copy).then_inc(turned_ready[k], 1)
                    for h in range(2):
                        part = slice(h * 512, (h + 1) * 512)
                        act.wait_ge(m_ready[k], 2 * r + (h + 1))
                        act.wait_ge(counted[k], 2 * r)
                        act.wait_ge(z_stored[k], 16 * r)
                        nc.scalar.activation(zt[k][:, part], m_ps[k][:, part], ACT.Relu,
                                             bias=net.gcn_b[:, layer:layer + 1]).then_inc(z_ready[k], 1)
                rounds(act, body)


def batch_norm_factors(net, layer, sems, stats, factor, offset):
    nc = net.nc
    with ExitStack() as ctx:
        def sb(name, shape, dt=F32):
            return ctx.enter_context(nc.sbuf_tensor(f"f{layer}_{name}", shape, dt))

        mv, moments, mean, var, square, root = sb("mv", [P, 2]), sb("moments", [P, 2]), sb("mean", [P, 1]), sb("var", [P, 1]), sb("square", [P, 1]), sb("root", [P, 1])
        mixed = ctx.enter_context(nc.psum_tensor(f"f{layer}_mixed", [P, 512], F32))
        moments_ready, mixed_ready, var_ready, root_ready, dve_step = (sems[n][0] for n in
            ("moments_ready", "mixed_ready", "var_ready", "root_ready", "factor_step"))
        with nc.Block() as block:
            @block.vector
            def _(dve):
                step = Chain(dve, dve_step, layer * 8)
                step(nc.vector.bn_aggr(mv[:, :], stats[:, :, :].rearrange("p c s -> p (c s)")))
                step(nc.vector.tensor_copy(moments[:, 0:1], mv[:, 0:1]))
                nc.vector.scalar_tensor_tensor(out=moments[:, 1:2], in0=mv[:, 0:1], scalar=mv[:, 0:1], in1=mv[:, 1:2],
                                               op0=ALU.mult, op1=ALU.add).then_inc(moments_ready, 1)
                dve.wait_ge(mixed_ready, layer + 1)
                step(nc.vector.tensor_copy(mean[:, :], mixed[:, 0:1]))
                step(nc.vector.tensor_tensor(square[:, :], mean[:, :], mean[:, :], ALU.mult))
                nc.vector.tensor_tensor(var[:, :], mixed[:, 1:2], square[:, :], ALU.subtract).then_inc(var_ready, 1)
                dve.wait_ge(root_ready, layer + 1)
                step(nc.vector.reciprocal(root[:, :], root[:, :]))
                step(nc.vector.tensor_tensor(factor[:, :], root[:, :], net.gamma[:, layer:layer + 1], ALU.mult))
                step(nc.vector.tensor_tensor(offset[:, :], mean[:, :], factor[:, :], ALU.mult))
                step(nc.vector.tensor_tensor(offset[:, :], net.beta[:, layer:layer + 1], offset[:, :], ALU.subtract))
                assert step.n == 8

            @block.tensor
            def _(pe):
                pe.wait_ge(moments_ready, layer + 1)
                nc.tensor.matmul(mixed[:, 0:2], net.pair_mean[:, :], moments[:, :], start=True, stop=True).then_inc(mixed_ready, 1)

            @block.scalar
            def _(act):
                act.wait_ge(var_ready, layer + 1)
                nc.scalar.activation(root[:, :], var[:, :], ACT.Sqrt, bias=net.eps[:, :]).then_inc(root_ready, 1)


def normalise(net, layer, sems, factor, offset, out):
    nc = net.nc
    S = 2
    final = layer == 2
    with ExitStack() as ctx:
        def sb(name, shape, dt=F32):
            return ctx.enter_context(nc.sbuf_tensor(f"b{layer}_{name}", shape, dt))

        zt = [sb(f"zt{k}", [P, G * F]) for k in range(S)]
        normed = [sb(f"normed{k}", [P, G * F]) for k in range(S)]
        rows = [sb(f"rows{k}", [P, G, F]) for k in range(S)]
        res = [sb(f"res{k}", [P, G, F]) for k in range(S)]
        ps = [ctx.enter_context(nc.psum_tensor(f"b{layer}_ps{k}", [P, G * F], F32)) for k in range(S)]
        loaded, normed_ready, t_ready, rows_ready, stored = (sems[n] for n in
            ("b_loaded", "normed_ready", "b_t_ready", "rows_ready", "stored"))
        res_in = sems["res_in"]
        done = [layer * (NC // S + 1), layer * (NC // S)]
        y, v = node_chunks(net.y), node_chunks(net.v)
        x1 = node_chunks(net.x1)
        out_chunks = node_chunks(out, (NC - 1) * CHUNK)

        def rounds(engine, body):
            with engine.Fori(0, NC // S) as i:
                for k in range(S):
                    body(i + done[k], k, i * S + k, False)
            body(NC // S + done[0], 0, NC - 1, True)

        with nc.Block() as block:
            @block.sync
            def _(sp):
                def body(r, k, c, last):
                    sp.wait_ge(normed_ready[k], r)
                    sp.dma_start(zt[k][:, :], chunk_of(net.z, c)).then_inc(loaded[k], 16)
                    if final:
                        sp.wait_ge(rows_ready[k], r)
                        sp.dma_start(res[k][:, :, :].rearrange("p g f -> p (g f)"), chunk_of(x1, c)).then_inc(res_in[k], 16)
                rounds(sp, body)

            @block.scalar
            def _(act):
                def body(r, k, c, last):
                    act.wait_ge(loaded[k], 16 * r + 16)
                    act.wait_ge(t_ready[k], r)
                    nc.scalar.activation(normed[k][:, :], zt[k][:, :], ACT.Identity, bias=offset[:, :], scale=factor[:, :]
                                         ).then_inc(normed_ready[k], 1)
                rounds(act, body)

            @block.tensor
            def _(pe):
                def body(r, k, c, last):
                    pe.wait_ge(normed_ready[k], r + 1)
                    pe.wait_ge(rows_ready[k], r)
                    for j in range(G // 2):
                        t = nc.tensor.transpose(ps[k][:, j * P:(j + 1) * P], normed[k][:, j * P:(j + 1) * P], net.ident[:, :])
                    t.then_inc(t_ready[k], 1)
                rounds(pe, body)

            @block.vector
            def _(dve):
                def body(r, k, c, last):
                    dve.wait_ge(t_ready[k], r + 1)
                    dve.wait_ge(stored[k], 32 * r)
                    got = ps[k][:, :].rearrange("p (g f) -> p g f", g=G)
                    if final:
                        dve.wait_ge(res_in[k], 16 * (r - done[k]) + 16)
                        nc.vector.tensor_tensor(rows[k][:, :, :], got, res[k][:, :, :], ALU.add).then_inc(rows_ready[k], 1)
                    else:
                        nc.vector.tensor_tensor(rows[k][:, :, :], got,
                                                net.dinv[:, bass.ds(c * G, G)].rearrange("p (g o) -> p g o", o=1).broadcast_to([P, G, F]),
                                                ALU.mult).then_inc(rows_ready[k], 1)
                rounds(dve, body)

            @block.gpsimd
            def _(pool):
                def body(r, k, c, last):
                    pool.wait_ge(rows_ready[k], r + 1)
                    flat = rows[k][:, :, :].rearrange("p g f -> p (g f)")
                    if not final:
                        pool.dma_start(chunk_of(y, c), flat).then_inc(stored[k], 16)
                        pool.dma_start(chunk_of(v, c), flat).then_inc(stored[k], 16)
                    elif not last:
                        for q in range(2):
                            pool.dma_start(out_chunks[bass.ds(c, 1), q * F:(q + 1) * F, :].rearrange("a p n -> (a p) n"),
                                           flat[q * F:(q + 1) * F, :]).then_inc(stored[k], 16)
                    else:
                        tail = out[(NC - 1) * CHUNK:N, :].rearrange("(p g) f -> p (g f)", g=G)
                        cut = TAIL_P // 16 * 16
                        pool.dma_start(tail[0:cut, :], flat[0:cut, :]).then_inc(stored[k], 16)
                        pool.dma_start(tail[cut:TAIL_P, :], flat[cut:TAIL_P, :]).then_inc(stored[k], 16)
                rounds(pool, body)
                for k in range(S):
                    pool.wait_ge(stored[k], 32 * (done[k] + NC // S + (k == 0)))


def build_network(nc, args, out, upto=99):
    with ExitStack() as ctx:
        net = Net(nc, ctx, args)

        def sems(names, n):
            return {name: [ctx.enter_context(nc.semaphore(f"{name}{k}")) for k in range(n)] for name in names}

        load_tables(net)
        count_nodes(net)
        for stage in range(2):
            nodes_to_hyperedges(net, stage)
            hyperedges_to_nodes(net, stage)
        norm_nodes(net)
        stats = ctx.enter_context(nc.sbuf_tensor("stats", [P, 2 * NC, 6], F32))
        factor = ctx.enter_context(nc.sbuf_tensor("factor", [P, 1], F32))
        offset = ctx.enter_context(nc.sbuf_tensor("offset", [P, 1], F32))
        edge_sems = sems(("idx_ready", "same_in", "gathered", "sums_ready", "summed_ready", "added"), 2)
        node_sems = sems(("loaded", "scaled_ready", "t_ready", "turned_ready", "m_ready", "z_ready", "counted", "z_stored"), 2)
        norm_sems = sems(("b_loaded", "normed_ready", "b_t_ready", "rows_ready", "stored", "res_in"), 2)
        factor_sems = sems(("moments_ready", "mixed_ready", "var_ready", "root_ready", "factor_step"), 1)
        for layer in range(3):
            add_edges(net, layer, edge_sems)
            transform(net, layer, node_sems, stats)
            batch_norm_factors(net, layer, factor_sems, stats, factor, offset)
            normalise(net, layer, norm_sems, factor, offset, out)


_INS = ["x", "src", "dst", "L0_gnn_W1", "L0_gnn_b1", "L0_gnn_W2", "L0_gnn_b2"] + [
    f"L1_gnn_{n}{i}" for i in (1, 2, 3) for n in ("W", "b", "gamma", "beta")]


def kernel(**inputs):
    import numpy as np
    import concourse.bacc as bacc
    from concourse.bass_utils import run_bass_kernel_spmd

    nc = bacc.Bacc("TRN2", target_bir_lowering=False, num_devices=1)
    arrays, args = {}, {}
    for name in _INS:
        a = np.ascontiguousarray(inputs[name])
        arrays[f"in_{name}"] = a
        args[name] = nc.dram_tensor(f"in_{name}", a.shape, mybir.dt.from_np(a.dtype), kind="ExternalInput").ap()
    out = nc.dram_tensor("out", (N, F), F32, kind="ExternalOutput").ap()
    build_network(nc, args, out)
    return run_bass_kernel_spmd(nc, [arrays], core_ids=[0]).results[0]["out"]
```

```python
import concourse.bass as bass
from concourse import mybir
from contextlib import ExitStack

F32 = mybir.dt.float32
F16 = mybir.dt.float16
I32 = mybir.dt.int32
ACT = mybir.ActivationFunctionType
ALU = mybir.AluOpType
AX = mybir.AxisListType

P = 128
N, E, F = 100000, 25000, 64
HYPER = 3125
EPS = 1e-5

G = 16
CHUNK = P * G
NC = -(-N // CHUNK)
NP = NC * CHUNK
SLOTS = 4
KEPT = 36
SPILLED = (-(-(NC - KEPT) // 2), (NC - KEPT) // 2)
TAIL_P = (N - (NC - 1) * CHUNK) // G
COLS = NC * G
DUMMY = NP

TILES = -(-E // P)
LANES = 7
STEPS = TILES // LANES
EP = TILES * P
PAD_NODE = NP - 1
ROWS2 = TILES - P
HDUMMY = HYPER
HROWS = 26 * P
HW = F + 1


def node_chunks(table, rows=NP):
    return table[0:rows, :].rearrange("(c p g) f -> c p (g f)", p=P, g=G)


def chunk_of(view, c):
    return view[bass.ds(c, 1), :, :].rearrange("a p n -> (a p) n")


class Net:

    def __init__(self, nc, ctx, args):
        self.nc, self.args = nc, args

        def sb(name, shape, dt=F32):
            return ctx.enter_context(nc.sbuf_tensor(name, shape, dt))

        def dram(name, shape, dt=F32):
            return nc.dram_tensor(name, shape, dt, kind="Internal").ap()

        self.passed = ctx.enter_context(nc.semaphore("passed"))
        self.x1 = dram("x1_rows", (NP + P, F))
        self.conv = dram("conv_rows", (NP + P, F))
        self.y = dram("y_rows", (NP, F))
        self.v = dram("v_rows", (NP + LANES * P, F))
        self.z = dram("z_units", (NC, P, G // 2 * P))
        self.node_scalars = dram("node_scalars", (NP, 2))
        self.hyper1 = dram("hyper1_rows", (HROWS, HW))
        self.hyper2 = dram("hyper2_rows", (HROWS, HW))
        self.src_padded = dram("src_padded", (TILES, P), I32)
        self.dst_padded = dram("dst_padded", (TILES, P), I32)
        self.same_dst = dram("same_dst", (STEPS, P, LANES * P))
        self.src_f = sb("src_f", [P, TILES])
        self.dst_f = sb("dst_f", [P, TILES])
        self.light = sb("light", [P, TILES])
        self.src_idx = sb("src_idx", [P, TILES], I32)
        self.clip_idx = sb("clip_idx", [P, TILES], I32)
        self.light_idx = sb("light_idx", [P, TILES], I32)
        self.dst_idx = sb("dst_idx", [P, TILES], I32)
        self.bounds = sb("bounds", [1, 2], I32)
        self.dinv = sb("dinv", [P, COLS])
        self.far_share = sb("far_share", [P, COLS])
        self.ident = sb("ident", [P, P])
        self.before = sb("before", [P, P])
        self.pair_mean = sb("pair_mean", [P, P])
        self.part = sb("part", [P, 1])
        self.eps = sb("eps", [P, 1])
        self.conv_w = [sb(f"conv_w{i}", [F, F]) for i in range(2)]
        self.conv_b = [sb(f"conv_b{i}", [P, F]) for i in range(2)]
        self.gcn_w = [sb(f"gcn_w{i}", [P, P]) for i in range(3)]
        self.gcn_b = sb("gcn_b", [P, 3])
        self.gamma = sb("gamma", [P, 3])
        self.beta = sb("beta", [P, 3])
        self.e1_last = sb("e1_last", [P, F])
        self.e2_last = sb("e2_last", [P, F])


def wait_alone(engine, sem, value, net):
    engine.wait_ge(sem, value)
    engine.sem_inc(net.passed, 1)


class Chain:

    def __init__(self, engine, sem, base=0):
        self.engine, self.sem, self.base, self.n = engine, sem, base, 0

    def __call__(self, instruction):
        self.n += 1
        instruction.then_inc(self.sem, 1)
        self.engine.wait_ge(self.sem, self.base + self.n)


def load_tables(net):
    nc, a = net.nc, net.args
    with ExitStack() as ctx:
        def sb(name, shape, dt=F32):
            return ctx.enter_context(nc.sbuf_tensor(f"load_{name}", shape, dt))

        def sem(name):
            return ctx.enter_context(nc.semaphore(f"load_{name}"))

        names = ["src", "dst", "next"]
        rows = {n: sb(f"{n}_rows", [P, 2, P], I32) for n in names}
        rows_f = {n: sb(f"{n}_rows_f", [P, 2, P]) for n in names}
        zero = sb("zero", [P, 2512])
        worse = sb("worse", [P, 2])
        last_tile = sb("last_tile", [P, 2])
        step_no = sb("step_no", [P, TILES])
        light_no = sb("light_no", [P, TILES])
        flags = sb("flags", [1, 2])
        cols = {n: ctx.enter_context(nc.psum_tensor(f"{n}_cols", [P, 512], F32)) for n in ("src", "dst")}
        flag_rows = ctx.enter_context(nc.psum_tensor("flag_rows", [P, 512], F32))
        padded, edges_in, rows_ready, cols_ready = sem("padded"), sem("edges_in"), sem("rows_ready"), sem("cols_ready")
        consts_ready, zero_ready = sem("consts_ready"), sem("zero_ready")
        weights_in, copied, zeroed, padded_out = sem("weights_in"), sem("copied"), sem("zeroed"), sem("padded_out")
        flags_ready, flags_out, dve_step, pool_step = sem("flags_ready"), sem("flags_out"), sem("dve_step"), sem("pool_step")
        with nc.Block() as block:
            @block.sync
            def _(sp):
                sp.wait_ge(padded, 3)
                full = E // P - P
                rest = E - (P + full) * P
                count = 0
                for name, flat, off in (("src", a["src"], 0), ("dst", a["dst"], 0), ("next", a["dst"], 1)):
                    left = rest - off
                    sp.dma_start(rows[name][:, 0, :], flat[off:off + P * P].rearrange("(t p) -> t p", p=P)).then_inc(edges_in, 16)
                    sp.dma_start(rows[name][0:full, 1, :],
                                 flat[off + P * P:off + (P + full) * P].rearrange("(t p) -> t p", p=P)).then_inc(edges_in, 16)
                    sp.dma_start(rows[name][full:full + 1, 1, 0:left],
                                 flat[off + (P + full) * P:E].rearrange("(a p) -> a p", a=1)).then_inc(edges_in, 16)
                    count += 48
                sp.wait_ge(edges_in, count)
                for name, table in (("src", net.src_padded), ("dst", net.dst_padded)):
                    sp.dma_start(table[0:P, :], rows[name][:, 0, :]).then_inc(padded_out, 16)
                    sp.dma_start(table[P:TILES, :], rows[name][0:ROWS2, 1, :]).then_inc(padded_out, 16)
                sp.dma_start(net.x1[0:N, :].rearrange("(a b) f -> a (b f)", b=50),
                             a["x"].rearrange("(a b) f -> a (b f)", b=50)).then_inc(copied, 16)
                sp.wait_ge(padded_out, 64)
                sp.wait_ge(copied, 16)

            @block.scalar
            def _(act):
                act.wait_ge(zero_ready, 4)
                small = [(net.conv_w[0][:, :], a["L0_gnn_W1"]), (net.conv_w[1][:, :], a["L0_gnn_W2"])]
                for i, name in enumerate(("L0_gnn_b1", "L0_gnn_b2")):
                    small.append((net.conv_b[i][:, :], a[name].rearrange("(o f) -> o f", o=1).broadcast_to([P, F])))
                for i in range(3):
                    for h in range(2):
                        part = slice(h * F, (h + 1) * F)
                        small.append((net.gcn_w[i][part, part], a[f"L1_gnn_W{i + 1}"]))
                        for table, name in ((net.gcn_b, "b"), (net.gamma, "gamma"), (net.beta, "beta")):
                            small.append((table[part, i:i + 1], a[f"L1_gnn_{name}{i + 1}"].rearrange("(f o) -> f o", o=1)))
                for dst, src in small:
                    act.dma_start(dst, src).then_inc(weights_in, 16)
                act.dma_start(net.hyper1.rearrange("(p r) f -> p (r f)", p=P), zero[:, 0:HROWS // P * HW]).then_inc(zeroed, 16)
                act.dma_start(net.hyper2.rearrange("(p r) f -> p (r f)", p=P), zero[:, 0:HROWS // P * HW]).then_inc(zeroed, 16)
                act.dma_start(net.v[NP:NP + LANES * P, :].rearrange("(p r) f -> p (r f)", p=P), zero[:, 0:LANES * F]).then_inc(zeroed, 16)
                pads = (NP + P - N) * F // P
                act.dma_start(net.x1[N:NP + P, :].rearrange("(p r) f -> p (r f)", p=30),
                              zero[0:30, 0:(NP + P - N) * F // 30]).then_inc(zeroed, 16)
                width = (NP + P) * F // P
                conv = net.conv.rearrange("(p r) f -> p (r f)", p=P)
                for q in range(width // 2512):
                    act.dma_start(conv[:, q * 2512:(q + 1) * 2512], zero[:, :]).then_inc(zeroed, 16)
                act.wait_ge(weights_in, 16 * len(small))
                act.wait_ge(zeroed, 16 * (4 + width // 2512))

            @block.gpsimd
            def _(pool):
                for name in names:
                    nc.gpsimd.memset(rows[name][:, :, :], PAD_NODE).then_inc(padded, 1)
                for w in net.gcn_w:
                    nc.gpsimd.memset(w[:, :], 0.0).then_inc(zero_ready, 1)
                nc.gpsimd.memset(zero[:, :], 0.0).then_inc(zero_ready, 1)
                nc.gpsimd.memset(net.eps[:, :], EPS).then_inc(consts_ready, 1)
                step = Chain(pool, pool_step)
                step(nc.gpsimd.memset(net.ident[:, :], 0.0))
                nc.gpsimd.affine_select(out=net.ident[:, :], in_=net.ident[:, :], compare_op=ALU.not_equal, fill=1.0,
                                        base=0, pattern=[[-1, P]], channel_multiplier=1).then_inc(consts_ready, 1)
                step(nc.gpsimd.memset(net.before[:, :], 1.0))
                nc.gpsimd.affine_select(out=net.before[:, :], in_=net.before[:, :], compare_op=ALU.is_gt, fill=0.0,
                                        base=0, pattern=[[-1, P]], channel_multiplier=1).then_inc(consts_ready, 1)
                step(nc.gpsimd.memset(net.pair_mean[:, :], 0.0))
                for off in (-F, 0, F):
                    step(nc.gpsimd.affine_select(out=net.pair_mean[:, :], in_=net.pair_mean[:, :],
                                                 compare_op=ALU.not_equal, fill=0.5, base=off,
                                                 pattern=[[-1, P]], channel_multiplier=1))
                nc.gpsimd.iota(net.part[:, :], pattern=[[0, 1]], base=0, channel_multiplier=1,
                               allow_small_or_imprecise_dtypes=True).then_inc(consts_ready, 1)
                nc.gpsimd.iota(step_no[:, :], pattern=[[1, STEPS], [0, LANES]], base=1, channel_multiplier=0,
                               allow_small_or_imprecise_dtypes=True).then_inc(consts_ready, 1)

            @block.vector
            def _(dve):
                step = Chain(dve, dve_step)
                dve.wait_ge(edges_in, 144)
                for name in names:
                    nc.vector.tensor_copy(rows_f[name][:, :, :], rows[name][:, :, :]).then_inc(rows_ready, 1)
                dve.wait_ge(consts_ready, 5)
                dve.wait_ge(rows_ready, 3)
                step(nc.vector.tensor_tensor(rows_f["next"][:, :, :], rows_f["dst"][:, :, :], rows_f["next"][:, :, :], ALU.is_gt))
                step(nc.vector.tensor_reduce(worse[:, :], rows_f["next"][:, :, :], AX.X, ALU.max))
                step(nc.vector.tensor_reduce(last_tile[:, 1:2], worse[:, :], AX.X, ALU.max))
                dve.wait_ge(cols_ready, 4)
                for name, table in (("src", net.src_f), ("dst", net.dst_f)):
                    step(nc.vector.tensor_copy(table[:, :], cols[name][:, 0:TILES]))
                step(nc.vector.tensor_copy(net.src_idx[:, :], net.src_f[:, :]))
                step(nc.vector.tensor_scalar(net.light[:, :], net.dst_f[:, :], float(HYPER), None, ALU.is_lt))
                step(nc.vector.tensor_scalar(net.clip_idx[:, :], net.dst_f[:, :], float(HYPER - 1), None, ALU.min))
                step(nc.vector.tensor_tensor(light_no[:, :], net.light[:, :], step_no[:, :], ALU.mult))
                step(nc.vector.tensor_reduce(last_tile[:, 0:1], light_no[:, :], AX.X, ALU.max))
                nc.vector.tensor_scalar(last_tile[:, 0:1], last_tile[:, 0:1], 1.0, None, ALU.max).then_inc(flags_ready, 1)
                dve.wait_ge(flags_out, 2)
                for k in range(2):
                    step(nc.vector.tensor_reduce(flags[:, k:k + 1], flag_rows[0:1, k * P:(k + 1) * P], AX.X, ALU.max))
                step(nc.vector.tensor_copy(net.bounds[:, :], flags[:, :]))

            @block.tensor
            def _(pe):
                pe.wait_ge(consts_ready, 5)
                pe.wait_ge(rows_ready, 3)
                for name in ("src", "dst"):
                    nc.tensor.transpose(cols[name][:, 0:P], rows_f[name][:, 0, :], net.ident[:, :]).then_inc(cols_ready, 1)
                    nc.tensor.transpose(cols[name][:, P:TILES], rows_f[name][0:ROWS2, 1, :],
                                        net.ident[0:ROWS2, 0:ROWS2]).then_inc(cols_ready, 1)
                pe.wait_ge(flags_ready, 1)
                for k in range(2):
                    nc.tensor.transpose(flag_rows[0:1, k * P:(k + 1) * P], last_tile[:, k:k + 1], net.ident[:, :]).then_inc(flags_out, 1)


def count_nodes(net):
    nc = net.nc
    half = COLS // 2
    with ExitStack() as ctx:
        def sb(name, shape, dt=F32):
            return ctx.enter_context(nc.sbuf_tensor(f"count_{name}", shape, dt))

        def sem(name):
            return ctx.enter_context(nc.semaphore(f"count_{name}"))

        iota_col = sb("iota_col", [P, COLS], F16)
        iota_part = sb("iota_part", [P, P], F16)
        ints = [sb(f"ints{i}", [P, TILES], I32) for i in range(3)]
        col_f = {n: sb(f"{n}_col", [P, TILES]) for n in ("src", "dst")}
        part_f = {n: sb(f"{n}_part", [P, TILES]) for n in ("src", "dst")}
        hot_col = {n: [sb(f"{n}_hot_col{i}", [P, COLS], F16) for i in range(2)] for n in ("src", "dst")}
        hot_part = {n: [sb(f"{n}_hot_part{i}", [P, P], F16) for i in range(2)] for n in ("src", "dst")}
        nothing = sb("nothing", [P, 512], F16)
        dst_row = [sb(f"dst_row{i}", [P, LANES, P], I32) for i in range(2)]
        same = [sb(f"same{i}", [P, LANES, P]) for i in range(2)]
        earlier = sb("earlier", [P, LANES, P])
        n_earlier = sb("n_earlier", [P, TILES])
        first = sb("first", [P, TILES])
        row = sb("row", [P, TILES])
        dummy = sb("dummy", [P, 1])
        lane_dummy = sb("lane_dummy", [P, TILES])
        members = sb("members", [P, COLS])
        pairs = sb("pairs", [P, COLS, 2])
        names = ("dst", "src", "light")
        counts = {n: [ctx.enter_context(nc.psum_tensor(f"{n}_count{h}", [P, 512], F32)) for h in range(2)] for n in names}
        iotas_ready, hots_ready, hots_used = sem("iotas_ready"), [sem("hots_ready0"), sem("hots_ready1")], [sem("hots_used0"), sem("hots_used1")]
        light_hot, light_used, counted = sem("light_hot"), sem("light_used"), sem("counted")
        rows_in = [sem("rows_in0"), sem("rows_in1")]
        rows_used = [sem("rows_used0"), sem("rows_used1")]
        same_out = [sem("same_out0"), sem("same_out1")]
        dve_step, earlier_step, degree_ready, root_ready = sem("dve_step"), sem("earlier_step"), sem("degree_ready"), sem("root_ready")
        scalars_ready, scalars_out = sem("scalars_ready"), sem("scalars_out")
        dst_rows = net.dst_padded.rearrange("(u i) k -> i u k", u=LANES)

        with nc.Block() as block:
            @block.gpsimd
            def _(pool):
                nc.gpsimd.iota(iota_col[:, :], pattern=[[1, COLS]], base=0, channel_multiplier=0,
                               allow_small_or_imprecise_dtypes=True).then_inc(iotas_ready, 1)
                nc.gpsimd.iota(iota_part[:, :], pattern=[[1, P]], base=0, channel_multiplier=0,
                               allow_small_or_imprecise_dtypes=True).then_inc(iotas_ready, 1)
                nc.gpsimd.memset(nothing[:, :], 0.0).then_inc(iotas_ready, 1)
                nc.gpsimd.iota(lane_dummy[:, :], pattern=[[P, LANES], [0, STEPS]], base=DUMMY, channel_multiplier=1,
                               allow_small_or_imprecise_dtypes=True).then_inc(iotas_ready, 1)

            @block.sync
            def _(sp):
                with sp.Fori(0, STEPS // 2) as i:
                    for k in range(2):
                        sp.wait_ge(rows_used[k], i)
                        sp.dma_start(dst_row[k][:, :, :],
                                     dst_rows[bass.ds(2 * i + k, 1), :, :].broadcast_to([P, LANES, P])).then_inc(rows_in[k], 16)

            @block.scalar
            def _(act):
                with act.Fori(0, STEPS // 2) as i:
                    for k in range(2):
                        act.wait_ge(rows_used[k], i + 1)
                        act.dma_start(chunk_of(net.same_dst, 2 * i + k),
                                      same[k][:, :, :].rearrange("p u k -> p (u k)")).then_inc(same_out[k], 16)
                for k in range(2):
                    act.wait_ge(same_out[k], 16 * (STEPS // 2))
                act.wait_ge(degree_ready, 1)
                nc.scalar.activation(net.dinv[:, :], net.dinv[:, :], ACT.Sqrt).then_inc(root_ready, 1)
                act.wait_ge(scalars_ready, 1)
                act.dma_start(net.node_scalars.rearrange("(c p g) w -> p c (g w)", p=P, g=G),
                              pairs[:, :, :].rearrange("p (c g) w -> p c (g w)", g=G)).then_inc(scalars_out, 16)
                act.wait_ge(scalars_out, 16)

            @block.vector
            def _(dve):
                step = Chain(dve, dve_step)
                for name, table in (("src", net.src_f), ("dst", net.dst_f)):
                    step(nc.vector.tensor_copy(ints[0][:, :], table[:, :]))
                    step(nc.vector.tensor_scalar(ints[1][:, :], ints[0][:, :], 11, 4, ALU.logical_shift_right, ALU.logical_shift_left))
                    step(nc.vector.tensor_scalar(ints[2][:, :], ints[0][:, :], G - 1, None, ALU.bitwise_and))
                    step(nc.vector.tensor_tensor(col_f[name][:, :], ints[1][:, :], ints[2][:, :], ALU.add))
                    step(nc.vector.tensor_scalar(ints[1][:, :], ints[0][:, :], 4, P - 1, ALU.logical_shift_right, ALU.bitwise_and))
                    step(nc.vector.tensor_copy(part_f[name][:, :], ints[1][:, :]))
                dve.wait_ge(iotas_ready, 4)
                with dve.Fori(0, TILES // 2) as i:
                    for k in range(2):
                        dve.wait_ge(hots_used[k], i)
                        for name in ("dst", "src"):
                            nc.vector.tensor_scalar(hot_col[name][k][:, :], iota_col[:, :],
                                                    col_f[name][:, bass.ds(2 * i + k, 1)], None, ALU.is_equal).then_inc(hots_ready[k], 1)
                            nc.vector.tensor_scalar(hot_part[name][k][:, :], iota_part[:, :],
                                                    part_f[name][:, bass.ds(2 * i + k, 1)], None, ALU.is_equal).then_inc(hots_ready[k], 1)
                for k in range(2):
                    dve.wait_ge(hots_used[k], TILES // 2)
                n_light = dve.value_load(net.bounds[0:1, 0:1], min_val=1, max_val=STEPS)
                with dve.Fori(0, n_light * LANES) as i:
                    dve.wait_ge(light_used, i)
                    nc.vector.tensor_scalar(hot_col["src"][0][:, :], iota_col[:, :],
                                            col_f["src"][:, bass.ds(i, 1)], None, ALU.is_equal).then_inc(light_hot, 1)
                    nc.vector.tensor_scalar(hot_part["src"][0][:, :], iota_part[:, :],
                                            part_f["src"][:, bass.ds(i, 1)], net.light[:, bass.ds(i, 1)],
                                            ALU.is_equal, ALU.mult).then_inc(light_hot, 1)
                dst_cols = net.dst_f[:, :].rearrange("p (u i) -> p i u", u=LANES)
                earlier_cols = n_earlier[:, :].rearrange("p (u i) -> p i u", u=LANES)
                with dve.Fori(0, STEPS // 2) as i:
                    for k in range(2):
                        dve.wait_ge(rows_in[k], 16 * i + 16)
                        dve.wait_ge(same_out[k], 16 * i)
                        col = dst_cols[:, bass.ds(2 * i + k, 1), :].rearrange("p a u -> p (a u)")
                        nc.vector.tensor_tensor(same[k][:, :, :], dst_row[k][:, :, :],
                                                col.rearrange("p (u o) -> p u o", o=1).broadcast_to([P, LANES, P]),
                                                ALU.is_equal).then_inc(rows_used[k], 1)
                        dve.wait_ge(rows_used[k], i + 1)
                        nc.vector.tensor_tensor(earlier[:, :, :], same[k][:, :, :],
                                                net.before[:, :].rearrange("p (o k) -> p o k", o=1).broadcast_to([P, LANES, P]),
                                                ALU.mult).then_inc(earlier_step, 1)
                        dve.wait_ge(earlier_step, 4 * i + (2 * k + 1))
                        nc.vector.tensor_reduce(earlier_cols[:, bass.ds(2 * i + k, 1), :].rearrange("p a u -> p (a u)"),
                                                earlier[:, :, :], AX.X, ALU.add).then_inc(earlier_step, 1)
                        dve.wait_ge(earlier_step, 4 * i + (2 * k + 2))
                step(nc.vector.tensor_scalar(first[:, :], n_earlier[:, :], 0.0, None, ALU.is_equal))
                step(nc.vector.tensor_tensor(row[:, :], net.dst_f[:, :], lane_dummy[:, :], ALU.subtract))
                step(nc.vector.tensor_tensor(row[:, :], row[:, :], first[:, :], ALU.mult))
                step(nc.vector.tensor_tensor(net.dst_idx[:, :], row[:, :], lane_dummy[:, :], ALU.add))
                step(nc.vector.tensor_scalar(dummy[:, :], net.part[:, :], float(HDUMMY), None, ALU.add))
                step(nc.vector.tensor_scalar(row[:, :], net.dst_f[:, :], dummy[:, :], None, ALU.subtract))
                step(nc.vector.tensor_tensor(row[:, :], row[:, :], first[:, :], ALU.mult))
                step(nc.vector.tensor_tensor(row[:, :], row[:, :], net.light[:, :], ALU.mult))
                step(nc.vector.tensor_scalar(net.light_idx[:, :], row[:, :], dummy[:, :], None, ALU.add))
                dve.wait_ge(counted, 1)
                far, inverse = pairs[:, :, 0], pairs[:, :, 1]
                for h in range(2):
                    part = slice(h * half, (h + 1) * half)
                    step(nc.vector.tensor_scalar(net.dinv[:, part], counts["dst"][h][:, 0:half], 1.0, None, ALU.add))
                    step(nc.vector.tensor_copy(members[:, part], counts["src"][h][:, 0:half]))
                    step(nc.vector.tensor_tensor(far[:, part], members[:, part], counts["light"][h][:, 0:half], ALU.subtract))
                dve.engine_nop().then_inc(degree_ready, 1)
                step(nc.vector.tensor_scalar(members[:, :], members[:, :], 1.0, None, ALU.max))
                step(nc.vector.reciprocal(inverse, members[:, :]))
                nc.vector.tensor_tensor(net.far_share[:, :], far, inverse, ALU.mult).then_inc(scalars_ready, 1)
                dve.wait_ge(root_ready, 1)
                step(nc.vector.reciprocal(net.dinv[:, :], net.dinv[:, :]))

            @block.tensor
            def _(pe):
                pe.wait_ge(iotas_ready, 4)
                for n in names:
                    for h in range(2):
                        last = nc.tensor.matmul(counts[n][h][:, :], nothing[:, 0:P], nothing[:, :], start=True, stop=False)
                with pe.Fori(0, TILES // 2) as i:
                    for k in range(2):
                        pe.wait_ge(hots_ready[k], 4 * i + 4)
                        for name in ("dst", "src"):
                            for h in range(2):
                                last = nc.tensor.matmul(counts[name][h][:, 0:half], hot_part[name][k][:, :],
                                                        hot_col[name][k][:, h * half:(h + 1) * half], start=False, stop=False)
                        last.then_inc(hots_used[k], 1)
                n_light = pe.value_load(net.bounds[0:1, 0:1], min_val=1, max_val=STEPS)
                with pe.Fori(0, n_light * LANES) as i:
                    pe.wait_ge(light_hot, 2 * i + 2)
                    for h in range(2):
                        last = nc.tensor.matmul(counts["light"][h][:, 0:half], hot_part["src"][0][:, :],
                                                hot_col["src"][0][:, h * half:(h + 1) * half], start=False, stop=False)
                    last.then_inc(light_used, 1)
                for n in names:
                    for h in range(2):
                        last = nc.tensor.matmul(counts[n][h][:, :], nothing[:, 0:P], nothing[:, :], start=False, stop=True)
                last.then_inc(counted, 1)


def nodes_to_hyperedges(net, stage, sems):
    nc = net.nc
    table = (net.hyper1, net.hyper2)[stage]
    source = net.args["x"] if stage == 0 else net.conv
    with ExitStack() as ctx:
        def sb(name, shape, dt=F32):
            return ctx.enter_context(nc.sbuf_tensor(f"h{stage}_{name}", shape, dt))

        src_i, to_i = sb("src_i", [P, LANES], I32), sb("to_i", [P, LANES], I32)
        got, work, scal = sb("got", [P, LANES, F]), sb("work", [P, LANES, F]), sb("scal", [P, LANES, 2])
        mean, scale = sb("mean", [P, LANES]), sb("scale", [P, LANES])
        msg, summed = sb("msg", [P, LANES, HW]), sb("summed", [P, LANES, HW])
        same = sb("same", [P, LANES, P])
        sums = ctx.enter_context(nc.psum_tensor(f"h{stage}_sums", [P, 512], F32))
        idx_ready, gathered, same_in, act_in, act_out, msg_ready, sums_ready, summed_ready, added = (sems[n][0] for n in
            ("h_idx_ready", "h_gathered", "h_same_in", "h_act_in", "h_act_out", "h_msg_ready", "h_sums_ready", "h_summed_ready", "h_added"))
        dve_step, scal_in = sems["h_dve_step"][stage], sems["h_scal_in"][0]
        n_steps = (6, 4)[stage]

        def light_rounds(engine):
            n = engine.value_load(net.bounds[0:1, 0:1], min_val=1, max_val=STEPS)
            return engine.Fori(0, n), n if stage else 0

        def tiles_of(table, i):
            return table[:, bass.ds(i * LANES, LANES)]

        def over_features(t, width=F):
            return t.rearrange("p (u o) -> p u o", o=1).broadcast_to([P, LANES, width])

        def over_tiles(t):
            return t.rearrange("p (o f) -> p o f", o=1).broadcast_to([P, LANES, F])

        with nc.Block() as block:
            @block.sync
            def _(sp):
                tiles = net.same_dst.rearrange("i p (u k) -> u p i k", u=LANES)
                per_lane = STEPS // LANES
                loop, first = light_rounds(sp)
                with loop as i:
                    r = i + first
                    sp.wait_ge(sums_ready, r)
                    sp.dma_start(same[:, :, :], tiles[bass.ds(i // per_lane, 1), :,
                                                      bass.ds(i % per_lane * LANES, LANES), :]
                                 .rearrange("a p i k -> (a p) i k")).then_inc(same_in, 16)

            @block.gpsimd
            def _(pool):
                loop, first = light_rounds(pool)
                with loop as i:
                    r = i + first
                    wait_alone(pool, idx_ready, 2 * r + 2, net)
                    for u in range(LANES):
                        at = bass.IndirectOffsetOnAxis(ap=src_i[:, u:u + 1], axis=0)
                        pool.indirect_dma_start(out=got[:, u, :], out_offset=None, in_=source[:, :], in_offset=at).then_inc(gathered, 16)
                        if stage == 1:
                            pool.indirect_dma_start(out=scal[:, u, :], out_offset=None, in_=net.node_scalars[:, :],
                                                    in_offset=at).then_inc(scal_in, 16)
                    wait_alone(pool, summed_ready, r + 1, net)
                    for u in range(LANES):
                        pool.indirect_dma_start(out=table[:, :], out_offset=bass.IndirectOffsetOnAxis(ap=to_i[:, u:u + 1], axis=0),
                                                in_=summed[:, u, :], in_offset=None, compute_op=ALU.add).then_inc(added, 16)
                        wait_alone(pool, added, 16 * LANES * r + 16 * (u + 1), net)

            @block.vector
            def _(dve):
                loop, first = light_rounds(dve)
                with loop as i:
                    r = i + first
                    step = Chain(dve, dve_step, i * n_steps)
                    wait_alone(dve, added, 16 * LANES * r, net)
                    nc.vector.tensor_copy(src_i[:, :], tiles_of(net.src_idx, i)).then_inc(idx_ready, 1)
                    nc.vector.tensor_copy(to_i[:, :], tiles_of(net.light_idx, i)).then_inc(idx_ready, 1)
                    light = tiles_of(net.light, i)
                    dve.wait_ge(gathered, 16 * LANES * r + 16 * LANES)
                    if stage == 0:
                        step(nc.vector.tensor_reduce(mean[:, :], got[:, :, :], AX.X, ALU.add))
                        step(nc.vector.tensor_scalar(mean[:, :], mean[:, :], 1.0 / F, None, ALU.mult))
                        step(nc.vector.tensor_tensor(got[:, :, :], got[:, :, :], over_features(mean[:, :]), ALU.subtract))
                        step(nc.vector.tensor_tensor(work[:, :, :], got[:, :, :], got[:, :, :], ALU.mult))
                        nc.vector.tensor_reduce(scale[:, :], work[:, :, :], AX.X, ALU.add).then_inc(act_in, 1)
                        dve.wait_ge(act_out, 2 * r + 1)
                        step(nc.vector.reciprocal(scale[:, :], scale[:, :]))
                        step(nc.vector.tensor_tensor(scale[:, :], scale[:, :], light, ALU.mult))
                        nc.vector.tensor_tensor(work[:, :, :], got[:, :, :], over_features(scale[:, :]), ALU.mult).then_inc(act_in, 1)
                    else:
                        dve.wait_ge(scal_in, 16 * LANES * i + 16 * LANES)
                        step(nc.vector.tensor_tensor(work[:, :, :], over_tiles(net.e1_last[:, :]), scal[:, :, 0:1].broadcast_to([P, LANES, F]), ALU.mult))
                        step(nc.vector.tensor_tensor(got[:, :, :], got[:, :, :], work[:, :, :], ALU.add))
                        step(nc.vector.tensor_tensor(got[:, :, :], got[:, :, :], scal[:, :, 1:2].broadcast_to([P, LANES, F]), ALU.mult))
                        step(nc.vector.tensor_tensor(got[:, :, :], got[:, :, :], over_tiles(net.conv_b[0][:, :]), ALU.add))
                        nc.vector.tensor_tensor(work[:, :, :], got[:, :, :], over_features(light), ALU.mult).then_inc(act_in, 2)
                    assert step.n == n_steps
                    nc.vector.tensor_copy(msg[:, :, F:HW], light.rearrange("p (u o) -> p u o", o=1)).then_inc(msg_ready, 1)
                    dve.wait_ge(sums_ready, r + 1)
                    nc.vector.tensor_copy(summed[:, :, :].rearrange("p u f -> p (u f)"), sums[:, 0:LANES * HW]).then_inc(summed_ready, 1)

            @block.scalar
            def _(act):
                loop, first = light_rounds(act)
                with loop as i:
                    r = i + first
                    if stage == 0:
                        act.wait_ge(act_in, 2 * r + 1)
                        nc.scalar.activation(scale[:, :], scale[:, :], ACT.Sqrt, bias=net.eps[:, :], scale=1.0 / F).then_inc(act_out, 1)
                    act.wait_ge(act_in, 2 * r + 2)
                    nc.scalar.activation(msg[:, :, 0:F], work[:, :, :], ACT.Relu).then_inc(act_out, 1 + (stage == 1))

            @block.tensor
            def _(pe):
                loop, first = light_rounds(pe)
                with loop as i:
                    r = i + first
                    pe.wait_ge(msg_ready, r + 1)
                    pe.wait_ge(act_out, 2 * r + 2)
                    pe.wait_ge(same_in, 16 * r + 16)
                    for u in range(LANES):
                        last = nc.tensor.matmul(sums[:, u * HW:(u + 1) * HW], same[:, u, :], msg[:, u, :], start=True, stop=True)
                    last.then_inc(sums_ready, 1)


def hyperedges_to_nodes(net, stage, sems):
    nc = net.nc
    table = (net.hyper1, net.hyper2)[stage]
    target = (net.conv, net.x1)[stage]
    last_row = (net.e1_last, net.e2_last)[stage]
    with ExitStack() as ctx:
        def sb(name, shape, dt=F32):
            return ctx.enter_context(nc.sbuf_tensor(f"n{stage}_{name}", shape, dt))

        from_i, src_i, to_i = (sb(n, [P, LANES], I32) for n in ("from_i", "src_i", "to_i"))
        src_row = sb("src_row", [P, LANES, P], I32)
        got, last_got, scal = sb("got", [P, LANES, HW]), sb("last_got", [P, HW]), sb("scal", [P, LANES, 2])
        inverse, mean, mean_t, summed = sb("inverse", [P, LANES]), sb("mean", [P, LANES, F]), sb("mean_t", [F, LANES * P]), sb("summed", [P, LANES * F])
        same, earlier = sb("same", [P, LANES, P]), sb("earlier", [P, LANES, P])
        n_earlier, row, dummy = sb("n_earlier", [P, LANES]), sb("row", [P, LANES]), sb("dummy", [P, 1])
        turned = ctx.enter_context(nc.psum_tensor(f"n{stage}_turned", [P, 1024], F32))
        product = ctx.enter_context(nc.psum_tensor(f"n{stage}_product", [P, 512], F32))
        last_in, idx_ready, to_ready, gathered, row_in, row_used = (sems[n][0] for n in
            ("n_last_in", "n_idx_ready", "n_to_ready", "n_gathered", "n_row_in", "n_row_used"))
        mean_ready, turned_ready, mean_t_ready, product_ready, summed_ready, added, scal_in = (sems[n][0] for n in
            ("n_mean_ready", "n_turned_ready", "n_mean_t_ready", "n_product_ready", "n_summed_ready", "n_added", "n_scal_in"))
        dve_step = sems["n_dve_step"][stage]
        before_loop = 4
        n_steps = (8, 9)[stage]

        def light_rounds(engine):
            n = engine.value_load(net.bounds[0:1, 0:1], min_val=1, max_val=STEPS)
            return engine.Fori(0, n), n if stage else 0

        def tiles_of(table, i):
            return table[:, bass.ds(i * LANES, LANES)]

        def over(t, width):
            return t.rearrange("p (u o) -> p u o", o=1).broadcast_to([P, LANES, width])

        with nc.Block() as block:
            @block.sync
            def _(sp):
                sp.dma_start(last_got[:, :], table[HYPER - 1:HYPER, :].broadcast_to([P, HW])).then_inc(last_in, 16)
                loop, first = light_rounds(sp)
                with loop as i:
                    r = i + first
                    sp.wait_ge(row_used, r)
                    sp.dma_start(src_row[:, :, :].rearrange("p u k -> p (u k)"),
                                 net.src_padded.rearrange("(s u) k -> s (u k)", u=LANES)[bass.ds(i, 1), :]
                                 .broadcast_to([P, LANES * P])).then_inc(row_in, 16)

            @block.gpsimd
            def _(pool):
                loop, first = light_rounds(pool)
                with loop as i:
                    r = i + first
                    wait_alone(pool, idx_ready, 2 * r + 2, net)
                    for u in range(LANES):
                        pool.indirect_dma_start(out=got[:, u, :], out_offset=None, in_=table[:, :],
                                                in_offset=bass.IndirectOffsetOnAxis(ap=from_i[:, u:u + 1], axis=0)).then_inc(gathered, 16)
                        if stage == 1:
                            pool.indirect_dma_start(out=scal[:, u, :], out_offset=None, in_=net.node_scalars[:, :],
                                                    in_offset=bass.IndirectOffsetOnAxis(ap=src_i[:, u:u + 1], axis=0)).then_inc(scal_in, 16)
                    pool.wait_ge(to_ready, r + 1)
                    wait_alone(pool, summed_ready, r + 1, net)
                    for u in range(LANES):
                        pool.indirect_dma_start(out=target[:, :], out_offset=bass.IndirectOffsetOnAxis(ap=to_i[:, u:u + 1], axis=0),
                                                in_=summed[:, u * F:(u + 1) * F], in_offset=None, compute_op=ALU.add).then_inc(added, 16)
                        wait_alone(pool, added, 16 * LANES * r + 16 * (u + 1), net)

            @block.vector
            def _(dve):
                step = Chain(dve, dve_step)
                step(nc.vector.tensor_scalar(dummy[:, :], net.part[:, :], float(DUMMY), None, ALU.add))
                dve.wait_ge(last_in, 16 * stage + 16)
                step(nc.vector.tensor_scalar(inverse[:, 0:1], last_got[:, F:HW], 1.0, None, ALU.max))
                step(nc.vector.reciprocal(inverse[:, 0:1], inverse[:, 0:1]))
                nc.vector.tensor_scalar(mean[:, 0, :], last_got[:, 0:F], inverse[:, 0:1], None, ALU.mult).then_inc(mean_ready, 1)
                loop, first = light_rounds(dve)
                dve.wait_ge(turned_ready, first + (stage + 1))
                nc.vector.tensor_copy(mean_t[:, 0:P], turned[0:F, 0:P]).then_inc(mean_t_ready, 1)
                dve.wait_ge(product_ready, first + (stage + 1))
                step(nc.vector.tensor_copy(last_row[:, :], product[:, 0:F]))
                assert step.n == before_loop
                with loop as i:
                    r = i + first
                    step = Chain(dve, dve_step, i * n_steps + before_loop)
                    wait_alone(dve, added, 16 * LANES * r, net)
                    nc.vector.tensor_copy(from_i[:, :], tiles_of(net.clip_idx, i)).then_inc(idx_ready, 1)
                    nc.vector.tensor_copy(src_i[:, :], tiles_of(net.src_idx, i)).then_inc(idx_ready, 1)
                    src = tiles_of(net.src_f, i)
                    dve.wait_ge(row_in, 16 * r + 16)
                    nc.vector.tensor_tensor(same[:, :, :], src_row[:, :, :], over(src, P), ALU.is_equal).then_inc(row_used, 1)
                    dve.wait_ge(row_used, r + 1)
                    step(nc.vector.tensor_tensor(earlier[:, :, :], same[:, :, :],
                                                 net.before[:, :].rearrange("p (o k) -> p o k", o=1).broadcast_to([P, LANES, P]), ALU.mult))
                    step(nc.vector.tensor_reduce(n_earlier[:, :], earlier[:, :, :], AX.X, ALU.add))
                    step(nc.vector.tensor_scalar(n_earlier[:, :], n_earlier[:, :], 0.0, None, ALU.is_equal))
                    step(nc.vector.tensor_scalar(row[:, :], src, dummy[:, :], None, ALU.subtract))
                    step(nc.vector.tensor_tensor(row[:, :], row[:, :], n_earlier[:, :], ALU.mult))
                    nc.vector.tensor_scalar(to_i[:, :], row[:, :], dummy[:, :], None, ALU.add).then_inc(to_ready, 1)
                    dve.wait_ge(gathered, 16 * LANES * r + 16 * LANES)
                    step(nc.vector.tensor_scalar(inverse[:, :], got[:, :, F:HW].rearrange("p u o -> p (u o)"), 1.0, None, ALU.max))
                    step(nc.vector.reciprocal(inverse[:, :], inverse[:, :]))
                    if stage == 1:
                        dve.wait_ge(scal_in, 16 * LANES * i + 16 * LANES)
                        step(nc.vector.tensor_tensor(inverse[:, :], inverse[:, :], scal[:, :, 1:2].rearrange("p u o -> p (u o)"), ALU.mult))
                    step(nc.vector.tensor_tensor(inverse[:, :], inverse[:, :], tiles_of(net.light, i), ALU.mult))
                    nc.vector.tensor_tensor(mean[:, :, :], got[:, :, 0:F], over(inverse[:, :], F), ALU.mult).then_inc(mean_ready, 1)
                    assert step.n == n_steps
                    dve.wait_ge(turned_ready, r + (stage + 2))
                    nc.vector.tensor_copy(mean_t[:, :], turned[0:F, 0:LANES * P]).then_inc(mean_t_ready, 1)
                    dve.wait_ge(product_ready, r + (stage + 2))
                    nc.vector.tensor_copy(summed[:, :], product[:, 0:LANES * F]).then_inc(summed_ready, 1)

            @block.tensor
            def _(pe):
                def through_w(n, tiles, to_sum):
                    pe.wait_ge(mean_ready, n)
                    for u in range(tiles):
                        last = nc.tensor.matmul(turned[0:F, u * P:(u + 1) * P], mean[:, u, :], to_sum(u), start=True, stop=True)
                    last.then_inc(turned_ready, 1)
                    pe.wait_ge(mean_t_ready, n)
                    for u in range(tiles):
                        last = nc.tensor.matmul(product[:, u * F:(u + 1) * F], mean_t[:, u * P:(u + 1) * P],
                                                net.conv_w[stage][:, :], start=True, stop=True)
                    last.then_inc(product_ready, 1)

                loop, first = light_rounds(pe)
                through_w(first + (stage + 1), 1, lambda u: net.ident[:, :])
                with loop as i:
                    r = i + first
                    through_w(r + (stage + 2), LANES, lambda u: same[:, u, :])


def chunk_ticks(engine, *stages):
    last_lag = max(lag for _, lag in stages)
    turn = KEPT // SLOTS

    def ticks(i, at, k_range=range(SLOTS)):
        for k in k_range:
            for step, lag in stages:
                n = SLOTS * at + k - lag
                if 0 <= n < NC:
                    step(SLOTS * i + (k - lag), n % SLOTS, i + (n // SLOTS - at), n < KEPT)

    ticks(0, 0)
    with engine.Fori(1, turn) as i:
        ticks(i, turn - 1)
    ticks(turn, turn)
    with engine.Fori(turn + 1, NC // SLOTS) as i:
        ticks(i, turn + 1)
    ticks(NC // SLOTS, NC // SLOTS, range(1 + last_lag))


def wait_chunks(engine, sem, before, chunks):
    if not isinstance(chunks, int) or chunks > 0:
        engine.wait_ge(sem, chunks + before)


def slot_rounds(k):
    return NC // SLOTS + (k < NC % SLOTS)


def norm_nodes(net):
    nc = net.nc
    with ExitStack() as ctx:
        def sb(name, shape, dt=F32):
            return ctx.enter_context(nc.sbuf_tensor(f"ln_{name}", shape, dt))

        def sem(name):
            return ctx.enter_context(nc.semaphore(f"ln_{name}"))

        bias = sb("bias", [P, G, F])
        xt, far, dev, h = ([sb(f"{n}{k}", [P, G, F]) for k in range(SLOTS)] for n in ("xt", "far", "dev", "h"))
        sq = [sb(f"sq{k}", [P, G, F]) for k in range(2)]
        mean, var, scale = ([sb(f"{n}{k}", [P, G]) for k in range(SLOTS)] for n in ("mean", "var", "scale"))
        far_ready, far_added, x_ready, mean_ready, dev_ready, sq_ready, var_ready, root_ready, scale_ready, h_ready, dve_step, scale_step = (
            sem(n) for n in ("far_ready", "far_added", "x_ready", "mean_ready", "dev_ready", "sq_ready", "var_ready",
                             "root_ready", "scale_ready", "h_ready", "dve_step", "scale_step"))
        loaded, x_stored, y_stored = ([sem(f"{n}{k}") for k in range(SLOTS)] for n in ("loaded", "x_stored", "y_stored"))
        x1, y = node_chunks(net.x1), node_chunks(net.y)

        def over_features(t):
            return t.rearrange("p (g o) -> p g o", o=1).broadcast_to([P, G, F])

        def over_nodes(t):
            return t.rearrange("p (o f) -> p o f", o=1).broadcast_to([P, G, F])

        def flat(t):
            return t[:, :, :].rearrange("p g f -> p (g f)")

        with nc.Block() as block:
            @block.sync
            def _(sp):
                def load(c, k, i, kept):
                    sp.wait_ge(x_stored[k], 16 * i)
                    wait_chunks(sp, dev_ready, 0, c - (SLOTS - 1))
                    sp.dma_start(flat(xt[k]), chunk_of(x1, c)).then_inc(loaded[k], 16)

                def store(c, k, i, kept):
                    sp.wait_ge(x_ready, c + 1)
                    sp.dma_start(chunk_of(x1, c), flat(xt[k])).then_inc(x_stored[k], 16)

                chunk_ticks(sp, (load, 0), (store, 2))
                for k in range(SLOTS):
                    sp.wait_ge(x_stored[k], 16 * slot_rounds(k))

            @block.gpsimd
            def _(pool):
                def far_row(c, k, i, kept):
                    wait_chunks(pool, x_ready, 0, c - (SLOTS - 1))
                    nc.gpsimd.tensor_tensor(far[k][:, :, :], over_features(net.far_share[:, bass.ds(c * G, G)]),
                                            over_nodes(net.e2_last[:, :]), ALU.mult).then_inc(far_ready, 1)

                def deviation(c, k, i, kept):
                    pool.wait_ge(mean_ready, c + 1)
                    wait_chunks(pool, h_ready, 0, c - (SLOTS - 1))
                    nc.gpsimd.tensor_tensor(dev[k][:, :, :], xt[k][:, :, :], over_features(mean[k][:, :]), ALU.subtract).then_inc(dev_ready, 1)

                chunk_ticks(pool, (far_row, 0), (deviation, 1))

            @block.vector
            def _(dve):
                nc.vector.tensor_copy(bias[:, :, :], over_nodes(net.conv_b[1][:, :])).then_inc(dve_step, 1)
                dve.wait_ge(dve_step, 1)

                def add(c, k, i, kept):
                    step = Chain(dve, dve_step, c + 1)
                    dve.wait_ge(far_ready, c + 1)
                    nc.vector.tensor_tensor(far[k][:, :, :], far[k][:, :, :], bias[:, :, :], ALU.add).then_inc(far_added, 1)
                    dve.wait_ge(far_added, c + 1)
                    dve.wait_ge(loaded[k], 16 * i + 16)
                    nc.vector.tensor_tensor(xt[k][:, :, :], xt[k][:, :, :], far[k][:, :, :], ALU.add).then_inc(x_ready, 1)
                    dve.wait_ge(x_ready, c + 1)
                    step(nc.vector.tensor_reduce(mean[k][:, :], xt[k][:, :, :], AX.X, ALU.add))
                    nc.vector.tensor_scalar(mean[k][:, :], mean[k][:, :], 1.0 / F, None, ALU.mult).then_inc(mean_ready, 1)

                def variance(c, k, i, kept):
                    dve.wait_ge(sq_ready, c + 1)
                    nc.vector.tensor_reduce(var[k][:, :], sq[k % 2][:, :, :], AX.X, ALU.add).then_inc(var_ready, 1)

                def scales(c, k, i, kept):
                    step = Chain(dve, scale_step, c)
                    dve.wait_ge(root_ready, c + 1)
                    step(nc.vector.reciprocal(scale[k][:, :], scale[k][:, :]))
                    nc.vector.tensor_tensor(scale[k][:, :], scale[k][:, :], net.dinv[:, bass.ds(c * G, G)], ALU.mult).then_inc(scale_ready, 1)

                chunk_ticks(dve, (add, 0), (variance, 2), (scales, 3))

            @block.scalar
            def _(act):
                def square(c, k, i, kept):
                    act.wait_ge(dev_ready, c + 1)
                    wait_chunks(act, var_ready, 0, c - 1)
                    nc.scalar.activation(sq[k % 2][:, :, :], dev[k][:, :, :], ACT.Square).then_inc(sq_ready, 1)

                def root(c, k, i, kept):
                    act.wait_ge(var_ready, c + 1)
                    nc.scalar.activation(scale[k][:, :], var[k][:, :], ACT.Sqrt, bias=net.eps[:, :], scale=1.0 / F).then_inc(root_ready, 1)

                def relu(c, k, i, kept):
                    act.wait_ge(scale_ready, c + 1)
                    act.wait_ge(y_stored[k], 16 * i)
                    for g in range(G):
                        last = nc.scalar.activation(h[k][:, g, :], dev[k][:, g, :], ACT.Relu, scale=scale[k][:, g:g + 1])
                    last.then_inc(h_ready, 1)
                    act.wait_ge(h_ready, c + 1)
                    act.dma_start(chunk_of(y, c), flat(h[k])).then_inc(y_stored[k], 16)

                chunk_ticks(act, (square, 1), (root, 2), (relu, 3))
                for k in range(SLOTS):
                    act.wait_ge(y_stored[k], 16 * slot_rounds(k))


def add_edges(net, layer, sems):
    nc = net.nc
    with ExitStack() as ctx:
        def sb(name, shape, dt=F32):
            return ctx.enter_context(nc.sbuf_tensor(f"e{layer}_{name}", shape, dt))

        B = 2
        src_i = [sb(f"src_i{b}", [P, LANES], I32) for b in range(B)]
        dst_i = [sb(f"dst_i{b}", [P, LANES], I32) for b in range(B)]
        same = [sb(f"same{b}", [P, LANES, P]) for b in range(B)]
        got = [sb(f"got{b}", [P, LANES, F]) for b in range(B)]
        summed = sb("summed", [P, STEPS, LANES * F])
        to_add = [sb(f"to_add{b}", [P, LANES, F]) for b in range(B)]
        sums = [ctx.enter_context(nc.psum_tensor(f"e{layer}_sums{b}", [P, 512], F32)) for b in range(B)]
        src_ready, same_in, gathered, sums_ready, summed_ready, add_ready = (sems[n] for n in
            ("src_ready", "same_in", "gathered", "sums_ready", "summed_ready", "add_ready"))
        added, v_copied = sems["added"], sems["v_copied"][0]
        done = layer * (STEPS // B)
        src_cols = net.src_idx[:, :].rearrange("p (u i) -> p i u", u=LANES)
        dst_cols = net.dst_idx[:, :].rearrange("p (u i) -> p i u", u=LANES)

        with nc.Block() as block:
            @block.sync
            def _(sp):
                sp.dma_start(net.v[0:NP, :].rearrange("(a b) f -> a (b f)", b=64),
                             net.y.rearrange("(a b) f -> a (b f)", b=64)).then_inc(v_copied, 16)
                with sp.Fori(0, STEPS // B) as i:
                    for b in range(B):
                        sp.wait_ge(sums_ready[b], done + i)
                        sp.dma_start(same[b][:, :, :].rearrange("p u k -> p (u k)"),
                                     chunk_of(net.same_dst, i * B + b)).then_inc(same_in[b], 16)

            @block.gpsimd
            def _(pool):
                unsorted = pool.value_load(net.bounds[0:1, 1:2], min_val=0, max_val=1)
                with pool.Fori(0, STEPS // B) as i:
                    for b in range(B):
                        pool.wait_ge(src_ready[b], done + i + 1)
                        wait_alone(pool, sums_ready[b], done + i, net)
                        for u in range(LANES):
                            pool.indirect_dma_start(out=got[b][:, u, :], out_offset=None, in_=net.y[:, :],
                                                    in_offset=bass.IndirectOffsetOnAxis(ap=src_i[b][:, u:u + 1], axis=0)
                                                    ).then_inc(gathered[b], 16)
                pool.wait_ge(v_copied, 16 * layer + 16)
                with pool.Fori(0, STEPS // B) as i:
                    for b in range(B):
                        pool.wait_ge(add_ready[b], 2 * (done + i) + 2)
                        for u in range(LANES):
                            before = 16 * STEPS * layer + 32 * i + 16 * (b + (u > 0))
                            pool.wait_ge(added[u - 1], before * unsorted)
                            wait_alone(pool, added[u], 16 * STEPS * layer + 32 * i + 16 * b, net)
                            pool.indirect_dma_start(out=net.v[:, :],
                                                    out_offset=bass.IndirectOffsetOnAxis(ap=dst_i[b][:, u:u + 1], axis=0),
                                                    in_=to_add[b][:, u, :], in_offset=None, compute_op=ALU.add
                                                    ).then_inc(added[u], 16)
                for u in range(LANES):
                    pool.wait_ge(added[u], 16 * STEPS * (layer + 1))

            @block.vector
            def _(dve):
                with dve.Fori(0, STEPS // B) as i:
                    for b in range(B):
                        wait_alone(dve, gathered[b], 16 * LANES * (done + i), net)
                        nc.vector.tensor_copy(src_i[b][:, :], src_cols[:, bass.ds(i * B + b, 1), :].rearrange("p a u -> p (a u)")
                                              ).then_inc(src_ready[b], 1)
                    for b in range(B):
                        dve.wait_ge(sums_ready[b], done + i + 1)
                        nc.vector.tensor_copy(summed[:, bass.ds(i * B + b, 1), :].rearrange("p a n -> p (a n)"),
                                              sums[b][:, 0:LANES * F]).then_inc(summed_ready[b], 1)
                for b in range(B):
                    dve.wait_ge(summed_ready[b], done + STEPS // B)
                def stage_adds(b, at):
                    nc.vector.tensor_copy(dst_i[b][:, :], dst_cols[:, bass.ds(at, 1), :].rearrange("p a u -> p (a u)")
                                          ).then_inc(add_ready[b], 1)
                    nc.vector.tensor_copy(to_add[b][:, :, :].rearrange("p u f -> p (u f)"),
                                          summed[:, bass.ds(at, 1), :].rearrange("p a n -> p (a n)")).then_inc(add_ready[b], 1)

                for b in range(B):
                    stage_adds(b, b)
                with dve.Fori(1, STEPS // B) as i:
                    for b in range(B):
                        for u in range(LANES - 1):
                            dve.wait_ge(added[u], 16 * STEPS * layer + 32 * i + 16 * (b - 1))
                        wait_alone(dve, added[LANES - 1], 16 * STEPS * layer + 32 * i + 16 * (b - 1), net)
                        stage_adds(b, i * B + b)

            @block.tensor
            def _(pe):
                with pe.Fori(0, STEPS // B) as i:
                    for b in range(B):
                        pe.wait_ge(same_in[b], 16 * (done + i) + 16)
                        pe.wait_ge(gathered[b], 16 * LANES * (done + i) + 16 * LANES)
                        pe.wait_ge(summed_ready[b], done + i)
                        for u in range(LANES):
                            last = nc.tensor.matmul(sums[b][:, u * F:(u + 1) * F], same[b][:, u, :], got[b][:, u, :],
                                                    start=True, stop=True)
                        last.then_inc(sums_ready[b], 1)


def transform(net, layer, sems, stats, z_kept):
    nc = net.nc
    with ExitStack() as ctx:
        def sb(name, shape, dt=F32):
            return ctx.enter_context(nc.sbuf_tensor(f"t{layer}_{name}", shape, dt))

        rows = [sb(f"rows{k}", [P, G, F]) for k in range(SLOTS)]
        turned = [sb(f"turned{k}", [P, G * F]) for k in range(2)]
        z_out = [sb(f"z_out{k}", [P, G * F]) for k in range(2)]
        t_ps = [ctx.enter_context(nc.psum_tensor(f"t{layer}_t_ps{k}", [P, G * F], F32)) for k in range(2)]
        m_ps = [ctx.enter_context(nc.psum_tensor(f"t{layer}_m_ps{k}", [P, G * F], F32)) for k in range(2)]
        scaled_ready, t_ready, turned_ready, m_ready, z_ready, counted = (sems[n][0] for n in
            ("scaled_ready", "t_ready", "turned_ready", "m_ready", "z_ready", "counted"))
        loaded, z_stored = sems["loaded"], sems["z_stored"]
        v = node_chunks(net.v)
        chunks, halves = layer * NC, 2 * layer * NC

        def z_half(c, k, h, kept):
            if kept:
                return z_kept[:, bass.ds(c * (G * F) + h * 512, 512)]
            return z_out[k % 2][:, h * 512:(h + 1) * 512]

        with nc.Block() as block:
            @block.sync
            def _(sp):
                def load(c, k, i, kept):
                    wait_chunks(sp, t_ready, halves, 2 * (c - (SLOTS - 1)))
                    sp.dma_start(rows[k][:, :, :].rearrange("p g f -> p (g f)"), chunk_of(v, c)).then_inc(loaded[k], 16)

                chunk_ticks(sp, (load, 0))

            @block.gpsimd
            def _(pool):
                def store(c, k, i, kept):
                    if not kept:
                        pool.wait_ge(z_ready, 2 * c + (halves + 2))
                        pool.dma_start(chunk_of(net.z, c), z_out[k % 2][:, :]).then_inc(z_stored[k % 2], 16)

                chunk_ticks(pool, (store, 0))
                for k in range(2):
                    pool.wait_ge(z_stored[k], 16 * SPILLED[k] * (layer + 1))

            @block.vector
            def _(dve):
                def scale(c, k, i, kept):
                    dve.wait_ge(loaded[k], 16 * (i + layer * slot_rounds(k)) + 16)
                    nc.vector.tensor_tensor(rows[k][:, :, :], rows[k][:, :, :],
                                            net.dinv[:, bass.ds(c * G, G)].rearrange("p (g o) -> p g o", o=1).broadcast_to([P, G, F]),
                                            ALU.mult).then_inc(scaled_ready, 1)

                def count(c, k, i, kept):
                    for h in range(2):
                        dve.wait_ge(z_ready, 2 * c + (halves + h + 1))
                        unit = z_half(c, k, h, kept)
                        if isinstance(c, int) and c == NC - 1:
                            unit = unit.rearrange("q (j p) -> q j p", p=P)[:, :, 0:TAIL_P]
                        nc.vector.bn_stats(stats[:, bass.ds(2 * c + h, 1), :].rearrange("p a s -> p (a s)"), unit).then_inc(counted, 1)

                chunk_ticks(dve, (scale, 0), (count, 3))

            @block.tensor
            def _(pe):
                def turn(c, k, i, kept):
                    pe.wait_ge(scaled_ready, c + (chunks + 1))
                    wait_chunks(pe, turned_ready, halves, 2 * (c - 1))
                    for j in range(G // 2):
                        t = nc.tensor.transpose(t_ps[k % 2][:, j * P:(j + 1) * P],
                                                rows[k][:, 2 * j:2 * j + 2, :].rearrange("p g f -> p (g f)"), net.ident[:, :])
                        if j % 4 == 3:
                            t.then_inc(t_ready, 1)

                def product(c, k, i, kept):
                    wait_chunks(pe, z_ready, halves, 2 * (c - 1))
                    for h in range(2):
                        pe.wait_ge(turned_ready, 2 * c + (halves + h + 1))
                        nc.tensor.matmul(m_ps[k % 2][:, h * 512:(h + 1) * 512], net.gcn_w[layer][:, :],
                                         turned[k % 2][:, h * 512:(h + 1) * 512], start=True, stop=True).then_inc(m_ready, 1)

                chunk_ticks(pe, (turn, 0), (product, 1))

            @block.scalar
            def _(act):
                def copy(c, k, i, kept):
                    wait_chunks(act, m_ready, halves, 2 * (c - 1))
                    for h in range(2):
                        part = slice(h * 512, (h + 1) * 512)
                        act.wait_ge(t_ready, 2 * c + (halves + h + 1))
                        nc.scalar.activation(turned[k % 2][:, part], t_ps[k % 2][:, part], ACT.Copy).then_inc(turned_ready, 1)

                def relu(c, k, i, kept):
                    if not kept:
                        wait_chunks(act, counted, halves, 2 * (c - 1))
                        act.wait_ge(z_stored[k % 2], 16 * (2 * i + k // 2 - KEPT // 2 + layer * SPILLED[k % 2]))
                    for h in range(2):
                        act.wait_ge(m_ready, 2 * c + (halves + h + 1))
                        nc.scalar.activation(z_half(c, k, h, kept), m_ps[k % 2][:, h * 512:(h + 1) * 512], ACT.Relu,
                                             bias=net.gcn_b[:, layer:layer + 1]).then_inc(z_ready, 1)

                chunk_ticks(act, (copy, 0), (relu, 1))


def batch_norm_factors(net, layer, sems, stats, factor, offset):
    nc = net.nc
    with ExitStack() as ctx:
        def sb(name, shape, dt=F32):
            return ctx.enter_context(nc.sbuf_tensor(f"f{layer}_{name}", shape, dt))

        mv, moments, mean, var, square, root = sb("mv", [P, 2]), sb("moments", [P, 2]), sb("mean", [P, 1]), sb("var", [P, 1]), sb("square", [P, 1]), sb("root", [P, 1])
        mixed = ctx.enter_context(nc.psum_tensor(f"f{layer}_mixed", [P, 512], F32))
        moments_ready, mixed_ready, var_ready, root_ready, dve_step = (sems[n][0] for n in
            ("moments_ready", "mixed_ready", "var_ready", "root_ready", "factor_step"))
        with nc.Block() as block:
            @block.vector
            def _(dve):
                step = Chain(dve, dve_step, layer * 8)
                step(nc.vector.bn_aggr(mv[:, :], stats[:, :, :].rearrange("p c s -> p (c s)")))
                step(nc.vector.tensor_copy(moments[:, 0:1], mv[:, 0:1]))
                nc.vector.scalar_tensor_tensor(out=moments[:, 1:2], in0=mv[:, 0:1], scalar=mv[:, 0:1], in1=mv[:, 1:2],
                                               op0=ALU.mult, op1=ALU.add).then_inc(moments_ready, 1)
                dve.wait_ge(mixed_ready, layer + 1)
                step(nc.vector.tensor_copy(mean[:, :], mixed[:, 0:1]))
                step(nc.vector.tensor_tensor(square[:, :], mean[:, :], mean[:, :], ALU.mult))
                nc.vector.tensor_tensor(var[:, :], mixed[:, 1:2], square[:, :], ALU.subtract).then_inc(var_ready, 1)
                dve.wait_ge(root_ready, layer + 1)
                step(nc.vector.reciprocal(root[:, :], root[:, :]))
                step(nc.vector.tensor_tensor(factor[:, :], root[:, :], net.gamma[:, layer:layer + 1], ALU.mult))
                step(nc.vector.tensor_tensor(offset[:, :], mean[:, :], factor[:, :], ALU.mult))
                step(nc.vector.tensor_tensor(offset[:, :], net.beta[:, layer:layer + 1], offset[:, :], ALU.subtract))
                assert step.n == 8

            @block.tensor
            def _(pe):
                pe.wait_ge(moments_ready, layer + 1)
                nc.tensor.matmul(mixed[:, 0:2], net.pair_mean[:, :], moments[:, :], start=True, stop=True).then_inc(mixed_ready, 1)

            @block.scalar
            def _(act):
                act.wait_ge(var_ready, layer + 1)
                nc.scalar.activation(root[:, :], var[:, :], ACT.Sqrt, bias=net.eps[:, :]).then_inc(root_ready, 1)


def normalise(net, layer, sems, factor, offset, out, z_kept):
    nc = net.nc
    final = layer == 2
    with ExitStack() as ctx:
        def sb(name, shape, dt=F32):
            return ctx.enter_context(nc.sbuf_tensor(f"b{layer}_{name}", shape, dt))

        z_in = [sb(f"z_in{k}", [P, G * F]) for k in range(2)]
        normed = [sb(f"normed{k}", [P, G * F]) for k in range(2)]
        rows = [sb(f"rows{k}", [P, G, F]) for k in range(SLOTS)]
        ps = [ctx.enter_context(nc.psum_tensor(f"b{layer}_ps{k}", [P, G * F], F32)) for k in range(SLOTS)]
        normed_ready, t_ready, rows_ready = (sems[n][0] for n in ("normed_ready", "b_t_ready", "rows_ready"))
        z_loaded, stored, x_in = sems["z_loaded"], sems["stored"], sems["x_in"]
        y, x1 = node_chunks(net.y), node_chunks(net.x1)
        out_chunks = node_chunks(out, (NC - 1) * CHUNK)
        chunks = layer * NC

        with nc.Block() as block:
            @block.sync
            def _(sp):
                def load(c, k, i, kept):
                    if not kept:
                        wait_chunks(sp, normed_ready, chunks, c - 1)
                        sp.dma_start(z_in[k % 2][:, :], chunk_of(net.z, c)).then_inc(z_loaded[k % 2], 16)
                    if final:
                        sp.wait_ge(stored[k], 16 * (i + layer * slot_rounds(k)))
                        sp.dma_start(rows[k][:, :, :].rearrange("p g f -> p (g f)"), chunk_of(x1, c)).then_inc(x_in[k], 16)

                chunk_ticks(sp, (load, 0))

            @block.scalar
            def _(act):
                def norm(c, k, i, kept):
                    wait_chunks(act, t_ready, chunks, c - 1)
                    if not kept:
                        act.wait_ge(z_loaded[k % 2], 16 * (2 * i + k // 2 - KEPT // 2 + layer * SPILLED[k % 2]) + 16)
                    z = z_kept[:, bass.ds(c * (G * F), G * F)] if kept else z_in[k % 2][:, :]
                    nc.scalar.activation(normed[k % 2][:, :], z, ACT.Identity, bias=offset[:, :], scale=factor[:, :]
                                         ).then_inc(normed_ready, 1)

                chunk_ticks(act, (norm, 0))

            @block.tensor
            def _(pe):
                def turn(c, k, i, kept):
                    pe.wait_ge(normed_ready, c + (chunks + 1))
                    wait_chunks(pe, rows_ready, chunks, c - (SLOTS - 1))
                    for j in range(G // 2):
                        t = nc.tensor.transpose(ps[k][:, j * P:(j + 1) * P], normed[k % 2][:, j * P:(j + 1) * P], net.ident[:, :])
                    t.then_inc(t_ready, 1)

                chunk_ticks(pe, (turn, 0))

            @block.vector
            def _(dve):
                def finish(c, k, i, kept):
                    dve.wait_ge(t_ready, c + (chunks + 1))
                    got = ps[k][:, :].rearrange("p (g f) -> p g f", g=G)
                    if final:
                        dve.wait_ge(x_in[k], 16 * i + 16)
                        nc.vector.tensor_tensor(rows[k][:, :, :], got, rows[k][:, :, :], ALU.add).then_inc(rows_ready, 1)
                    else:
                        dve.wait_ge(stored[k], 16 * (i + layer * slot_rounds(k)))
                        nc.vector.tensor_tensor(rows[k][:, :, :], got,
                                                net.dinv[:, bass.ds(c * G, G)].rearrange("p (g o) -> p g o", o=1).broadcast_to([P, G, F]),
                                                ALU.mult).then_inc(rows_ready, 1)

                chunk_ticks(dve, (finish, 0))

            @block.gpsimd
            def _(pool):
                def store(c, k, i, kept):
                    pool.wait_ge(rows_ready, c + (chunks + 1))
                    flat = rows[k][:, :, :].rearrange("p g f -> p (g f)")
                    if not final:
                        pool.dma_start(chunk_of(y, c), flat).then_inc(stored[k], 16)
                    elif not (isinstance(c, int) and c == NC - 1):
                        pool.dma_start(chunk_of(out_chunks, c), flat).then_inc(stored[k], 16)
                    else:
                        tail = out[(NC - 1) * CHUNK:N, :].rearrange("(p g) f -> p (g f)", g=G)
                        cut = TAIL_P // 16 * 16
                        pool.dma_start(tail[0:cut, :], flat[0:cut, :]).then_inc(stored[k], 16)
                        pool.dma_start(tail[cut:TAIL_P, :], flat[cut:TAIL_P, :]).then_inc(stored[k], 16)

                chunk_ticks(pool, (store, 0))
                for k in range(SLOTS):
                    pool.wait_ge(stored[k], 16 * (slot_rounds(k) * (layer + 1) + (final and k == 0)))


def build_network(nc, args, out, upto=99):
    with ExitStack() as ctx:
        net = Net(nc, ctx, args)

        def sems(names, n):
            return {name: [ctx.enter_context(nc.semaphore(f"{name}{k}")) for k in range(n)] for name in names}

        load_tables(net)
        count_nodes(net)
        conv_sems = sems(("h_idx_ready", "h_gathered", "h_same_in", "h_act_in", "h_act_out", "h_msg_ready", "h_sums_ready",
                          "h_summed_ready", "h_added", "h_scal_in", "n_last_in", "n_idx_ready", "n_to_ready", "n_gathered",
                          "n_row_in", "n_row_used", "n_mean_ready", "n_turned_ready", "n_mean_t_ready", "n_product_ready",
                          "n_summed_ready", "n_added", "n_scal_in"), 1) | sems(("h_dve_step", "n_dve_step"), 2)
        for stage in range(2):
            nodes_to_hyperedges(net, stage, conv_sems)
            hyperedges_to_nodes(net, stage, conv_sems)
        norm_nodes(net)
        stats = ctx.enter_context(nc.sbuf_tensor("stats", [P, 2 * NC, 6], F32))
        factor = ctx.enter_context(nc.sbuf_tensor("factor", [P, 1], F32))
        offset = ctx.enter_context(nc.sbuf_tensor("offset", [P, 1], F32))
        edge_sems = sems(("src_ready", "same_in", "gathered", "sums_ready", "summed_ready", "add_ready"), 2)
        edge_sems |= sems(("added",), LANES) | sems(("v_copied",), 1)
        node_sems = sems(("scaled_ready", "t_ready", "turned_ready", "m_ready", "z_ready", "counted"), 1)
        node_sems |= sems(("z_stored",), 2) | sems(("loaded",), SLOTS)
        norm_sems = sems(("normed_ready", "b_t_ready", "rows_ready"), 1) | sems(("z_loaded",), 2) | sems(("stored", "x_in"), SLOTS)
        factor_sems = sems(("moments_ready", "mixed_ready", "var_ready", "root_ready", "factor_step"), 1)
        for layer in range(3):
            add_edges(net, layer, edge_sems)
            with nc.sbuf_tensor(f"z_kept{layer}", [P, KEPT * G * F], F32) as z_kept:
                transform(net, layer, node_sems, stats, z_kept)
                batch_norm_factors(net, layer, factor_sems, stats, factor, offset)
                normalise(net, layer, norm_sems, factor, offset, out, z_kept)


_INS = ["x", "src", "dst", "L0_gnn_W1", "L0_gnn_b1", "L0_gnn_W2", "L0_gnn_b2"] + [
    f"L1_gnn_{n}{i}" for i in (1, 2, 3) for n in ("W", "b", "gamma", "beta")]


def kernel(**inputs):
    import numpy as np
    import concourse.bacc as bacc
    from concourse.bass_utils import run_bass_kernel_spmd

    nc = bacc.Bacc("TRN2", target_bir_lowering=False, num_devices=1)
    arrays, args = {}, {}
    for name in _INS:
        a = np.ascontiguousarray(inputs[name])
        arrays[f"in_{name}"] = a
        args[name] = nc.dram_tensor(f"in_{name}", a.shape, mybir.dt.from_np(a.dtype), kind="ExternalInput").ap()
    out = nc.dram_tensor("out", (N, F), F32, kind="ExternalOutput").ap()
    build_network(nc, args, out)
    return run_bass_kernel_spmd(nc, [arrays], core_ids=[0]).results[0]["out"]
```

```python
import concourse.bass as bass
from concourse import mybir
from contextlib import ExitStack

F32 = mybir.dt.float32
F16 = mybir.dt.float16
I32 = mybir.dt.int32
ACT = mybir.ActivationFunctionType
ALU = mybir.AluOpType
AX = mybir.AxisListType

P = 128
N, E, F = 100000, 25000, 64
HYPER = 3125
EPS = 1e-5

G = 16
CHUNK = P * G
NC = -(-N // CHUNK)
NP = NC * CHUNK
SLOTS = 4
KEPT = 36
KEPT_G = 28
LOAD_LEAD = 3
GW = F + 1
SPILLED = (-(-(NC - KEPT) // 2), (NC - KEPT) // 2)
TAIL_P = (N - (NC - 1) * CHUNK) // G
COLS = NC * G
DUMMY = NP

TILES = -(-E // P)
LANES = 7
STEPS = TILES // LANES
ROUNDS = STEPS // SLOTS
DEPTH = 2
WINDOWS = STEPS // DEPTH
TURN_CHUNKS = NC // ROUNDS
REACH = DEPTH - 1
EP = TILES * P
PAD_NODE = NP - 1
ROWS2 = TILES - P
HDUMMY = HYPER
HROWS = 32 * P
X_PIECES = 10
CONV_PIECES = 20
HW = F + 1


def node_chunks(table, rows=NP):
    return table[0:rows, :].rearrange("(c p g) f -> c p (g f)", p=P, g=G)


def window_of(i, b):
    return i * (SLOTS // DEPTH) + b // DEPTH


def chunk_of(view, c):
    return view[bass.ds(c, 1), :, :].rearrange("a p n -> (a p) n")


class Net:

    def __init__(self, nc, ctx, early_ctx, args):
        self.nc, self.args = nc, args

        def sb(name, shape, dt=F32):
            return ctx.enter_context(nc.sbuf_tensor(name, shape, dt))

        def early(name, shape, dt=F32):
            return early_ctx.enter_context(nc.sbuf_tensor(name, shape, dt))

        def dram(name, shape, dt=F32):
            return nc.dram_tensor(name, shape, dt, kind="Internal").ap()

        self.prepared = ctx.enter_context(nc.semaphore("prepared"))
        self.passed = ctx.enter_context(nc.semaphore("passed"))
        self.x1 = dram("x1_rows", (NP + P, F))
        self.conv = dram("conv_rows", (NP + P, F))
        self.y = dram("y_rows", (NP, F))
        self.g = dram("g_rows", (NP, GW))
        self.v = dram("v_rows", (NP + LANES * P, F))
        self.z = dram("z_units", (NC, P, G // 2 * P))
        self.node_scalars = dram("node_scalars", (NP, 2))
        self.hyper1 = dram("hyper1_rows", (HROWS, HW))
        self.hyper2 = dram("hyper2_rows", (HROWS, HW))
        self.src_padded = dram("src_padded", (TILES, P), I32)
        self.dst_padded = dram("dst_padded", (TILES, P), I32)
        self.same_dst = dram("same_dst", (TILES, P, P))
        self.summed = dram("summed_rows", (STEPS, P, LANES * F))
        self.src_idx = sb("src_idx", [P, TILES], I32)
        self.dst_idx = sb("dst_idx", [P, TILES], I32)
        self.bounds = sb("bounds", [1, 2], I32)
        self.windows = sb("windows", [1, NC], I32)
        self.dinv = sb("dinv", [P, COLS])
        self.ident = sb("ident", [P, P])
        self.pair_mean = sb("pair_mean", [P, P])
        self.part = sb("part", [P, 1])
        self.eps = sb("eps", [P, 1])
        self.ones = sb("ones", [F, P])
        self.gcn_w = [sb(f"gcn_w{i}", [P, P]) for i in range(3)]
        self.gcn_b = sb("gcn_b", [P, 3])
        self.gamma = sb("gamma", [P, 3])
        self.beta = sb("beta", [P, 3])
        self.far_share = early("far_share", [P, COLS])
        self.before = early("before", [P, P])
        self.src_f = early("src_f", [P, TILES])
        self.dst_f = early("dst_f", [P, TILES])
        self.light = early("light", [P, TILES])
        self.clip_idx = early("clip_idx", [P, TILES], I32)
        self.light_idx = early("light_idx", [P, TILES], I32)
        self.e1_last = early("e1_last", [P, F])
        self.e2_last = early("e2_last", [P, F])
        self.conv_w = [early(f"conv_w{i}", [F, F]) for i in range(2)]
        self.conv_b = [early(f"conv_b{i}", [P, F]) for i in range(2)]


def wait_alone(engine, sem, value, net):
    engine.wait_ge(sem, value)
    engine.sem_inc(net.passed, 1)


class Chain:

    def __init__(self, engine, sem, base=0):
        self.engine, self.sem, self.base, self.n = engine, sem, base, 0

    def __call__(self, instruction):
        self.n += 1
        instruction.then_inc(self.sem, 1)
        self.engine.wait_ge(self.sem, self.base + self.n)


def load_tables(net):
    nc, a = net.nc, net.args
    with ExitStack() as ctx:
        def sb(name, shape, dt=F32):
            return ctx.enter_context(nc.sbuf_tensor(f"load_{name}", shape, dt))

        def sem(name):
            return ctx.enter_context(nc.semaphore(f"load_{name}"))

        names = ["src", "dst", "next"]
        rows = {n: sb(f"{n}_rows", [P, 2, P], I32) for n in names}
        rows_f = {n: sb(f"{n}_rows_f", [P, 2, P]) for n in names}
        zero = net.zero
        worse = sb("worse", [P, 2])
        last_tile = sb("last_tile", [P, 2])
        step_no = sb("step_no", [P, TILES])
        light_no = sb("light_no", [P, TILES])
        flags = sb("flags", [1, 2])
        far_equal = sb("far_equal", [P, TILES - REACH])
        far_any = sb("far_any", [P, 1])
        lowest = sb("lowest", [P, WINDOWS])
        lowest_all = sb("lowest_all", [1, WINDOWS])
        chunk_end = sb("chunk_end", [1, NC])
        window_no = sb("window_no", [1, NC, WINDOWS])
        reaches = sb("reaches", [1, NC, WINDOWS])
        n_windows = sb("n_windows", [1, NC])
        cols = {n: ctx.enter_context(nc.psum_tensor(f"{n}_cols", [P, 512], F32)) for n in ("src", "dst")}
        flag_rows = ctx.enter_context(nc.psum_tensor("flag_rows", [P, 512], F32))
        lowest_rows = ctx.enter_context(nc.psum_tensor("lowest_rows", [P, WINDOWS * P], F32))
        padded, edges_in, rows_ready, cols_ready = sem("padded"), sem("edges_in"), sem("rows_ready"), sem("cols_ready")
        consts_ready, zero_ready = sem("consts_ready"), sem("zero_ready")
        weights_in, padded_out = sem("weights_in"), sem("padded_out")
        flags_ready, flags_out, dve_step, pool_step = sem("flags_ready"), sem("flags_out"), sem("dve_step"), sem("pool_step")
        with nc.Block() as block:
            @block.sync
            def _(sp):
                sp.wait_ge(padded, 3)
                full = E // P - P
                rest = E - (P + full) * P
                count = 0
                for name, flat, off in (("src", a["src"], 0), ("dst", a["dst"], 0), ("next", a["dst"], 1)):
                    left = rest - off
                    sp.dma_start(rows[name][:, 0, :], flat[off:off + P * P].rearrange("(t p) -> t p", p=P)).then_inc(edges_in, 16)
                    sp.dma_start(rows[name][0:full, 1, :],
                                 flat[off + P * P:off + (P + full) * P].rearrange("(t p) -> t p", p=P)).then_inc(edges_in, 16)
                    sp.dma_start(rows[name][full:full + 1, 1, 0:left],
                                 flat[off + (P + full) * P:E].rearrange("(a p) -> a p", a=1)).then_inc(edges_in, 16)
                    count += 48
                sp.wait_ge(edges_in, count)
                for name, table in (("src", net.src_padded), ("dst", net.dst_padded)):
                    sp.dma_start(table[0:P, :], rows[name][:, 0, :]).then_inc(padded_out, 16)
                    sp.dma_start(table[P:TILES, :], rows[name][0:ROWS2, 1, :]).then_inc(padded_out, 16)
                sp.wait_ge(padded_out, 64)

            @block.scalar
            def _(act):
                act.wait_ge(zero_ready, 4)
                small = [(net.conv_w[0][:, :], a["L0_gnn_W1"]), (net.conv_w[1][:, :], a["L0_gnn_W2"])]
                for i, name in enumerate(("L0_gnn_b1", "L0_gnn_b2")):
                    small.append((net.conv_b[i][:, :], a[name].rearrange("(o f) -> o f", o=1).broadcast_to([P, F])))
                for i in range(3):
                    for h in range(2):
                        part = slice(h * F, (h + 1) * F)
                        small.append((net.gcn_w[i][part, part], a[f"L1_gnn_W{i + 1}"]))
                        for table, name in ((net.gcn_b, "b"), (net.gamma, "gamma"), (net.beta, "beta")):
                            small.append((table[part, i:i + 1], a[f"L1_gnn_{name}{i + 1}"].rearrange("(f o) -> f o", o=1)))
                for dst, src in small:
                    act.dma_start(dst, src).then_inc(weights_in, 16)
                act.dma_start(net.hyper1.rearrange("(p r) f -> p (r f)", p=P), zero[:, 0:HROWS // P * HW]).then_inc(net.prepared, 16)
                act.dma_start(net.hyper2.rearrange("(p r) f -> p (r f)", p=P), zero[:, 0:HROWS // P * HW]).then_inc(net.prepared, 16)
                act.dma_start(net.v[NP:NP + LANES * P, :].rearrange("(p r) f -> p (r f)", p=P), zero[:, 0:LANES * F]).then_inc(net.prepared, 16)
                act.dma_start(net.x1[N:NP + P, :].rearrange("(p r) f -> p (r f)", p=30),
                              zero[0:30, 0:(NP + P - N) * F // 30]).then_inc(net.prepared, 16)
                act.wait_ge(weights_in, 16 * len(small))

            @block.gpsimd
            def _(pool):
                for name in names:
                    nc.gpsimd.memset(rows[name][:, :, :], PAD_NODE).then_inc(padded, 1)
                for w in net.gcn_w:
                    nc.gpsimd.memset(w[:, :], 0.0).then_inc(zero_ready, 1)
                nc.gpsimd.memset(zero[:, :], 0.0).then_inc(zero_ready, 1)
                nc.gpsimd.memset(net.eps[:, :], EPS).then_inc(consts_ready, 1)
                nc.gpsimd.memset(net.ones[:, :], 1.0).then_inc(consts_ready, 1)
                step = Chain(pool, pool_step)
                step(nc.gpsimd.memset(net.ident[:, :], 0.0))
                nc.gpsimd.affine_select(out=net.ident[:, :], in_=net.ident[:, :], compare_op=ALU.not_equal, fill=1.0,
                                        base=0, pattern=[[-1, P]], channel_multiplier=1).then_inc(consts_ready, 1)
                step(nc.gpsimd.memset(net.before[:, :], 1.0))
                nc.gpsimd.affine_select(out=net.before[:, :], in_=net.before[:, :], compare_op=ALU.is_gt, fill=0.0,
                                        base=0, pattern=[[-1, P]], channel_multiplier=1).then_inc(consts_ready, 1)
                step(nc.gpsimd.memset(net.pair_mean[:, :], 0.0))
                for off in (-F, 0, F):
                    step(nc.gpsimd.affine_select(out=net.pair_mean[:, :], in_=net.pair_mean[:, :],
                                                 compare_op=ALU.not_equal, fill=0.5, base=off,
                                                 pattern=[[-1, P]], channel_multiplier=1))
                nc.gpsimd.iota(net.part[:, :], pattern=[[0, 1]], base=0, channel_multiplier=1,
                               allow_small_or_imprecise_dtypes=True).then_inc(consts_ready, 1)
                nc.gpsimd.iota(step_no[:, :], pattern=[[1, STEPS], [0, LANES]], base=1, channel_multiplier=0,
                               allow_small_or_imprecise_dtypes=True).then_inc(consts_ready, 1)
                nc.gpsimd.iota(chunk_end[:, :], pattern=[[CHUNK, NC]], base=CHUNK, channel_multiplier=0,
                               allow_small_or_imprecise_dtypes=True).then_inc(consts_ready, 1)
                nc.gpsimd.iota(window_no[:, :, :], pattern=[[0, NC], [1, WINDOWS]], base=1, channel_multiplier=0,
                               allow_small_or_imprecise_dtypes=True).then_inc(consts_ready, 1)

            @block.vector
            def _(dve):
                step = Chain(dve, dve_step)
                dve.wait_ge(edges_in, 144)
                for name in names:
                    nc.vector.tensor_copy(rows_f[name][:, :, :], rows[name][:, :, :]).then_inc(rows_ready, 1)
                dve.wait_ge(consts_ready, 8)
                dve.wait_ge(rows_ready, 3)
                step(nc.vector.tensor_tensor(rows_f["next"][:, :, :], rows_f["dst"][:, :, :], rows_f["next"][:, :, :], ALU.is_gt))
                step(nc.vector.tensor_reduce(worse[:, :], rows_f["next"][:, :, :], AX.X, ALU.max))
                step(nc.vector.tensor_reduce(last_tile[:, 1:2], worse[:, :], AX.X, ALU.max))
                dve.wait_ge(cols_ready, 4)
                for name, table in (("src", net.src_f), ("dst", net.dst_f)):
                    step(nc.vector.tensor_copy(table[:, :], cols[name][:, 0:TILES]))
                step(nc.vector.tensor_copy(net.src_idx[:, :], net.src_f[:, :]))
                step(nc.vector.tensor_scalar(net.light[:, :], net.dst_f[:, :], float(HYPER), None, ALU.is_lt))
                step(nc.vector.tensor_scalar(net.clip_idx[:, :], net.dst_f[:, :], float(HYPER - 1), None, ALU.min))
                step(nc.vector.tensor_tensor(far_equal[:, :], net.dst_f[:, 0:TILES - REACH], net.dst_f[:, REACH:TILES], ALU.is_equal))
                step(nc.vector.tensor_reduce(far_any[:, :], far_equal[:, :], AX.X, ALU.max))
                step(nc.vector.tensor_tensor(last_tile[:, 1:2], last_tile[:, 1:2], far_any[:, :], ALU.max))
                step(nc.vector.tensor_reduce(lowest[:, :], net.dst_f[:, :].rearrange("p (m t) -> p m t", m=WINDOWS), AX.X, ALU.min))
                step(nc.vector.tensor_tensor(light_no[:, :], net.light[:, :], step_no[:, :], ALU.mult))
                step(nc.vector.tensor_reduce(last_tile[:, 0:1], light_no[:, :], AX.X, ALU.max))
                nc.vector.tensor_scalar(last_tile[:, 0:1], last_tile[:, 0:1], 1.0, None, ALU.max).then_inc(flags_ready, 1)
                dve.wait_ge(flags_out, 2 + WINDOWS)
                for k in range(2):
                    step(nc.vector.tensor_reduce(flags[:, k:k + 1], flag_rows[0:1, k * P:(k + 1) * P], AX.X, ALU.max))
                step(nc.vector.tensor_copy(net.bounds[:, :], flags[:, :]))
                step(nc.vector.tensor_reduce(lowest_all[:, :], lowest_rows[0:1, :].rearrange("o (m p) -> o m p", m=WINDOWS), AX.X, ALU.min))
                step(nc.vector.tensor_tensor(reaches[:, :, :], chunk_end[:, :].rearrange("o (c a) -> o c a", a=1).broadcast_to([1, NC, WINDOWS]),
                                             lowest_all[:, :].rearrange("o (a m) -> o a m", a=1).broadcast_to([1, NC, WINDOWS]), ALU.is_gt))
                step(nc.vector.tensor_tensor(reaches[:, :, :], reaches[:, :, :], window_no[:, :, :], ALU.mult))
                step(nc.vector.tensor_reduce(n_windows[:, :], reaches[:, :, :], AX.X, ALU.max))
                step(nc.vector.tensor_copy(net.windows[:, :], n_windows[:, :]))

            @block.tensor
            def _(pe):
                pe.wait_ge(consts_ready, 8)
                pe.wait_ge(rows_ready, 3)
                for name in ("src", "dst"):
                    nc.tensor.transpose(cols[name][:, 0:P], rows_f[name][:, 0, :], net.ident[:, :]).then_inc(cols_ready, 1)
                    nc.tensor.transpose(cols[name][:, P:TILES], rows_f[name][0:ROWS2, 1, :],
                                        net.ident[0:ROWS2, 0:ROWS2]).then_inc(cols_ready, 1)
                pe.wait_ge(flags_ready, 1)
                for k in range(2):
                    nc.tensor.transpose(flag_rows[0:1, k * P:(k + 1) * P], last_tile[:, k:k + 1], net.ident[:, :]).then_inc(flags_out, 1)
                for m in range(WINDOWS):
                    nc.tensor.transpose(lowest_rows[0:1, m * P:(m + 1) * P], lowest[:, m:m + 1], net.ident[:, :]).then_inc(flags_out, 1)


def zero_conv(engine, net, first, last):
    conv = net.conv.rearrange("(p r) f -> p (r f)", p=P)
    width = (NP + P) * F // P // CONV_PIECES
    with engine.Fori(first, last) as i:
        engine.dma_start(conv[:, bass.ds(i * width, width)], net.zero[:, 0:width]).then_inc(net.prepared, 16)


def count_nodes(net):
    nc = net.nc
    half = COLS // 2
    with ExitStack() as ctx:
        def sb(name, shape, dt=F32):
            return ctx.enter_context(nc.sbuf_tensor(f"count_{name}", shape, dt))

        def sem(name):
            return ctx.enter_context(nc.semaphore(f"count_{name}"))

        iota_col = sb("iota_col", [P, COLS], F16)
        iota_part = sb("iota_part", [P, P], F16)
        ints = [sb(f"ints{i}", [P, TILES], I32) for i in range(3)]
        col_f = {n: sb(f"{n}_col", [P, TILES]) for n in ("src", "dst")}
        part_f = {n: sb(f"{n}_part", [P, TILES]) for n in ("src", "dst")}
        hot_col = {n: [sb(f"{n}_hot_col{u}", [P, COLS], F16) for u in range(LANES)] for n in ("src", "dst")}
        minus_part = [sb(f"minus_{n}_part", [P, TILES]) for n in ("dst", "src")]
        distance = [sb(f"distance{k}", [P, 2, LANES, P], F16) for k in range(2)]
        hot_part = [sb(f"hot_part{k}", [P, 2, LANES, P], F16) for k in range(2)]
        light_part = sb("light_part", [P, P], F16)
        one = sb("one", [P, 1])
        nothing = sb("nothing", [P, 512], F16)
        dst_row = [sb(f"dst_row{i}", [P, LANES, P], I32) for i in range(2)]
        same = [sb(f"same{i}", [P, LANES, P]) for i in range(2)]
        earlier = [sb(f"earlier{i}", [P, LANES, P]) for i in range(2)]
        n_earlier = sb("n_earlier", [P, TILES])
        first = sb("first", [P, TILES])
        row = sb("row", [P, TILES])
        dummy = sb("dummy", [P, TILES])
        lane_dummy = sb("lane_dummy", [P, TILES])
        members = sb("members", [P, COLS])
        pairs = sb("pairs", [P, COLS, 2])
        names = ("dst", "src", "light")
        counts = {n: [ctx.enter_context(nc.psum_tensor(f"{n}_count{h}", [P, 512], F32)) for h in range(2)] for n in names}
        iotas_ready, hots_ready, hots_used = sem("iotas_ready"), sem("hots_ready"), sem("hots_used")
        light_hot, light_used, counted = sem("light_hot"), sem("light_used"), sem("counted")
        part_step = sem("part_step")
        rows_in = [sem("rows_in0"), sem("rows_in1")]
        rows_used = sem("rows_used")
        same_out = [sem("same_out0"), sem("same_out1")]
        dve_step, earlier_ready, earlier_used, degree_ready, root_ready = sem("dve_step"), sem("earlier_ready"), sem("earlier_used"), sem("degree_ready"), sem("root_ready")
        scalars_ready, scalars_out = sem("scalars_ready"), sem("scalars_out")
        dst_rows = net.dst_padded.rearrange("(i u) k -> i u k", u=LANES)
        same_dst = net.same_dst.rearrange("(i u) p k -> i p u k", u=LANES)

        with nc.Block() as block:
            @block.gpsimd
            def _(pool):
                nc.gpsimd.iota(iota_col[:, :], pattern=[[1, COLS]], base=0, channel_multiplier=0,
                               allow_small_or_imprecise_dtypes=True).then_inc(iotas_ready, 1)
                nc.gpsimd.iota(iota_part[:, :], pattern=[[1, P]], base=0, channel_multiplier=0,
                               allow_small_or_imprecise_dtypes=True).then_inc(iotas_ready, 1)
                nc.gpsimd.memset(nothing[:, :], 0.0).then_inc(iotas_ready, 1)
                nc.gpsimd.memset(one[:, :], 1.0).then_inc(iotas_ready, 1)
                nc.gpsimd.iota(dummy[:, :], pattern=[[0, STEPS], [P, LANES]], base=HDUMMY, channel_multiplier=1,
                               allow_small_or_imprecise_dtypes=True).then_inc(iotas_ready, 1)
                nc.gpsimd.iota(lane_dummy[:, :], pattern=[[0, WINDOWS], [P, LANES], [0, DEPTH]], base=DUMMY, channel_multiplier=1,
                               allow_small_or_imprecise_dtypes=True).then_inc(iotas_ready, 1)
                with pool.Fori(0, STEPS // 2) as i:
                    for k in range(2):
                        pool.wait_ge(rows_used, 2 * i + (k + 1))
                        pool.wait_ge(earlier_used, 2 * i)
                        nc.gpsimd.tensor_tensor(earlier[k][:, :, :], same[k][:, :, :],
                                                net.before[:, :].rearrange("p (o k) -> p o k", o=1).broadcast_to([P, LANES, P]),
                                                ALU.mult).then_inc(earlier_ready, 1)

            @block.sync
            def _(sp):
                def load_rows(i):
                    for k in range(2):
                        sp.wait_ge(rows_used, 2 * i + k - 1)
                        sp.dma_start(dst_row[k][:, :, :],
                                     dst_rows[bass.ds(2 * i + k, 1), :, :].broadcast_to([P, LANES, P])).then_inc(rows_in[k], 16)

                for k in range(2):
                    sp.dma_start(dst_row[k][:, :, :], dst_rows[k:k + 1, :, :].broadcast_to([P, LANES, P])).then_inc(rows_in[k], 16)
                x_parts, x1_parts = (t.rearrange("(s a b) f -> s a (b f)", s=X_PIECES, b=50) for t in (net.args["x"], net.x1[0:N, :]))
                with sp.Fori(1, X_PIECES + 1) as i:
                    load_rows(i)
                    sp.dma_start(chunk_of(x1_parts, i - 1), chunk_of(x_parts, i - 1)).then_inc(net.prepared, 16)
                with sp.Fori(X_PIECES + 1, STEPS // 2) as i:
                    load_rows(i)
                zero_conv(sp, net, 0, CONV_PIECES // 2)
                sp.wait_ge(net.prepared, 16 * (4 + X_PIECES + CONV_PIECES // 2))

            @block.scalar
            def _(act):
                def part_hots(i, k):
                    act.wait_ge(part_step, 4 * i)
                    for n in range(2):
                        for u in range(LANES):
                            last = nc.scalar.activation(distance[k][:, n, u, :], iota_part[:, :], ACT.Abs,
                                                        bias=minus_part[n][:, bass.ds(2 * LANES * i + (LANES * k + u), 1)])
                    last.then_inc(part_step, 1)
                    act.wait_ge(part_step, 4 * i + (2 * k + 1))
                    if k or not isinstance(i, int):
                        act.wait_ge(hots_used, 2 * LANES * i + LANES * (k - 1))
                    nc.scalar.activation(hot_part[k][:, :, :, :], distance[k][:, :, :, :], ACT.Relu, scale=-1.0, bias=one[:, :]
                                         ).then_inc(part_step, 1)

                def store_same(i, k):
                    act.wait_ge(rows_used, 2 * i + (k + 1))
                    act.dma_start(same_dst[bass.ds(2 * i + k, 1), :, :, :].rearrange("a p u k -> (a p) u k"),
                                  same[k][:, :, :]).then_inc(same_out[k], 16)

                act.wait_ge(iotas_ready, 8)
                for k in range(2):
                    part_hots(0, k)
                    store_same(0, k)
                with act.Fori(1, STEPS // 2) as i:
                    for k in range(2):
                        part_hots(i, k)
                        store_same(i, k)
                for k in range(2):
                    act.wait_ge(same_out[k], 16 * (STEPS // 2))
                act.wait_ge(degree_ready, 1)
                nc.scalar.activation(net.dinv[:, :], net.dinv[:, :], ACT.Sqrt).then_inc(root_ready, 1)
                act.wait_ge(scalars_ready, 1)
                act.dma_start(net.node_scalars.rearrange("(c p g) o -> p c (g o)", p=P, g=G),
                              pairs[:, :, :].rearrange("p (c g) o -> p c (g o)", g=G)).then_inc(scalars_out, 16)
                act.wait_ge(scalars_out, 16)

            @block.vector
            def _(dve):
                step = Chain(dve, dve_step)
                for name, table in (("src", net.src_f), ("dst", net.dst_f)):
                    step(nc.vector.tensor_copy(ints[0][:, :], table[:, :]))
                    step(nc.vector.tensor_scalar(ints[1][:, :], ints[0][:, :], 11, 4, ALU.logical_shift_right, ALU.logical_shift_left))
                    step(nc.vector.tensor_scalar(ints[2][:, :], ints[0][:, :], G - 1, None, ALU.bitwise_and))
                    step(nc.vector.tensor_tensor(col_f[name][:, :], ints[1][:, :], ints[2][:, :], ALU.add))
                    step(nc.vector.tensor_scalar(ints[1][:, :], ints[0][:, :], 4, P - 1, ALU.logical_shift_right, ALU.bitwise_and))
                    step(nc.vector.tensor_copy(part_f[name][:, :], ints[1][:, :]))
                for minus, name in zip(minus_part, ("dst", "src")):
                    nc.vector.tensor_scalar(minus[:, :], part_f[name][:, :], -1.0, None, ALU.mult).then_inc(iotas_ready, 1)
                dve.wait_ge(iotas_ready, 8)

                def one_hots(t, u):
                    for name in ("dst", "src"):
                        nc.vector.tensor_scalar(hot_col[name][u][:, :], iota_col[:, :],
                                                col_f[name][:, bass.ds(t, 1)], None, ALU.is_equal).then_inc(hots_ready, 1)

                def compare(i, k, sent):
                    dve.wait_ge(rows_in[k], 16 * i + 16)
                    dve.wait_ge(same_out[k], sent)
                    col = dst_cols[:, bass.ds(2 * i + k, 1), :].rearrange("p a u -> p (a u)")
                    nc.vector.tensor_tensor(same[k][:, :, :], dst_row[k][:, :, :],
                                            col.rearrange("p (u o) -> p u o", o=1).broadcast_to([P, LANES, P]),
                                            ALU.is_equal).then_inc(rows_used, 1)

                def sum_earlier(s, k):
                    dve.wait_ge(earlier_ready, s + 1)
                    nc.vector.tensor_reduce(earlier_cols[:, bass.ds(s, 1), :].rearrange("p a u -> p (a u)"),
                                            earlier[k][:, :, :], AX.X, ALU.add).then_inc(earlier_used, 1)

                dst_cols = net.dst_f[:, :].rearrange("p (i u) -> p i u", u=LANES)
                earlier_cols = n_earlier[:, :].rearrange("p (i u) -> p i u", u=LANES)
                compare(0, 0, 0)
                for u in range(LANES):
                    one_hots(u, u)
                with dve.Fori(0, STEPS // 2 - 1) as i:
                    for k in range(2):
                        compare(i + k, 1 - k, 16 * (i + k))
                        for u in range(LANES):
                            dve.wait_ge(hots_used, 2 * LANES * i + (LANES * k + u + 1))
                            one_hots(2 * LANES * i + (LANES * (k + 1) + u), u)
                        sum_earlier(2 * i + k, k)
                compare(STEPS // 2 - 1, 1, 16 * (STEPS // 2 - 1))
                for u in range(LANES):
                    dve.wait_ge(hots_used, TILES - 2 * LANES + u + 1)
                    one_hots(TILES - LANES + u, u)
                for k in range(2):
                    sum_earlier(STEPS - 2 + k, k)
                dve.wait_ge(earlier_used, STEPS)
                dve.wait_ge(hots_used, TILES)
                n_light = dve.value_load(net.bounds[0:1, 0:1], min_val=1, max_val=STEPS)
                with dve.Fori(0, n_light * LANES) as i:
                    dve.wait_ge(light_used, i)
                    nc.vector.tensor_scalar(hot_col["src"][0][:, :], iota_col[:, :],
                                            col_f["src"][:, bass.ds(i, 1)], None, ALU.is_equal).then_inc(light_hot, 1)
                    nc.vector.tensor_scalar(light_part[:, :], iota_part[:, :],
                                            part_f["src"][:, bass.ds(i, 1)], net.light[:, bass.ds(i, 1)],
                                            ALU.is_equal, ALU.mult).then_inc(light_hot, 1)
                step(nc.vector.tensor_scalar(first[:, :], n_earlier[:, :], 0.0, None, ALU.is_equal))
                step(nc.vector.tensor_tensor(row[:, :], net.dst_f[:, :], lane_dummy[:, :], ALU.subtract))
                step(nc.vector.tensor_tensor(row[:, :], row[:, :], first[:, :], ALU.mult))
                step(nc.vector.tensor_tensor(net.dst_idx[:, :], row[:, :], lane_dummy[:, :], ALU.add))
                step(nc.vector.tensor_tensor(row[:, :], net.dst_f[:, :], dummy[:, :], ALU.subtract))
                step(nc.vector.tensor_tensor(row[:, :], row[:, :], first[:, :], ALU.mult))
                step(nc.vector.tensor_tensor(row[:, :], row[:, :], net.light[:, :], ALU.mult))
                step(nc.vector.tensor_tensor(net.light_idx[:, :], row[:, :], dummy[:, :], ALU.add))
                dve.wait_ge(counted, 1)
                far, inverse = pairs[:, :, 0], pairs[:, :, 1]
                for h in range(2):
                    part = slice(h * half, (h + 1) * half)
                    step(nc.vector.tensor_scalar(net.dinv[:, part], counts["dst"][h][:, 0:half], 1.0, None, ALU.add))
                    step(nc.vector.tensor_copy(members[:, part], counts["src"][h][:, 0:half]))
                    step(nc.vector.tensor_tensor(far[:, part], members[:, part], counts["light"][h][:, 0:half], ALU.subtract))
                dve.engine_nop().then_inc(degree_ready, 1)
                step(nc.vector.tensor_scalar(members[:, :], members[:, :], 1.0, None, ALU.max))
                step(nc.vector.reciprocal(inverse, members[:, :]))
                nc.vector.tensor_tensor(net.far_share[:, :], far, inverse, ALU.mult).then_inc(scalars_ready, 1)
                dve.wait_ge(root_ready, 1)
                step(nc.vector.reciprocal(net.dinv[:, :], net.dinv[:, :]))

            @block.tensor
            def _(pe):
                pe.wait_ge(iotas_ready, 8)
                for n in names:
                    for h in range(2):
                        last = nc.tensor.matmul(counts[n][h][:, :], nothing[:, 0:P], nothing[:, :], start=True, stop=False)
                with pe.Fori(0, STEPS // 2) as i:
                    for k in range(2):
                        pe.wait_ge(part_step, 4 * i + (2 * k + 2))
                        for u in range(LANES):
                            pe.wait_ge(hots_ready, 4 * LANES * i + 2 * (LANES * k + u + 1))
                            for n, name in enumerate(("dst", "src")):
                                for h in range(2):
                                    last = nc.tensor.matmul(counts[name][h][:, 0:half], hot_part[k][:, n, u, :],
                                                            hot_col[name][u][:, h * half:(h + 1) * half], start=False, stop=False)
                            last.then_inc(hots_used, 1)
                n_light = pe.value_load(net.bounds[0:1, 0:1], min_val=1, max_val=STEPS)
                with pe.Fori(0, n_light * LANES) as i:
                    pe.wait_ge(light_hot, 2 * i + 2)
                    for h in range(2):
                        last = nc.tensor.matmul(counts["light"][h][:, 0:half], light_part[:, :],
                                                hot_col["src"][0][:, h * half:(h + 1) * half], start=False, stop=False)
                    last.then_inc(light_used, 1)
                for n in names:
                    for h in range(2):
                        last = nc.tensor.matmul(counts[n][h][:, :], nothing[:, 0:P], nothing[:, :], start=False, stop=True)
                last.then_inc(counted, 1)


def nodes_to_hyperedges(net, stage, sems):
    nc = net.nc
    table = (net.hyper1, net.hyper2)[stage]
    source = net.x1 if stage == 0 else net.conv
    with ExitStack() as ctx:
        def sb(name, shape, dt=F32):
            return ctx.enter_context(nc.sbuf_tensor(f"h{stage}_{name}", shape, dt))

        src_i, to_i = sb("src_i", [P, LANES], I32), sb("to_i", [P, LANES], I32)
        got, work, scal = sb("got", [P, LANES, F]), sb("work", [P, LANES, F]), sb("scal", [P, LANES, 2])
        mean, scale = sb("mean", [P, LANES]), sb("scale", [P, LANES])
        msg, summed = sb("msg", [P, LANES, HW]), sb("summed", [P, LANES, HW])
        same = sb("same", [P, LANES, P])
        sums = ctx.enter_context(nc.psum_tensor(f"h{stage}_sums", [P, 512], F32))
        idx_ready, gathered, same_in, act_in, act_out, msg_ready, sums_ready, summed_ready, added = (sems[n][0] for n in
            ("h_idx_ready", "h_gathered", "h_same_in", "h_act_in", "h_act_out", "h_msg_ready", "h_sums_ready", "h_summed_ready", "h_added"))
        dve_step, scal_in = sems["h_dve_step"][stage], sems["h_scal_in"][0]
        n_steps = (6, 4)[stage]

        def light_rounds(engine):
            n = engine.value_load(net.bounds[0:1, 0:1], min_val=1, max_val=STEPS)
            return engine.Fori(0, n), n if stage else 0

        def tiles_of(table, i):
            return table[:, bass.ds(i * LANES, LANES)]

        def over_features(t, width=F):
            return t.rearrange("p (u o) -> p u o", o=1).broadcast_to([P, LANES, width])

        def over_tiles(t):
            return t.rearrange("p (o f) -> p o f", o=1).broadcast_to([P, LANES, F])

        with nc.Block() as block:
            @block.sync
            def _(sp):
                if stage == 0:
                    zero_conv(sp, net, CONV_PIECES // 2, CONV_PIECES)
                tiles = net.same_dst.rearrange("(i u) p k -> i p u k", u=LANES)
                loop, first = light_rounds(sp)
                with loop as i:
                    r = i + first
                    sp.wait_ge(sums_ready, r)
                    sp.dma_start(same[:, :, :], tiles[bass.ds(i, 1), :, :, :].rearrange("a p u k -> (a p) u k")).then_inc(same_in, 16)
                if stage == 0:
                    sp.wait_ge(net.prepared, 16 * (4 + X_PIECES + CONV_PIECES))

            @block.gpsimd
            def _(pool):
                loop, first = light_rounds(pool)
                one_by_one = pool.value_load(net.bounds[0:1, 1:2], min_val=0, max_val=1)
                with loop as i:
                    r = i + first
                    wait_alone(pool, idx_ready, 2 * r + 2, net)
                    for u in range(LANES):
                        at = bass.IndirectOffsetOnAxis(ap=src_i[:, u:u + 1], axis=0)
                        pool.indirect_dma_start(out=got[:, u, :], out_offset=None, in_=source[:, :], in_offset=at).then_inc(gathered, 16)
                        if stage == 1:
                            pool.indirect_dma_start(out=scal[:, u, :], out_offset=None, in_=net.node_scalars[:, :],
                                                    in_offset=at).then_inc(scal_in, 16)
                    wait_alone(pool, summed_ready, r + 1, net)
                    order = [*range(0, LANES, 2), *range(1, LANES, 2)]
                    for n, u in enumerate(order):
                        if u == 1:
                            wait_alone(pool, added, 16 * LANES * r + 16 * n, net)
                        elif n > 0:
                            wait_alone(pool, added, 16 * LANES * r + one_by_one * (16 * n), net)
                        pool.indirect_dma_start(out=table[:, :], out_offset=bass.IndirectOffsetOnAxis(ap=to_i[:, u:u + 1], axis=0),
                                                in_=summed[:, u, :], in_offset=None, compute_op=ALU.add).then_inc(added, 16)
                    wait_alone(pool, added, 16 * LANES * (r + 1), net)

            @block.vector
            def _(dve):
                loop, first = light_rounds(dve)
                with loop as i:
                    r = i + first
                    step = Chain(dve, dve_step, i * n_steps)
                    wait_alone(dve, added, 16 * LANES * r, net)
                    nc.vector.tensor_copy(src_i[:, :], tiles_of(net.src_idx, i)).then_inc(idx_ready, 1)
                    nc.vector.tensor_copy(to_i[:, :], tiles_of(net.light_idx, i)).then_inc(idx_ready, 1)
                    light = tiles_of(net.light, i)
                    dve.wait_ge(gathered, 16 * LANES * r + 16 * LANES)
                    if stage == 0:
                        step(nc.vector.tensor_reduce(mean[:, :], got[:, :, :], AX.X, ALU.add))
                        step(nc.vector.tensor_scalar(mean[:, :], mean[:, :], 1.0 / F, None, ALU.mult))
                        step(nc.vector.tensor_tensor(got[:, :, :], got[:, :, :], over_features(mean[:, :]), ALU.subtract))
                        step(nc.vector.tensor_tensor(work[:, :, :], got[:, :, :], got[:, :, :], ALU.mult))
                        nc.vector.tensor_reduce(scale[:, :], work[:, :, :], AX.X, ALU.add).then_inc(act_in, 1)
                        dve.wait_ge(act_out, 2 * r + 1)
                        step(nc.vector.reciprocal(scale[:, :], scale[:, :]))
                        step(nc.vector.tensor_tensor(scale[:, :], scale[:, :], light, ALU.mult))
                        nc.vector.tensor_tensor(work[:, :, :], got[:, :, :], over_features(scale[:, :]), ALU.mult).then_inc(act_in, 1)
                    else:
                        dve.wait_ge(scal_in, 16 * LANES * i + 16 * LANES)
                        step(nc.vector.tensor_tensor(work[:, :, :], over_tiles(net.e1_last[:, :]), scal[:, :, 0:1].broadcast_to([P, LANES, F]), ALU.mult))
                        step(nc.vector.tensor_tensor(got[:, :, :], got[:, :, :], work[:, :, :], ALU.add))
                        step(nc.vector.tensor_tensor(got[:, :, :], got[:, :, :], scal[:, :, 1:2].broadcast_to([P, LANES, F]), ALU.mult))
                        step(nc.vector.tensor_tensor(got[:, :, :], got[:, :, :], over_tiles(net.conv_b[0][:, :]), ALU.add))
                        nc.vector.tensor_tensor(work[:, :, :], got[:, :, :], over_features(light), ALU.mult).then_inc(act_in, 2)
                    assert step.n == n_steps
                    nc.vector.tensor_copy(msg[:, :, F:HW], light.rearrange("p (u o) -> p u o", o=1)).then_inc(msg_ready, 1)
                    dve.wait_ge(sums_ready, r + 1)
                    nc.vector.tensor_copy(summed[:, :, :].rearrange("p u f -> p (u f)"), sums[:, 0:LANES * HW]).then_inc(summed_ready, 1)

            @block.scalar
            def _(act):
                loop, first = light_rounds(act)
                with loop as i:
                    r = i + first
                    if stage == 0:
                        act.wait_ge(act_in, 2 * r + 1)
                        nc.scalar.activation(scale[:, :], scale[:, :], ACT.Sqrt, bias=net.eps[:, :], scale=1.0 / F).then_inc(act_out, 1)
                    act.wait_ge(act_in, 2 * r + 2)
                    nc.scalar.activation(msg[:, :, 0:F], work[:, :, :], ACT.Relu).then_inc(act_out, 1 + (stage == 1))

            @block.tensor
            def _(pe):
                loop, first = light_rounds(pe)
                with loop as i:
                    r = i + first
                    pe.wait_ge(msg_ready, r + 1)
                    pe.wait_ge(act_out, 2 * r + 2)
                    pe.wait_ge(same_in, 16 * r + 16)
                    for u in range(LANES):
                        last = nc.tensor.matmul(sums[:, u * HW:(u + 1) * HW], same[:, u, :], msg[:, u, :], start=True, stop=True)
                    last.then_inc(sums_ready, 1)


def hyperedges_to_nodes(net, stage, sems):
    nc = net.nc
    table = (net.hyper1, net.hyper2)[stage]
    target = (net.conv, net.x1)[stage]
    last_row = (net.e1_last, net.e2_last)[stage]
    with ExitStack() as ctx:
        def sb(name, shape, dt=F32):
            return ctx.enter_context(nc.sbuf_tensor(f"n{stage}_{name}", shape, dt))

        from_i, src_i, to_i = (sb(n, [P, LANES], I32) for n in ("from_i", "src_i", "to_i"))
        src_row = sb("src_row", [P, LANES, P], I32)
        got, last_got, scal = sb("got", [P, LANES, HW]), sb("last_got", [P, HW]), sb("scal", [P, LANES, 2])
        inverse, mean, mean_t, summed = sb("inverse", [P, LANES]), sb("mean", [P, LANES, F]), sb("mean_t", [F, LANES * P]), sb("summed", [P, LANES * F])
        same, earlier = sb("same", [P, LANES, P]), sb("earlier", [P, LANES, P])
        n_earlier, row, dummy = sb("n_earlier", [P, LANES]), sb("row", [P, LANES]), sb("dummy", [P, 1])
        turned = ctx.enter_context(nc.psum_tensor(f"n{stage}_turned", [P, 1024], F32))
        product = ctx.enter_context(nc.psum_tensor(f"n{stage}_product", [P, 512], F32))
        last_in, idx_ready, to_ready, gathered, row_in, row_used = (sems[n][0] for n in
            ("n_last_in", "n_idx_ready", "n_to_ready", "n_gathered", "n_row_in", "n_row_used"))
        mean_ready, turned_ready, mean_t_ready, product_ready, summed_ready, added, scal_in = (sems[n][0] for n in
            ("n_mean_ready", "n_turned_ready", "n_mean_t_ready", "n_product_ready", "n_summed_ready", "n_added", "n_scal_in"))
        dve_step = sems["n_dve_step"][stage]
        before_loop = 4
        n_steps = (8, 9)[stage]

        def light_rounds(engine):
            n = engine.value_load(net.bounds[0:1, 0:1], min_val=1, max_val=STEPS)
            return engine.Fori(0, n), n if stage else 0

        def tiles_of(table, i):
            return table[:, bass.ds(i * LANES, LANES)]

        def over(t, width):
            return t.rearrange("p (u o) -> p u o", o=1).broadcast_to([P, LANES, width])

        with nc.Block() as block:
            @block.sync
            def _(sp):
                sp.dma_start(last_got[:, :], table[HYPER - 1:HYPER, :].broadcast_to([P, HW])).then_inc(last_in, 16)
                loop, first = light_rounds(sp)
                with loop as i:
                    r = i + first
                    sp.wait_ge(row_used, r)
                    sp.dma_start(src_row[:, :, :].rearrange("p u k -> p (u k)"),
                                 net.src_padded.rearrange("(s u) k -> s (u k)", u=LANES)[bass.ds(i, 1), :]
                                 .broadcast_to([P, LANES * P])).then_inc(row_in, 16)

            @block.gpsimd
            def _(pool):
                loop, first = light_rounds(pool)
                with loop as i:
                    r = i + first
                    wait_alone(pool, idx_ready, 2 * r + 2, net)
                    for u in range(LANES):
                        pool.indirect_dma_start(out=got[:, u, :], out_offset=None, in_=table[:, :],
                                                in_offset=bass.IndirectOffsetOnAxis(ap=from_i[:, u:u + 1], axis=0)).then_inc(gathered, 16)
                        if stage == 1:
                            pool.indirect_dma_start(out=scal[:, u, :], out_offset=None, in_=net.node_scalars[:, :],
                                                    in_offset=bass.IndirectOffsetOnAxis(ap=src_i[:, u:u + 1], axis=0)).then_inc(scal_in, 16)
                    pool.wait_ge(to_ready, r + 1)
                    wait_alone(pool, summed_ready, r + 1, net)
                    for u in range(LANES):
                        pool.indirect_dma_start(out=target[:, :], out_offset=bass.IndirectOffsetOnAxis(ap=to_i[:, u:u + 1], axis=0),
                                                in_=summed[:, u * F:(u + 1) * F], in_offset=None, compute_op=ALU.add).then_inc(added, 16)
                        wait_alone(pool, added, 16 * LANES * r + 16 * (u + 1), net)

            @block.vector
            def _(dve):
                step = Chain(dve, dve_step)
                step(nc.vector.tensor_scalar(dummy[:, :], net.part[:, :], float(DUMMY), None, ALU.add))
                dve.wait_ge(last_in, 16 * stage + 16)
                step(nc.vector.tensor_scalar(inverse[:, 0:1], last_got[:, F:HW], 1.0, None, ALU.max))
                step(nc.vector.reciprocal(inverse[:, 0:1], inverse[:, 0:1]))
                nc.vector.tensor_scalar(mean[:, 0, :], last_got[:, 0:F], inverse[:, 0:1], None, ALU.mult).then_inc(mean_ready, 1)
                loop, first = light_rounds(dve)
                dve.wait_ge(turned_ready, first + (stage + 1))
                nc.vector.tensor_copy(mean_t[:, 0:P], turned[0:F, 0:P]).then_inc(mean_t_ready, 1)
                dve.wait_ge(product_ready, first + (stage + 1))
                step(nc.vector.tensor_copy(last_row[:, :], product[:, 0:F]))
                assert step.n == before_loop
                with loop as i:
                    r = i + first
                    step = Chain(dve, dve_step, i * n_steps + before_loop)
                    wait_alone(dve, added, 16 * LANES * r, net)
                    nc.vector.tensor_copy(from_i[:, :], tiles_of(net.clip_idx, i)).then_inc(idx_ready, 1)
                    nc.vector.tensor_copy(src_i[:, :], tiles_of(net.src_idx, i)).then_inc(idx_ready, 1)
                    src = tiles_of(net.src_f, i)
                    dve.wait_ge(row_in, 16 * r + 16)
                    nc.vector.tensor_tensor(same[:, :, :], src_row[:, :, :], over(src, P), ALU.is_equal).then_inc(row_used, 1)
                    dve.wait_ge(row_used, r + 1)
                    step(nc.vector.tensor_tensor(earlier[:, :, :], same[:, :, :],
                                                 net.before[:, :].rearrange("p (o k) -> p o k", o=1).broadcast_to([P, LANES, P]), ALU.mult))
                    step(nc.vector.tensor_reduce(n_earlier[:, :], earlier[:, :, :], AX.X, ALU.add))
                    step(nc.vector.tensor_scalar(n_earlier[:, :], n_earlier[:, :], 0.0, None, ALU.is_equal))
                    step(nc.vector.tensor_scalar(row[:, :], src, dummy[:, :], None, ALU.subtract))
                    step(nc.vector.tensor_tensor(row[:, :], row[:, :], n_earlier[:, :], ALU.mult))
                    nc.vector.tensor_scalar(to_i[:, :], row[:, :], dummy[:, :], None, ALU.add).then_inc(to_ready, 1)
                    dve.wait_ge(gathered, 16 * LANES * r + 16 * LANES)
                    step(nc.vector.tensor_scalar(inverse[:, :], got[:, :, F:HW].rearrange("p u o -> p (u o)"), 1.0, None, ALU.max))
                    step(nc.vector.reciprocal(inverse[:, :], inverse[:, :]))
                    if stage == 1:
                        dve.wait_ge(scal_in, 16 * LANES * i + 16 * LANES)
                        step(nc.vector.tensor_tensor(inverse[:, :], inverse[:, :], scal[:, :, 1:2].rearrange("p u o -> p (u o)"), ALU.mult))
                    step(nc.vector.tensor_tensor(inverse[:, :], inverse[:, :], tiles_of(net.light, i), ALU.mult))
                    nc.vector.tensor_tensor(mean[:, :, :], got[:, :, 0:F], over(inverse[:, :], F), ALU.mult).then_inc(mean_ready, 1)
                    assert step.n == n_steps
                    dve.wait_ge(turned_ready, r + (stage + 2))
                    nc.vector.tensor_copy(mean_t[:, :], turned[0:F, 0:LANES * P]).then_inc(mean_t_ready, 1)
                    dve.wait_ge(product_ready, r + (stage + 2))
                    nc.vector.tensor_copy(summed[:, :], product[:, 0:LANES * F]).then_inc(summed_ready, 1)

            @block.tensor
            def _(pe):
                def through_w(n, tiles, to_sum):
                    pe.wait_ge(mean_ready, n)
                    for u in range(tiles):
                        last = nc.tensor.matmul(turned[0:F, u * P:(u + 1) * P], mean[:, u, :], to_sum(u), start=True, stop=True)
                    last.then_inc(turned_ready, 1)
                    pe.wait_ge(mean_t_ready, n)
                    for u in range(tiles):
                        last = nc.tensor.matmul(product[:, u * F:(u + 1) * F], mean_t[:, u * P:(u + 1) * P],
                                                net.conv_w[stage][:, :], start=True, stop=True)
                    last.then_inc(product_ready, 1)

                loop, first = light_rounds(pe)
                through_w(first + (stage + 1), 1, lambda u: net.ident[:, :])
                with loop as i:
                    r = i + first
                    through_w(r + (stage + 2), LANES, lambda u: same[:, u, :])


def chunk_ticks(engine, *stages, peeled=1, spills=True, kept=KEPT):
    last_lag = max(lag for _, lag in stages)
    turn = kept // SLOTS if spills else NC // SLOTS

    def ticks(i, at, k_range=range(SLOTS)):
        for k in k_range:
            for step, lag in stages:
                n = SLOTS * at + k - lag
                if 0 <= n < NC:
                    step(SLOTS * i + (k - lag), n % SLOTS, i + (n // SLOTS - at), n < kept)

    for i in range(peeled):
        ticks(i, i)
    with engine.Fori(peeled, turn) as i:
        ticks(i, turn - 1)
    if spills:
        for i in range(turn, turn + peeled):
            ticks(i, i)
        with engine.Fori(turn + peeled, NC // SLOTS) as i:
            ticks(i, turn + peeled)
    ticks(NC // SLOTS, NC // SLOTS, range(1 + last_lag))


def wait_chunks(engine, sem, before, chunks):
    if not isinstance(chunks, int) or chunks > 0:
        engine.wait_ge(sem, chunks + before)


def slot_rounds(k):
    return NC // SLOTS + (k < NC % SLOTS)


def norm_nodes(net):
    nc = net.nc
    with ExitStack() as ctx:
        def sb(name, shape, dt=F32):
            return ctx.enter_context(nc.sbuf_tensor(f"ln_{name}", shape, dt))

        def sem(name):
            return ctx.enter_context(nc.semaphore(f"ln_{name}"))

        far_share = [sb(f"far_share{k}", [P, G + 1]) for k in range(2)]
        shares = [sb(f"shares{k}", [G + 1, P]) for k in range(2)]
        to_rows = sb("to_rows", [G + 1, G, F])
        b2_row = sb("b2_row", [G + 1, F])
        xt, dev, h = ([sb(f"{n}{k}", [P, G, F]) for k in range(SLOTS)] for n in ("xt", "dev", "h"))
        sq = [sb(f"sq{k}", [P, G, F]) for k in range(2)]
        mean, var, scale = ([sb(f"{n}{k}", [P, G]) for k in range(SLOTS)] for n in ("mean", "var", "scale"))
        shares_ps = [ctx.enter_context(nc.psum_tensor(f"ln_shares_ps{k}", [P, 512], F32)) for k in range(2)]
        far_ps = [ctx.enter_context(nc.psum_tensor(f"ln_far_ps{k}", [P, G * F], F32)) for k in range(2)]
        ones_ready, share_ready, share_turned, shares_ready, far_ready, x_ready = (
            sem(n) for n in ("ones_ready", "share_ready", "share_turned", "shares_ready", "far_ready", "x_ready"))
        mean_ready, dev_ready, sq_ready, var_ready, root_ready, scale_ready, scaled_ready, h_ready = (
            sem(n) for n in ("mean_ready", "dev_ready", "sq_ready", "var_ready", "root_ready", "scale_ready", "scaled_ready", "h_ready"))
        dve_step, scale_step = sem("dve_step"), sem("scale_step")
        loaded, x_stored, y_stored = ([sem(f"{n}{k}") for k in range(SLOTS)] for n in ("loaded", "x_stored", "y_stored"))
        x1, y = node_chunks(net.x1), node_chunks(net.y)
        constants = 3

        def over_features(t):
            return t.rearrange("p (g o) -> p g o", o=1).broadcast_to([t.shape[0], G, F])

        def over_nodes(t):
            return t.rearrange("p (o f) -> p o f", o=1).broadcast_to([t.shape[0], G, F])

        def flat(t):
            return t[:, :, :].rearrange("p g f -> p (g f)")

        def ticks(engine, *stages):
            chunk_ticks(engine, *stages, peeled=2, spills=False)

        with nc.Block() as block:
            @block.sync
            def _(sp):
                def load(c, k, i, kept):
                    sp.wait_ge(x_stored[k], 16 * i)
                    wait_chunks(sp, dev_ready, 0, c - (SLOTS - 1))
                    sp.dma_start(flat(xt[k]), chunk_of(x1, c)).then_inc(loaded[k], 16)

                def store(c, k, i, kept):
                    sp.wait_ge(x_ready, c + 1)
                    sp.dma_start(chunk_of(x1, c), flat(xt[k])).then_inc(x_stored[k], 16)

                ticks(sp, (store, 3), (load, 0))
                for k in range(SLOTS):
                    sp.wait_ge(x_stored[k], 16 * slot_rounds(k))

            @block.gpsimd
            def _(pool):
                for k in range(2):
                    nc.gpsimd.memset(far_share[k][:, :], 1.0).then_inc(ones_ready, 1)

                def deviation(c, k, i, kept):
                    pool.wait_ge(mean_ready, c + 1)
                    wait_chunks(pool, h_ready, 0, c - (SLOTS - 1))
                    nc.gpsimd.tensor_tensor(dev[k][:, :, :], xt[k][:, :, :], over_features(mean[k][:, :]), ALU.subtract).then_inc(dev_ready, 1)

                def multiply(c, k, i, kept):
                    pool.wait_ge(scale_ready, c + 1)
                    nc.gpsimd.tensor_tensor(dev[k][:, :, :], dev[k][:, :, :], over_features(scale[k][:, :]), ALU.mult).then_inc(scaled_ready, 1)

                ticks(pool, (deviation, 3), (multiply, 5))

            @block.vector
            def _(dve):
                step = Chain(dve, dve_step)
                rows = slice(0, G + 1)
                step(nc.vector.tensor_tensor(to_rows[:, :, :], over_nodes(net.e2_last[rows, :]), over_features(net.ident[rows, 0:G]), ALU.mult))
                step(nc.vector.tensor_scalar(b2_row[:, :], net.conv_b[1][rows, :], net.ident[rows, G:G + 1], None, ALU.mult))
                step(nc.vector.tensor_tensor(to_rows[:, :, :], to_rows[:, :, :], over_nodes(b2_row[:, :]), ALU.add))
                assert step.n == constants

                def add(c, k, i, kept):
                    step = Chain(dve, dve_step, c + constants)
                    dve.wait_ge(far_ready, c + 1)
                    dve.wait_ge(loaded[k], 16 * i + 16)
                    nc.vector.tensor_tensor(flat(xt[k]), flat(xt[k]), far_ps[k % 2][:, :], ALU.add).then_inc(x_ready, 1)
                    dve.wait_ge(x_ready, c + 1)
                    step(nc.vector.tensor_reduce(mean[k][:, :], xt[k][:, :, :], AX.X, ALU.add))
                    nc.vector.tensor_scalar(mean[k][:, :], mean[k][:, :], 1.0 / F, None, ALU.mult).then_inc(mean_ready, 1)

                def variance(c, k, i, kept):
                    dve.wait_ge(sq_ready, c + 1)
                    nc.vector.tensor_reduce(var[k][:, :], sq[k % 2][:, :, :], AX.X, ALU.add).then_inc(var_ready, 1)

                def scales(c, k, i, kept):
                    step = Chain(dve, scale_step, c)
                    dve.wait_ge(root_ready, c + 1)
                    step(nc.vector.reciprocal(scale[k][:, :], scale[k][:, :]))
                    nc.vector.tensor_tensor(scale[k][:, :], scale[k][:, :], net.dinv[:, bass.ds(c * G, G)], ALU.mult).then_inc(scale_ready, 1)

                ticks(dve, (scales, 5), (variance, 4), (add, 2))

            @block.tensor
            def _(pe):
                def turn(c, k, i, kept):
                    pe.wait_ge(share_ready, c + 1)
                    wait_chunks(pe, shares_ready, 0, c - 1)
                    nc.tensor.transpose(shares_ps[k % 2][0:G + 1, 0:P], far_share[k % 2][:, :], net.ident[:, :]).then_inc(share_turned, 1)

                def far_rows(c, k, i, kept):
                    pe.wait_ge(shares_ready, c + 1)
                    wait_chunks(pe, x_ready, 0, c - 1)
                    for half in range(2):
                        part = slice(half * 512, (half + 1) * 512)
                        last = nc.tensor.matmul(far_ps[k % 2][:, part], shares[k % 2][:, :],
                                                flat(to_rows)[:, part], start=True, stop=True)
                    last.then_inc(far_ready, 1)

                pe.wait_ge(dve_step, constants)
                ticks(pe, (turn, 0), (far_rows, 1))

            @block.scalar
            def _(act):
                def take_share(c, k, i, kept):
                    wait_chunks(act, share_turned, 0, c - 1)
                    nc.scalar.activation(far_share[k % 2][:, 0:G], net.far_share[:, bass.ds(c * G, G)], ACT.Copy).then_inc(share_ready, 1)

                def take_turned(c, k, i, kept):
                    act.wait_ge(share_turned, c + 1)
                    wait_chunks(act, far_ready, 0, c - 1)
                    nc.scalar.activation(shares[k % 2][:, :], shares_ps[k % 2][0:G + 1, 0:P], ACT.Copy).then_inc(shares_ready, 1)

                def square(c, k, i, kept):
                    act.wait_ge(dev_ready, c + 1)
                    wait_chunks(act, var_ready, 0, c - 1)
                    nc.scalar.activation(sq[k % 2][:, :, :], dev[k][:, :, :], ACT.Square).then_inc(sq_ready, 1)

                def root(c, k, i, kept):
                    act.wait_ge(var_ready, c + 1)
                    nc.scalar.activation(scale[k][:, :], var[k][:, :], ACT.Sqrt, bias=net.eps[:, :], scale=1.0 / F).then_inc(root_ready, 1)

                def relu(c, k, i, kept):
                    act.wait_ge(scaled_ready, c + 1)
                    act.wait_ge(y_stored[k], 16 * i)
                    nc.scalar.activation(h[k][:, :, :], dev[k][:, :, :], ACT.Relu).then_inc(h_ready, 1)
                    act.wait_ge(h_ready, c + 1)
                    act.dma_start(chunk_of(y, c), flat(h[k])).then_inc(y_stored[k], 16)

                act.wait_ge(ones_ready, 2)
                ticks(act, (take_share, 0), (take_turned, 1), (relu, 6), (root, 4), (square, 3))
                for k in range(SLOTS):
                    act.wait_ge(y_stored[k], 16 * slot_rounds(k))


def gather_edges(net, layer, sems):
    nc = net.nc
    with ExitStack() as ctx:
        def sb(name, shape, dt=F32):
            return ctx.enter_context(nc.sbuf_tensor(f"e{layer}_{name}", shape, dt))

        src_i = [sb(f"src_i{b}", [P, LANES], I32) for b in range(SLOTS)]
        same = [sb(f"same{b}", [P, LANES, P]) for b in range(SLOTS)]
        got = [sb(f"got{b}", [P, LANES, F]) for b in range(SLOTS)]
        summed = [sb(f"summed{b}", [P, LANES * F]) for b in range(SLOTS)]
        sums = [ctx.enter_context(nc.psum_tensor(f"e{layer}_sums{b}", [P, 512], F32)) for b in range(SLOTS)]
        src_ready, sums_ready, summed_ready, v_copied = (sems[n][0] for n in
            ("src_ready", "sums_ready", "summed_ready", "v_copied"))
        same_in, gathered, summed_out = sems["same_in"], sems["gathered"], sems["summed_out"]
        steps, rounds = layer * STEPS, layer * ROUNDS
        src_cols = net.src_idx[:, :].rearrange("p (m u q) -> p m u q", u=LANES, q=DEPTH)
        same_dst = net.same_dst.rearrange("(m u q) p k -> m q p u k", u=LANES, q=DEPTH)

        with nc.Block() as block:
            @block.sync
            def _(sp):
                v_parts, y_parts = (t.rearrange("(s a b) f -> s a (b f)", s=STEPS, a=64) for t in (net.v[0:NP, :], net.y))

                def load(i, b):
                    sp.dma_start(same[b][:, :, :], same_dst[bass.ds(window_of(i, b), 1), b % DEPTH, :, :, :].rearrange("a p u k -> (a p) u k")
                                 ).then_inc(same_in[b], 16)
                    s = i * SLOTS + b
                    sp.dma_start(chunk_of(v_parts, s), chunk_of(y_parts, s)).then_inc(v_copied, 16)

                for b in range(SLOTS):
                    load(0, b)
                with sp.Fori(1, ROUNDS) as i:
                    for b in range(SLOTS):
                        sp.wait_ge(sums_ready, i * SLOTS + (steps + b + 1 - SLOTS))
                        load(i, b)
                sp.wait_ge(v_copied, 16 * STEPS * (layer + 1))

            @block.gpsimd
            def _(pool):
                def gather(b):
                    for u in range(LANES):
                        pool.indirect_dma_start(out=got[b][:, u, :], out_offset=None, in_=net.y[:, :],
                                                in_offset=bass.IndirectOffsetOnAxis(ap=src_i[b][:, u:u + 1], axis=0)
                                                ).then_inc(gathered[b], 16)

                for b in range(SLOTS):
                    pool.wait_ge(src_ready, steps + b + 1)
                    gather(b)
                with pool.Fori(1, ROUNDS) as i:
                    for b in range(SLOTS):
                        pool.wait_ge(sums_ready, i * SLOTS + (steps + b + 1 - SLOTS))
                        wait_alone(pool, src_ready, i * SLOTS + (steps + b + 1), net)
                        gather(b)

            @block.vector
            def _(dve):
                def take_src(i, b):
                    nc.vector.tensor_copy(src_i[b][:, :], src_cols[:, bass.ds(window_of(i, b), 1), :, b % DEPTH].rearrange("p a u -> p (a u)")
                                          ).then_inc(src_ready, 1)

                def keep_sums(i, b):
                    dve.wait_ge(summed_out[b], 16 * (rounds + i))
                    dve.wait_ge(sums_ready, i * SLOTS + (steps + b + 1))
                    nc.vector.tensor_copy(summed[b][:, :], sums[b][:, 0:LANES * F]).then_inc(summed_ready, 1)

                for b in range(SLOTS):
                    take_src(0, b)
                with dve.Fori(0, ROUNDS - 1) as i:
                    for b in range(SLOTS):
                        keep_sums(i, b)
                        take_src(i + 1, b)
                for b in range(SLOTS):
                    keep_sums(ROUNDS - 1, b)

            @block.scalar
            def _(act):
                with act.Fori(0, ROUNDS) as i:
                    for b in range(SLOTS):
                        act.wait_ge(summed_ready, i * SLOTS + (steps + b + 1))
                        act.dma_start(chunk_of(net.summed, i * SLOTS + b), summed[b][:, :]).then_inc(summed_out[b], 16)
                for b in range(SLOTS):
                    act.wait_ge(summed_out[b], 16 * (rounds + ROUNDS))

            @block.tensor
            def _(pe):
                def sum_rows(b, i):
                    pe.wait_ge(same_in[b], 16 * (rounds + i) + 16)
                    pe.wait_ge(gathered[b], 16 * LANES * (rounds + i) + 16 * LANES)
                    for u in range(LANES):
                        last = nc.tensor.matmul(sums[b][:, u * F:(u + 1) * F], same[b][:, u, :], got[b][:, u, :],
                                                start=True, stop=True)
                    last.then_inc(sums_ready, 1)

                for b in range(SLOTS):
                    sum_rows(b, 0)
                with pe.Fori(1, ROUNDS) as i:
                    for b in range(SLOTS):
                        pe.wait_ge(summed_ready, i * SLOTS + (steps + b + 1 - SLOTS))
                        sum_rows(b, i)


def round_slots(q):
    return len(range(q, TURN_CHUNKS, SLOTS))


def normalise_and_gather(net, layer, sems, affine, g_kept):
    nc = net.nc
    with ExitStack() as ctx:
        def sb(name, shape, dt=F32):
            return ctx.enter_context(nc.sbuf_tensor(f"g{layer}_{name}", shape, dt))

        src_i = [sb(f"src_i{b}", [P, LANES], I32) for b in range(SLOTS)]
        same = [sb(f"same{b}", [P, LANES, P]) for b in range(SLOTS)]
        got = [sb(f"got{b}", [P, LANES, GW]) for b in range(SLOTS)]
        summed = [sb(f"summed{b}", [P, LANES, F]) for b in range(SLOTS)]
        edge_offset = sb("edge_offset", [P, LANES, F])
        g_in = [sb(f"g_in{q}", [P, G, GW]) for q in range(SLOTS)]
        v_out = [sb(f"v_out{q}", [P, G, F]) for q in range(SLOTS)]
        node_offset = [sb(f"node_offset{q}", [P, G, F]) for q in range(SLOTS)]
        sums = [ctx.enter_context(nc.psum_tensor(f"g{layer}_sums{b}", [P, 512], F32)) for b in range(SLOTS)]
        src_ready, sums_ready, summed_ready, v_ready, norm_step, offset_ready = (sems[n][0] for n in
            ("src_ready", "sums_ready", "summed_ready", "v_ready", "norm_step", "offset_ready"))
        same_in, gathered, summed_out, g_loaded, v_stored = (sems[n] for n in ("same_in", "gathered", "summed_out", "x_in", "stored"))
        steps, rounds = layer * STEPS, layer * ROUNDS
        past = layer - 1
        src_cols = net.src_idx[:, :].rearrange("p (m u q) -> p m u q", u=LANES, q=DEPTH)
        same_dst = net.same_dst.rearrange("(m u q) p k -> m q p u k", u=LANES, q=DEPTH)
        v, g = node_chunks(net.v), node_chunks(net.g)
        kept_rounds = KEPT_G // TURN_CHUNKS
        steps_of_round = 2 * SLOTS + TURN_CHUNKS
        factor_row, offset_row = affine[:, 0, :], affine[:, 1, :]

        def over(t, n):
            return t.rearrange("p (o f) -> p o f", o=1).broadcast_to([P, n, F])

        def in_turn(edge_step, chunk):
            for b in range(SLOTS):
                edge_step(b)
                for j in range(2 * b, min(2 * b + 2, TURN_CHUNKS)):
                    chunk(j)

        def wait_slot(engine, i, j):
            last = j - SLOTS if j >= SLOTS else (round_slots(j) - 1) * SLOTS + j - TURN_CHUNKS
            engine.wait_ge(v_ready, i * TURN_CHUNKS + (past * NC + last + 1))

        def by_rounds(engine, work):
            work(0, True)
            with engine.Fori(1, kept_rounds) as i:
                work(i, True)
            with engine.Fori(kept_rounds, ROUNDS - 1) as i:
                work(i, False)
            work(ROUNDS - 1, False)

        with nc.Block() as block:
            @block.sync
            def _(sp):
                def work(i, kept):
                    def edge_step(b):
                        if not isinstance(i, int) or i > 0:
                            sp.wait_ge(sums_ready, i * SLOTS + (steps + b + 1 - SLOTS))
                        sp.dma_start(same[b][:, :, :], same_dst[bass.ds(window_of(i, b), 1), b % DEPTH, :, :, :]
                                     .rearrange("a p u k -> (a p) u k")).then_inc(same_in[b], 16)

                    def chunk(j):
                        if not kept:
                            wait_slot(sp, i, j)
                            sp.dma_start(g_in[j % SLOTS][:, :, :].rearrange("p g f -> p (g f)"), chunk_of(g, i * TURN_CHUNKS + j)
                                         ).then_inc(g_loaded[j % SLOTS], 16)

                    in_turn(edge_step, chunk)

                by_rounds(sp, work)

            @block.gpsimd
            def _(pool):
                def gather(b):
                    for u in range(LANES):
                        pool.indirect_dma_start(out=got[b][:, u, :], out_offset=None, in_=net.g[:, :],
                                                in_offset=bass.IndirectOffsetOnAxis(ap=src_i[b][:, u:u + 1], axis=0)
                                                ).then_inc(gathered[b], 16)

                for b in range(SLOTS):
                    pool.wait_ge(src_ready, steps + b + 1)
                    gather(b)
                with pool.Fori(1, ROUNDS) as i:
                    for b in range(SLOTS):
                        pool.wait_ge(sums_ready, i * SLOTS + (steps + b + 1 - SLOTS))
                        wait_alone(pool, src_ready, i * SLOTS + (steps + b + 1), net)
                        gather(b)

            @block.vector
            def _(dve):
                def take_src(i, b):
                    nc.vector.tensor_copy(src_i[b][:, :], src_cols[:, bass.ds(window_of(i, b), 1), :, b % DEPTH].rearrange("p a u -> p (a u)")
                                          ).then_inc(src_ready, 1)

                def work(i, kept):
                    step = Chain(dve, norm_step, (i + past * ROUNDS) * steps_of_round)

                    def edge_step(b):
                        dve.wait_ge(summed_out[b], 16 * (rounds + i))
                        dve.wait_ge(sums_ready, i * SLOTS + (steps + b + 1))
                        got_sums = sums[b][:, 0:LANES * GW].rearrange("p (u f) -> p u f", f=GW)
                        step(nc.vector.tensor_tensor(summed[b][:, :, :], got_sums[:, :, 0:F], over(factor_row, LANES), ALU.mult))
                        step(nc.vector.tensor_tensor(edge_offset[:, :, :], over(offset_row, LANES),
                                                     got_sums[:, :, F:GW].broadcast_to([P, LANES, F]), ALU.mult))
                        nc.vector.tensor_tensor(summed[b][:, :, :], summed[b][:, :, :], edge_offset[:, :, :], ALU.add).then_inc(summed_ready, 1)
                        if not (isinstance(i, int) and i == ROUNDS - 1):
                            take_src(i + 1, b)

                    def chunk(j):
                        c, q = i * TURN_CHUNKS + j, j % SLOTS
                        if kept:
                            rows = g_kept[:, bass.ds(c, 1), :, 0:F].rearrange("p a g f -> p (a g) f")
                        else:
                            dve.wait_ge(g_loaded[q], 16 * ((i - kept_rounds) * round_slots(q) + (past * (ROUNDS - kept_rounds) * round_slots(q) + j // SLOTS + 1)))
                            rows = g_in[q][:, :, 0:F]
                        dve.wait_ge(v_stored[q], 16 * (i * round_slots(q) + (past * ROUNDS * round_slots(q) + j // SLOTS)))
                        step(nc.vector.tensor_tensor(v_out[q][:, :, :], rows, over(factor_row, G), ALU.mult))
                        dve.wait_ge(offset_ready, i * TURN_CHUNKS + (past * NC + j + 1))
                        nc.vector.tensor_tensor(v_out[q][:, :, :], v_out[q][:, :, :], node_offset[q][:, :, :], ALU.add).then_inc(v_ready, 1)

                    in_turn(edge_step, chunk)
                    assert step.n == steps_of_round

                for b in range(SLOTS):
                    take_src(0, b)
                by_rounds(dve, work)

            @block.scalar
            def _(act):
                def offsets(i, j):
                    if not isinstance(i, int) or i > 0 or j >= SLOTS:
                        wait_slot(act, i, j)
                    for s in range(G):
                        last = nc.scalar.activation(node_offset[j % SLOTS][:, s, :], offset_row, ACT.Copy,
                                                    scale=net.dinv[:, bass.ds(i * (TURN_CHUNKS * G) + (j * G + s), 1)])
                    last.then_inc(offset_ready, 1)

                def work(i, kept):
                    def edge_step(b):
                        act.wait_ge(summed_ready, i * SLOTS + (steps + b + 1))
                        act.dma_start(chunk_of(net.summed, i * SLOTS + b), summed[b][:, :, :].rearrange("p u f -> p (u f)")
                                      ).then_inc(summed_out[b], 16)

                    def chunk(j):
                        if j < TURN_CHUNKS - 1:
                            offsets(i, j + 1)
                        elif not (isinstance(i, int) and i == ROUNDS - 1):
                            offsets(i + 1, 0)
                        act.wait_ge(v_ready, i * TURN_CHUNKS + (past * NC + j + 1))
                        act.dma_start(chunk_of(v, i * TURN_CHUNKS + j), v_out[j % SLOTS][:, :, :].rearrange("p g f -> p (g f)")
                                      ).then_inc(v_stored[j % SLOTS], 16)

                    in_turn(edge_step, chunk)

                offsets(0, 0)
                by_rounds(act, work)
                for b in range(SLOTS):
                    act.wait_ge(summed_out[b], 16 * (rounds + ROUNDS))
                    act.wait_ge(v_stored[b], 16 * ROUNDS * round_slots(b) * layer)

            @block.tensor
            def _(pe):
                def sum_rows(b, i):
                    pe.wait_ge(same_in[b], 16 * (rounds + i) + 16)
                    pe.wait_ge(gathered[b], 16 * LANES * (rounds + i) + 16 * LANES)
                    for u in range(LANES):
                        last = nc.tensor.matmul(sums[b][:, u * GW:(u + 1) * GW], same[b][:, u, :], got[b][:, u, :],
                                                start=True, stop=True)
                    last.then_inc(sums_ready, 1)

                for b in range(SLOTS):
                    sum_rows(b, 0)
                with pe.Fori(1, ROUNDS) as i:
                    for b in range(SLOTS):
                        pe.wait_ge(summed_ready, i * SLOTS + (steps + b + 1 - SLOTS))
                        sum_rows(b, i)


def add_and_transform(net, layer, sems, stats, out_kept):
    nc = net.nc
    final = layer == 2
    n_kept = KEPT if final else KEPT_G
    with ExitStack() as ctx:
        def sb(name, shape, dt=F32):
            return ctx.enter_context(nc.sbuf_tensor(f"t{layer}_{name}", shape, dt))

        to_add = [sb(f"to_add{b}", [P, LANES, F]) for b in range(SLOTS)]
        dst_i = [sb(f"dst_i{b}", [P, LANES], I32) for b in range(SLOTS)]
        rows = [sb(f"rows{k}", [P, G, F]) for k in range(SLOTS)]
        turned = [sb(f"turned{k}", [P, G * F]) for k in range(2)]
        z_out = [sb(f"z_out{k}", [P, G * F]) for k in range(2)]
        t_ps = [ctx.enter_context(nc.psum_tensor(f"t{layer}_t_ps{h}", [P, 512], F32)) for h in range(2)]
        m_ps = [ctx.enter_context(nc.psum_tensor(f"t{layer}_m_ps{h}", [P, 512], F32)) for h in range(2)]
        if not final:
            b_ps = [ctx.enter_context(nc.psum_tensor(f"t{layer}_b_ps{k}", [P, G * F], F32)) for k in range(2)]
            g_out = [sb(f"g_out{k}", [P, G, GW]) for k in range(2)]
        dst_ready, scaled_ready, t_ready, turned_ready, m_ready, z_ready, counted = (sems[n][0] for n in
            ("dst_ready", "scaled_ready", "t_ready", "turned_ready", "m_ready", "z_ready", "counted"))
        back_ready, g_ready = sems["b_t_ready"][0], sems["rows_ready"][0]
        add_in, added, loaded, out_stored = sems["add_in"], sems["added"], sems["loaded"], sems["z_stored"]
        v, g = node_chunks(net.v), node_chunks(net.g)
        stored_before = [layer * (NC - NC // 2), layer * (NC // 2)]
        dst_cols = net.dst_idx[:, :].rearrange("p (m u q) -> p m u q", u=LANES, q=DEPTH)
        steps, rounds = layer * STEPS, layer * ROUNDS
        chunks, halves = layer * NC, 2 * layer * NC

        def z_half(c, k, h, kept):
            if kept and final:
                return out_kept[:, bass.ds(c * (G * F) + h * 512, 512)]
            return z_out[k % 2][:, h * 512:(h + 1) * 512]

        def g_rows(c, k, kept):
            if kept:
                return out_kept[:, bass.ds(c, 1), :, :].rearrange("p a g f -> p (a g) f")
            return g_out[k % 2][:, :, :]

        with nc.Block() as block:
            @block.sync
            def _(sp):
                def stage(i, b):
                    sp.dma_start(to_add[b][:, :, :].rearrange("p u f -> p (u f)"), chunk_of(net.summed, i * SLOTS + b)).then_inc(add_in[b], 16)

                for b in range(SLOTS):
                    stage(0, b)
                with sp.Fori(1, ROUNDS) as i:
                    for b in range(SLOTS):
                        for u in range(LANES):
                            sp.wait_ge(added[u], 16 * SLOTS * i + 16 * (steps + b + 1 - SLOTS))
                        stage(i, b)

            @block.gpsimd
            def _(pool):
                unsorted = pool.value_load(net.bounds[0:1, 1:2], min_val=0, max_val=1)

                def take_dst(i, b):
                    nc.gpsimd.tensor_copy(dst_i[b][:, :], dst_cols[:, bass.ds(window_of(i, b), 1), :, b % DEPTH].rearrange("p a u -> p (a u)")
                                          ).then_inc(dst_ready, 1)

                def add(i, b):
                    pool.wait_ge(add_in[b], 16 * (rounds + i) + 16)
                    pool.wait_ge(dst_ready, i * SLOTS + (steps + b + 1))
                    before = 16 * SLOTS * i + 16 * (steps + b)
                    for u in reversed(range(LANES)):
                        if u < LANES - 1:
                            pool.wait_ge(added[u + 1], (before + 16) * unsorted)
                        else:
                            pool.wait_ge(added[0], before * unsorted)
                        wait_alone(pool, added[u], before, net)
                        pool.indirect_dma_start(out=net.v[:, :], out_offset=bass.IndirectOffsetOnAxis(ap=dst_i[b][:, u:u + 1], axis=0),
                                                in_=to_add[b][:, u, :], in_offset=None, compute_op=ALU.add).then_inc(added[u], 16)

                with pool.Fori(0, ROUNDS) as i:
                    for b in range(SLOTS):
                        take_dst(i, b)
                        add(i, b)
                for u in range(LANES):
                    pool.wait_ge(added[u], 16 * (steps + STEPS))

            @block.vector
            def _(dve):
                def scale(c, k, i, kept):
                    dve.wait_ge(loaded[k], 16 * (i + layer * slot_rounds(k)) + 16)
                    nc.vector.tensor_tensor(rows[k][:, :, :], rows[k][:, :, :],
                                            net.dinv[:, bass.ds(c * G, G)].rearrange("p (g o) -> p g o", o=1).broadcast_to([P, G, F]),
                                            ALU.mult).then_inc(scaled_ready, 1)

                def count(c, k, i, kept):
                    for h in range(2):
                        dve.wait_ge(z_ready, 2 * c + (halves + h + 1))
                        unit = z_half(c, k, h, kept)
                        if isinstance(c, int) and c == NC - 1:
                            unit = unit.rearrange("q (j p) -> q j p", p=P)[:, :, 0:TAIL_P]
                        nc.vector.bn_stats(stats[:, bass.ds(2 * c + h, 1), :].rearrange("p a s -> p (a s)"), unit).then_inc(counted, 1)

                def back_rows(c, k, i, kept):
                    dve.wait_ge(back_ready, c + (chunks + 1))
                    if not kept:
                        dve.wait_ge(out_stored[k % 2], 16 * (2 * i + (k // 2 + stored_before[k % 2])))
                    dinv = net.dinv[:, bass.ds(c * G, G)].rearrange("p (g o) -> p g o", o=1)
                    nc.vector.tensor_tensor(g_rows(c, k, kept)[:, :, 0:F], b_ps[k % 2][:, :].rearrange("p (g f) -> p g f", g=G),
                                            dinv.broadcast_to([P, G, F]), ALU.mult)
                    nc.vector.tensor_scalar(g_rows(c, k, kept)[:, :, F:GW], dinv, 1.0, None, ALU.mult).then_inc(g_ready, 1)

                chunk_ticks(dve, (scale, 0), (count, 3), *([] if final else [(back_rows, 3)]), kept=n_kept)

            @block.tensor
            def _(pe):
                def turn(c, k, i, kept):
                    pe.wait_ge(scaled_ready, c + (chunks + 1))
                    for j in range(G // 2):
                        if j % 4 == 0:
                            wait_chunks(pe, turned_ready, halves, 2 * c + (j // 4 - 1))
                        t = nc.tensor.transpose(t_ps[j // 4][:, j % 4 * P:(j % 4 + 1) * P],
                                                rows[k][:, 2 * j:2 * j + 2, :].rearrange("p g f -> p (g f)"), net.ident[:, :])
                        if j % 4 == 3:
                            t.then_inc(t_ready, 1)

                def product(c, k, i, kept):
                    for h in range(2):
                        wait_chunks(pe, z_ready, halves, 2 * c + (h - 1))
                        pe.wait_ge(turned_ready, 2 * c + (halves + h + 1))
                        nc.tensor.matmul(m_ps[h][:, :], net.gcn_w[layer][:, :],
                                         turned[k % 2][:, h * 512:(h + 1) * 512], start=True, stop=True).then_inc(m_ready, 1)

                def back(c, k, i, kept):
                    pe.wait_ge(z_ready, 2 * c + (halves + 2))
                    wait_chunks(pe, g_ready, chunks, c - 1)
                    for j in range(G // 2):
                        t = nc.tensor.transpose(b_ps[k % 2][:, j * P:(j + 1) * P], z_out[k % 2][:, j * P:(j + 1) * P], net.ident[:, :])
                    t.then_inc(back_ready, 1)

                chunk_ticks(pe, (turn, 0), *([] if final else [(back, 2)]), (product, 1), kept=n_kept)

            @block.scalar
            def _(act):
                def load(c, k, i, kept):
                    wait_chunks(act, t_ready, halves, 2 * (c - (SLOTS - 1)))
                    n = act.value_load(net.windows[0:1, bass.ds(c, 1)], min_val=0, max_val=WINDOWS)
                    for u in range(LANES):
                        act.wait_ge(added[u], n * (16 * DEPTH) + 16 * steps)
                    act.dma_start(rows[k][:, :, :].rearrange("p g f -> p (g f)"), chunk_of(v, c)).then_inc(loaded[k], 16)

                def copy(c, k, i, kept):
                    wait_chunks(act, m_ready, halves, 2 * (c - 1))
                    for h in range(2):
                        part = slice(h * 512, (h + 1) * 512)
                        act.wait_ge(t_ready, 2 * c + (halves + h + 1))
                        nc.scalar.activation(turned[k % 2][:, part], t_ps[h][:, :], ACT.Copy).then_inc(turned_ready, 1)

                def relu(c, k, i, kept):
                    if not final:
                        wait_chunks(act, counted, halves, 2 * (c - 1))
                        wait_chunks(act, back_ready, chunks, c - 1)
                    elif not kept:
                        wait_chunks(act, counted, halves, 2 * (c - 1))
                        act.wait_ge(out_stored[k % 2], 16 * (2 * i + (k // 2 - KEPT // 2 + stored_before[k % 2])))
                    for h in range(2):
                        act.wait_ge(m_ready, 2 * c + (halves + h + 1))
                        nc.scalar.activation(z_half(c, k, h, kept), m_ps[h][:, :], ACT.Relu,
                                             bias=net.gcn_b[:, layer:layer + 1]).then_inc(z_ready, 1)
                    if final and not kept:
                        act.wait_ge(z_ready, 2 * c + (halves + 2))
                        act.dma_start(chunk_of(net.z, c), z_out[k % 2][:, :]).then_inc(out_stored[k % 2], 16)

                def store(c, k, i, kept):
                    act.wait_ge(g_ready, c + (chunks + 1))
                    act.dma_start(chunk_of(g, c), g_rows(c, k, kept).rearrange("p g f -> p (g f)")).then_inc(out_stored[k % 2], 16)

                chunk_ticks(act, (load, 0), (copy, LOAD_LEAD), (relu, LOAD_LEAD + 1), *([] if final else [(store, LOAD_LEAD + 2)]),
                            peeled=2, kept=n_kept)
                for k in range(2):
                    act.wait_ge(out_stored[k], 16 * (stored_before[k] + (SPILLED[k] if final else NC // 2 + (k < NC % 2))))


def batch_norm_factors(net, layer, sems, stats, factor, offset, affine):
    nc = net.nc
    with ExitStack() as ctx:
        def sb(name, shape, dt=F32):
            return ctx.enter_context(nc.sbuf_tensor(f"f{layer}_{name}", shape, dt))

        mv, moments, mean, var, square, root = sb("mv", [P, 2]), sb("moments", [P, 2]), sb("mean", [P, 1]), sb("var", [P, 1]), sb("square", [P, 1]), sb("root", [P, 1])
        mixed = ctx.enter_context(nc.psum_tensor(f"f{layer}_mixed", [P, 512], F32))
        moments_ready, mixed_ready, var_ready, root_ready, dve_step, diagonal_ready, affine_ready = (sems[n][0] for n in
            ("moments_ready", "mixed_ready", "var_ready", "root_ready", "factor_step", "diagonal_ready", "affine_ready"))
        final = layer == 2
        diagonal = sb("diagonal", [F, 2 * F])
        affine_ps = ctx.enter_context(nc.psum_tensor(f"f{layer}_affine_ps", [P, 512], F32))
        with nc.Block() as block:
            @block.vector
            def _(dve):
                step = Chain(dve, dve_step, layer * 9)
                step(nc.vector.bn_aggr(mv[:, :], stats[:, :, :].rearrange("p c s -> p (c s)")))
                step(nc.vector.tensor_copy(moments[:, 0:1], mv[:, 0:1]))
                nc.vector.scalar_tensor_tensor(out=moments[:, 1:2], in0=mv[:, 0:1], scalar=mv[:, 0:1], in1=mv[:, 1:2],
                                               op0=ALU.mult, op1=ALU.add).then_inc(moments_ready, 1)
                dve.wait_ge(mixed_ready, layer + 1)
                step(nc.vector.tensor_copy(mean[:, :], mixed[:, 0:1]))
                step(nc.vector.tensor_tensor(square[:, :], mean[:, :], mean[:, :], ALU.mult))
                nc.vector.tensor_tensor(var[:, :], mixed[:, 1:2], square[:, :], ALU.subtract).then_inc(var_ready, 1)
                dve.wait_ge(root_ready, layer + 1)
                step(nc.vector.reciprocal(root[:, :], root[:, :]))
                step(nc.vector.tensor_tensor(factor[:, :], root[:, :], net.gamma[:, layer:layer + 1], ALU.mult))
                step(nc.vector.tensor_tensor(offset[:, :], mean[:, :], factor[:, :], ALU.mult))
                step(nc.vector.tensor_tensor(offset[:, :], net.beta[:, layer:layer + 1], offset[:, :], ALU.subtract))
                assert step.n == 8
                if not final:
                    for n, column in enumerate((factor, offset)):
                        nc.vector.tensor_scalar(diagonal[:, n * F:(n + 1) * F], net.ident[0:F, 0:F], column[0:F, :], None, ALU.mult
                                                ).then_inc(diagonal_ready, 1)
                    dve.wait_ge(affine_ready, layer + 1)
                    step(nc.vector.tensor_copy(affine[:, :, :].rearrange("p n f -> p (n f)"), affine_ps[:, 0:2 * F]))

            @block.tensor
            def _(pe):
                pe.wait_ge(moments_ready, layer + 1)
                nc.tensor.matmul(mixed[:, 0:2], net.pair_mean[:, :], moments[:, :], start=True, stop=True).then_inc(mixed_ready, 1)
                if not final:
                    pe.wait_ge(diagonal_ready, 2 * (layer + 1))
                    nc.tensor.matmul(affine_ps[:, 0:2 * F], net.ones[:, :], diagonal[:, :], start=True, stop=True).then_inc(affine_ready, 1)

            @block.scalar
            def _(act):
                act.wait_ge(var_ready, layer + 1)
                nc.scalar.activation(root[:, :], var[:, :], ACT.Sqrt, bias=net.eps[:, :]).then_inc(root_ready, 1)


def normalise(net, layer, sems, factor, offset, out, z_kept):
    nc = net.nc
    with ExitStack() as ctx:
        def sb(name, shape, dt=F32):
            return ctx.enter_context(nc.sbuf_tensor(f"b{layer}_{name}", shape, dt))

        z_in = [sb(f"z_in{k}", [P, G * F]) for k in range(2)]
        normed = [sb(f"normed{k}", [P, G * F]) for k in range(2)]
        rows = [sb(f"rows{k}", [P, G, F]) for k in range(SLOTS)]
        ps = [ctx.enter_context(nc.psum_tensor(f"b{layer}_ps{k}", [P, G * F], F32)) for k in range(SLOTS)]
        normed_ready, t_ready, rows_ready = (sems[n][0] for n in ("normed_ready", "b_t_ready", "rows_ready"))
        z_loaded, stored, x_in = sems["z_loaded"], sems["out_stored"], sems["x_in"]
        x1 = node_chunks(net.x1)
        out_chunks = node_chunks(out, (NC - 1) * CHUNK)
        chunks = layer * NC
        loaded_before = [layer * (NC - KEPT_G) // TURN_CHUNKS * round_slots(k) for k in range(SLOTS)]

        with nc.Block() as block:
            @block.sync
            def _(sp):
                def load(c, k, i, kept):
                    if not kept:
                        wait_chunks(sp, normed_ready, 0, c - 1)
                        sp.dma_start(z_in[k % 2][:, :], chunk_of(net.z, c)).then_inc(z_loaded[k % 2], 16)
                    sp.wait_ge(stored[k], 16 * i)
                    sp.dma_start(rows[k][:, :, :].rearrange("p g f -> p (g f)"), chunk_of(x1, c)).then_inc(x_in[k], 16)

                chunk_ticks(sp, (load, 0))

            @block.scalar
            def _(act):
                def norm(c, k, i, kept):
                    wait_chunks(act, t_ready, chunks, c - 1)
                    if not kept:
                        act.wait_ge(z_loaded[k % 2], 16 * (2 * i + k // 2 - KEPT // 2) + 16)
                    z = z_kept[:, bass.ds(c * (G * F), G * F)] if kept else z_in[k % 2][:, :]
                    nc.scalar.activation(normed[k % 2][:, :], z, ACT.Identity, bias=offset[:, :], scale=factor[:, :]
                                         ).then_inc(normed_ready, 1)

                chunk_ticks(act, (norm, 0))

            @block.tensor
            def _(pe):
                def turn(c, k, i, kept):
                    pe.wait_ge(normed_ready, c + 1)
                    wait_chunks(pe, rows_ready, chunks, c - (SLOTS - 1))
                    for j in range(G // 2):
                        t = nc.tensor.transpose(ps[k][:, j * P:(j + 1) * P], normed[k % 2][:, j * P:(j + 1) * P], net.ident[:, :])
                    t.then_inc(t_ready, 1)

                chunk_ticks(pe, (turn, 0))

            @block.vector
            def _(dve):
                def finish(c, k, i, kept):
                    dve.wait_ge(t_ready, c + (chunks + 1))
                    got = ps[k][:, :].rearrange("p (g f) -> p g f", g=G)
                    dve.wait_ge(x_in[k], 16 * (i + loaded_before[k]) + 16)
                    nc.vector.tensor_tensor(rows[k][:, :, :], got, rows[k][:, :, :], ALU.add).then_inc(rows_ready, 1)

                chunk_ticks(dve, (finish, 0))

            @block.gpsimd
            def _(pool):
                def store(c, k, i, kept):
                    pool.wait_ge(rows_ready, c + (chunks + 1))
                    flat = rows[k][:, :, :].rearrange("p g f -> p (g f)")
                    if not (isinstance(c, int) and c == NC - 1):
                        pool.dma_start(chunk_of(out_chunks, c), flat).then_inc(stored[k], 16)
                    else:
                        tail = out[(NC - 1) * CHUNK:N, :].rearrange("(p g) f -> p (g f)", g=G)
                        cut = TAIL_P // 16 * 16
                        pool.dma_start(tail[0:cut, :], flat[0:cut, :]).then_inc(stored[k], 16)
                        pool.dma_start(tail[cut:TAIL_P, :], flat[cut:TAIL_P, :]).then_inc(stored[k], 16)

                chunk_ticks(pool, (store, 0))
                for k in range(SLOTS):
                    pool.wait_ge(stored[k], 16 * (slot_rounds(k) + (k == 0)))


def build_network(nc, args, out, upto=99):
    with ExitStack() as ctx:
        early_ctx = ExitStack()
        net = Net(nc, ctx, early_ctx, args)

        def sems(names, n):
            return {name: [ctx.enter_context(nc.semaphore(f"{name}{k}")) for k in range(n)] for name in names}

        conv_sems = sems(("h_idx_ready", "h_gathered", "h_same_in", "h_act_in", "h_act_out", "h_msg_ready", "h_sums_ready",
                          "h_summed_ready", "h_added", "h_scal_in", "n_last_in", "n_idx_ready", "n_to_ready", "n_gathered",
                          "n_row_in", "n_row_used", "n_mean_ready", "n_turned_ready", "n_mean_t_ready", "n_product_ready",
                          "n_summed_ready", "n_added", "n_scal_in"), 1) | sems(("h_dve_step", "n_dve_step"), 2)
        with nc.sbuf_tensor("zero", [P, (NP + P) * F // P // CONV_PIECES], F32) as net.zero:
            load_tables(net)
            count_nodes(net)
            nodes_to_hyperedges(net, 0, conv_sems)
        hyperedges_to_nodes(net, 0, conv_sems)
        nodes_to_hyperedges(net, 1, conv_sems)
        hyperedges_to_nodes(net, 1, conv_sems)
        norm_nodes(net)
        early_ctx.close()
        stats = ctx.enter_context(nc.sbuf_tensor("stats", [P, 2 * NC, 6], F32))
        factor = ctx.enter_context(nc.sbuf_tensor("factor", [P, 1], F32))
        offset = ctx.enter_context(nc.sbuf_tensor("offset", [P, 1], F32))
        edge_sems = sems(("src_ready", "sums_ready", "summed_ready", "v_copied"), 1) | sems(("same_in", "gathered", "summed_out"), SLOTS)
        node_sems = sems(("add_in",), SLOTS) | sems(("added",), LANES)
        node_sems |= sems(("dst_ready", "scaled_ready", "t_ready", "turned_ready", "m_ready", "z_ready", "counted"), 1)
        node_sems |= sems(("z_stored",), 2) | sems(("loaded",), SLOTS)
        norm_sems = sems(("normed_ready", "b_t_ready", "rows_ready", "v_ready", "norm_step", "offset_ready"), 1) | sems(("z_loaded",), 2)
        norm_sems |= sems(("stored", "out_stored", "x_in"), SLOTS)
        factor_sems = sems(("moments_ready", "mixed_ready", "var_ready", "root_ready", "factor_step", "diagonal_ready", "affine_ready"), 1)
        affine = ctx.enter_context(nc.sbuf_tensor("affine", [P, 2, F], F32))
        gather_edges(net, 0, edge_sems)
        for layer in range(2):
            with nc.sbuf_tensor(f"g_kept{layer}", [P, KEPT_G, G, GW], F32) as g_kept:
                add_and_transform(net, layer, node_sems | norm_sems, stats, g_kept)
                batch_norm_factors(net, layer, factor_sems, stats, factor, offset, affine)
                normalise_and_gather(net, layer + 1, edge_sems | norm_sems, affine, g_kept)
        with nc.sbuf_tensor("z_kept", [P, KEPT * G * F], F32) as z_kept:
            add_and_transform(net, 2, node_sems | norm_sems, stats, z_kept)
            batch_norm_factors(net, 2, factor_sems, stats, factor, offset, affine)
            normalise(net, 2, norm_sems, factor, offset, out, z_kept)


_INS = ["x", "src", "dst", "L0_gnn_W1", "L0_gnn_b1", "L0_gnn_W2", "L0_gnn_b2"] + [
    f"L1_gnn_{n}{i}" for i in (1, 2, 3) for n in ("W", "b", "gamma", "beta")]


def kernel(**inputs):
    import numpy as np
    import concourse.bacc as bacc
    from concourse.bass_utils import run_bass_kernel_spmd

    nc = bacc.Bacc("TRN2", target_bir_lowering=False, num_devices=1)
    arrays, args = {}, {}
    for name in _INS:
        a = np.ascontiguousarray(inputs[name])
        arrays[f"in_{name}"] = a
        args[name] = nc.dram_tensor(f"in_{name}", a.shape, mybir.dt.from_np(a.dtype), kind="ExternalInput").ap()
    out = nc.dram_tensor("out", (N, F), F32, kind="ExternalOutput").ap()
    build_network(nc, args, out)
    return run_bass_kernel_spmd(nc, [arrays], core_ids=[0]).results[0]["out"]
```
